# Optimizing a Trainium2 kernel written in Bass

```python
import numpy as np
import jax
import jax.numpy as jnp

def _softmax(x, axis=-1):
    return jax.nn.softmax(x, axis=axis)

def _gelu(x):
    return jax.nn.gelu(x, approximate=True)

def _silu(x):
    return jax.nn.silu(x)

def _sigmoid(x):
    return jax.nn.sigmoid(x)

def _layernorm(x, axis=-1, eps=1e-05):
    m = jnp.mean(x, axis=axis, keepdims=True)
    v = jnp.var(x, axis=axis, keepdims=True)
    return (x - m) / jnp.sqrt(v + eps)

def _scatter_add(tgt, idx, src, axis=0):
    return tgt.at[idx].add(src)

def _segment_sum(src, seg, n):
    return jax.ops.segment_sum(src, seg, n)
kernel_name = 'mk_early_fusion_d2_tok_img256_r4_790c99'

def setup_inputs(seed: int=0):
    np.random.seed(seed)
    _w = jnp.asarray

    def _rec_inputs():
        import jax
        import jax.numpy as jnp
        _rk = jax.random.key(seed)
        x = -0.000520686 + 1.00062 * jax.random.normal(jax.random.fold_in(_rk, 1), (64, 64, 64, 4), jnp.float32)
        txt = -0.00209228 + 0.0210958 * jax.random.normal(jax.random.fold_in(_rk, 2), (64, 32, 64), jnp.float32)
        return (x, txt)
    x, txt = _rec_inputs()

    def _L0_tok_setup():
        import jax, jax.numpy as jnp
        import numpy as np
        HIDDEN_DIM = 128
        key = jax.random.key(seed)
        k_geom, k_w, k_b = jax.random.split(key, 3)
        B, N, F = (8, 64, 4)
        geom = jax.random.normal(k_geom, (B, N, N, F), dtype=jnp.float32)
        bound = 1.0 / np.sqrt(F)
        W = jax.random.uniform(k_w, (HIDDEN_DIM, F), dtype=jnp.float32, minval=-bound, maxval=bound)
        b = jax.random.uniform(k_b, (HIDDEN_DIM,), dtype=jnp.float32, minval=-bound, maxval=bound)
        return {'geom': geom, 'W': W, 'b': b}
    _L0_tok_all = _L0_tok_setup()
    _L0_tok_in = {k: v for k, v in _L0_tok_all.items() if k in ('W', 'b')}
    del _L0_tok_all

    def _L0_attn_setup():
        import jax, jax.numpy as jnp
        import numpy as np
        B_SZ, T, H, N, L = (4, 128, 64, 64, 4)
        EPS = 1e-05

        def _hippo(n):
            i = np.arange(n)[:, None]
            j = np.arange(n)[None, :]
            A = np.where(i >= j, (-1.0) ** (i - j) * np.sqrt((2 * i + 1.0) * (2 * j + 1.0)), 0.0)
            A = A / (1.1 * np.linalg.norm(A, 2))
            return A.astype(np.float32)

        def _xavier(key, shape):
            fan_in, fan_out = (shape[1], shape[0])
            a = float(np.sqrt(6.0 / (fan_in + fan_out)))
            return jax.random.uniform(key, shape, jnp.float32, -a, a)

        def _ln(x):
            m = jnp.mean(x, -1, keepdims=True)
            v = jnp.mean((x - m) ** 2, -1, keepdims=True)
            return (x - m) / jnp.sqrt(v + EPS)

        def _ssm_layer(h, A, B, C, D):
            Cbar = C.mean(0)
            BT = B.T
            DT = D.T

            def step(state, u):
                y = jnp.einsum('bnh,n->bh', state, Cbar) + u @ DT
                new_state = jnp.einsum('nm,bmh->bnh', A, state) + (u @ BT)[:, :, None]
                return (new_state, y)
            state0 = jnp.zeros((h.shape[0], A.shape[0], h.shape[2]), h.dtype)
            _, ys = jax.lax.scan(step, state0, jnp.swapaxes(h, 0, 1))
            y = jnp.swapaxes(ys, 0, 1)
            y = jax.nn.gelu(y, approximate=False) + h
            return _ln(y)
        key = jax.random.key(seed)
        ks = jax.random.split(key, 8)
        x = jax.random.normal(ks[0], (B_SZ, T, H), jnp.float32)
        A = jnp.broadcast_to(jnp.asarray(_hippo(N)), (L, N, N))
        Bm = jnp.stack([_xavier(jax.random.fold_in(ks[1], l), (N, H)) for l in range(L)])
        Cm = jnp.stack([_xavier(jax.random.fold_in(ks[2], l), (H, N)) for l in range(L)])
        Dm = jnp.stack([_xavier(jax.random.fold_in(ks[3], l), (H, H)) for l in range(L)])
        Win = _xavier(ks[4], (H, H))
        bin_ = jnp.zeros((H,), jnp.float32)
        Wout = _xavier(ks[5], (H, H))
        bout = jnp.zeros((H,), jnp.float32)
        return {'x': x, 'Win': Win, 'bin_': bin_, 'Wout': Wout, 'bout': bout, 'A': A, 'Bm': Bm, 'Cm': Cm, 'Dm': Dm}
    _L0_attn_all = _L0_attn_setup()
    _L0_attn_in = {k: v for k, v in _L0_attn_all.items() if k in ('Win', 'bin_', 'Wout', 'bout', 'A', 'Bm', 'Cm', 'Dm')}
    del _L0_attn_all

    def _L0_ffn_setup():
        import jax, jax.numpy as jnp
        import numpy as np
        B, S, H, F, E, K = (8, 1024, 64, 128, 16, 2)
        EPS = 1e-05
        key = jax.random.key(seed)
        ks = jax.random.split(key, 9)
        sc = 0.02
        return {'x': jax.random.normal(ks[0], (B, S, H), dtype=jnp.float32), 'gate_w': jax.random.normal(ks[1], (H, E), dtype=jnp.float32) * sc, 'gate_b': jnp.zeros((E,), dtype=jnp.float32), 'w1': jax.random.normal(ks[2], (E, H, F), dtype=jnp.float32) * sc, 'b1': jnp.zeros((E, F), dtype=jnp.float32), 'w2': jax.random.normal(ks[3], (E, F, H), dtype=jnp.float32) * sc, 'b2': jnp.zeros((E, H), dtype=jnp.float32), 'gamma': jnp.ones((H,), dtype=jnp.float32), 'beta': jnp.zeros((H,), dtype=jnp.float32)}
    _L0_ffn_all = _L0_ffn_setup()
    _L0_ffn_in = {k: v for k, v in _L0_ffn_all.items() if k in ('gate_w', 'gate_b', 'w1', 'b1', 'w2', 'b2', 'gamma', 'beta')}
    del _L0_ffn_all

    def _L1_attn_setup():
        import jax, jax.numpy as jnp
        import numpy as np
        key = jax.random.key(seed)
        ks = jax.random.split(key, 5)
        b, t, e, h = (8, 256, 64, 8)
        w = lambda k, shape: jax.random.normal(k, shape, dtype=jnp.float32) * 0.02
        return {'x': jax.random.normal(ks[0], (b, t, e), dtype=jnp.float32), 'Wq': w(ks[1], (e, e * h)), 'bq': jnp.zeros((e * h,), jnp.float32), 'Wk': w(ks[2], (e, e * h)), 'bk': jnp.zeros((e * h,), jnp.float32), 'Wv': w(ks[3], (e, e * h)), 'bv': jnp.zeros((e * h,), jnp.float32), 'Wu': w(ks[4], (e * h, e)), 'bu': jnp.zeros((e,), jnp.float32)}
    _L1_attn_all = _L1_attn_setup()
    _L1_attn_in = {k: v for k, v in _L1_attn_all.items() if k in ('Wq', 'bq', 'Wk', 'bk', 'Wv', 'bv', 'Wu', 'bu')}
    del _L1_attn_all

    def _L1_ffn_setup():
        import jax, jax.numpy as jnp
        import numpy as np
        from jax import lax
        key = jax.random.key(seed)
        B, T, I, H = (64, 512, 64, 64)
        ks = jax.random.split(key, 13)
        s = 1.0 / np.sqrt(H)

        def w(k, shape):
            return jax.random.uniform(k, shape, jnp.float32, -s, s)
        return {'x': jax.random.normal(ks[0], (B, T, I), jnp.float32), 'U_i': w(ks[1], (I, H)), 'V_i': w(ks[2], (H, H)), 'b_i': w(ks[3], (H,)), 'U_f': w(ks[4], (I, H)), 'V_f': w(ks[5], (H, H)), 'b_f': w(ks[6], (H,)), 'U_c': w(ks[7], (I, H)), 'V_c': w(ks[8], (H, H)), 'b_c': w(ks[9], (H,)), 'U_o': w(ks[10], (I, H)), 'V_o': w(ks[11], (H, H)), 'b_o': w(ks[12], (H,))}
    _L1_ffn_all = _L1_ffn_setup()
    _L1_ffn_in = {k: v for k, v in _L1_ffn_all.items() if k in ('U_i', 'V_i', 'b_i', 'U_f', 'V_f', 'b_f', 'U_c', 'V_c', 'b_c', 'U_o', 'V_o', 'b_o')}
    del _L1_ffn_all
    return {'x': x, 'txt': txt, 'L0_tok_W': _L0_tok_in['W'], 'L0_tok_b': _L0_tok_in['b'], 'L0_attn_Win': _L0_attn_in['Win'], 'L0_attn_bin_': _L0_attn_in['bin_'], 'L0_attn_Wout': _L0_attn_in['Wout'], 'L0_attn_bout': _L0_attn_in['bout'], 'L0_attn_A': _L0_attn_in['A'], 'L0_attn_Bm': _L0_attn_in['Bm'], 'L0_attn_Cm': _L0_attn_in['Cm'], 'L0_attn_Dm': _L0_attn_in['Dm'], 'L0_ffn_gate_w': _L0_ffn_in['gate_w'], 'L0_ffn_gate_b': _L0_ffn_in['gate_b'], 'L0_ffn_w1': _L0_ffn_in['w1'], 'L0_ffn_b1': _L0_ffn_in['b1'], 'L0_ffn_w2': _L0_ffn_in['w2'], 'L0_ffn_b2': _L0_ffn_in['b2'], 'L0_ffn_gamma': _L0_ffn_in['gamma'], 'L0_ffn_beta': _L0_ffn_in['beta'], 'L1_attn_Wq': _L1_attn_in['Wq'], 'L1_attn_bq': _L1_attn_in['bq'], 'L1_attn_Wk': _L1_attn_in['Wk'], 'L1_attn_bk': _L1_attn_in['bk'], 'L1_attn_Wv': _L1_attn_in['Wv'], 'L1_attn_bv': _L1_attn_in['bv'], 'L1_attn_Wu': _L1_attn_in['Wu'], 'L1_attn_bu': _L1_attn_in['bu'], 'L1_ffn_U_i': _L1_ffn_in['U_i'], 'L1_ffn_V_i': _L1_ffn_in['V_i'], 'L1_ffn_b_i': _L1_ffn_in['b_i'], 'L1_ffn_U_f': _L1_ffn_in['U_f'], 'L1_ffn_V_f': _L1_ffn_in['V_f'], 'L1_ffn_b_f': _L1_ffn_in['b_f'], 'L1_ffn_U_c': _L1_ffn_in['U_c'], 'L1_ffn_V_c': _L1_ffn_in['V_c'], 'L1_ffn_b_c': _L1_ffn_in['b_c'], 'L1_ffn_U_o': _L1_ffn_in['U_o'], 'L1_ffn_V_o': _L1_ffn_in['V_o'], 'L1_ffn_b_o': _L1_ffn_in['b_o']}

def reference(x, txt, L0_tok_W, L0_tok_b, L0_attn_Win, L0_attn_bin_, L0_attn_Wout, L0_attn_bout, L0_attn_A, L0_attn_Bm, L0_attn_Cm, L0_attn_Dm, L0_ffn_gate_w, L0_ffn_gate_b, L0_ffn_w1, L0_ffn_b1, L0_ffn_w2, L0_ffn_b2, L0_ffn_gamma, L0_ffn_beta, L1_attn_Wq, L1_attn_bq, L1_attn_Wk, L1_attn_bk, L1_attn_Wv, L1_attn_bv, L1_attn_Wu, L1_attn_bu, L1_ffn_U_i, L1_ffn_V_i, L1_ffn_b_i, L1_ffn_U_f, L1_ffn_V_f, L1_ffn_b_f, L1_ffn_U_c, L1_ffn_V_c, L1_ffn_b_c, L1_ffn_U_o, L1_ffn_V_o, L1_ffn_b_o):
    import jax
    import jax.numpy as jnp

    def _L0_tok_ref(geom, W, b):
        import jax, jax.numpy as jnp
        import numpy as np
        HIDDEN_DIM = 128
        bias = jnp.einsum('bijf,hf->bijh', geom, W) + b
        return bias.mean(-1)

    def _L0_attn_ref(x, Win, bin_, Wout, bout, A, Bm, Cm, Dm):
        import jax, jax.numpy as jnp
        import numpy as np
        B_SZ, T, H, N, L = (4, 128, 64, 64, 4)
        EPS = 1e-05

        def _hippo(n):
            i = np.arange(n)[:, None]
            j = np.arange(n)[None, :]
            A = np.where(i >= j, (-1.0) ** (i - j) * np.sqrt((2 * i + 1.0) * (2 * j + 1.0)), 0.0)
            A = A / (1.1 * np.linalg.norm(A, 2))
            return A.astype(np.float32)

        def _xavier(key, shape):
            fan_in, fan_out = (shape[1], shape[0])
            a = float(np.sqrt(6.0 / (fan_in + fan_out)))
            return jax.random.uniform(key, shape, jnp.float32, -a, a)

        def _ln(x):
            m = jnp.mean(x, -1, keepdims=True)
            v = jnp.mean((x - m) ** 2, -1, keepdims=True)
            return (x - m) / jnp.sqrt(v + EPS)

        def _ssm_layer(h, A, B, C, D):
            Cbar = C.mean(0)
            BT = B.T
            DT = D.T

            def step(state, u):
                y = jnp.einsum('bnh,n->bh', state, Cbar) + u @ DT
                new_state = jnp.einsum('nm,bmh->bnh', A, state) + (u @ BT)[:, :, None]
                return (new_state, y)
            state0 = jnp.zeros((h.shape[0], A.shape[0], h.shape[2]), h.dtype)
            _, ys = jax.lax.scan(step, state0, jnp.swapaxes(h, 0, 1))
            y = jnp.swapaxes(ys, 0, 1)
            y = jax.nn.gelu(y, approximate=False) + h
            return _ln(y)
        h = x @ Win.T + bin_
        for l in range(L):
            h = _ssm_layer(h, A[l], Bm[l], Cm[l], Dm[l])
        h = _ln(h)
        return h @ Wout.T + bout

    def _L0_ffn_ref(x, gate_w, gate_b, w1, b1, w2, b2, gamma, beta):
        import jax, jax.numpy as jnp
        import numpy as np
        B, S, H, F, E, K = (8, 1024, 64, 128, 16, 2)
        EPS = 1e-05
        gate_logits = x @ gate_w + gate_b
        topk_vals, topk_idx = jax.lax.top_k(gate_logits, K)
        topk_w = jax.nn.softmax(topk_vals, axis=-1)
        h = jax.nn.relu(jnp.einsum('bsh,ehf->bsef', x, w1) + b1)
        expert_out = jnp.einsum('bsef,efh->bseh', h, w2) + b2
        sel = jnp.take_along_axis(expert_out, topk_idx[:, :, :, None], axis=2)
        moe = jnp.sum(topk_w[..., None] * sel, axis=2)
        y = x + moe
        mu = jnp.mean(y, axis=-1, keepdims=True)
        var = jnp.var(y, axis=-1, keepdims=True)
        return (y - mu) / jnp.sqrt(var + EPS) * gamma + beta

    def _L1_attn_ref(x, Wq, bq, Wk, bk, Wv, bv, Wu, bu):
        import jax, jax.numpy as jnp
        import numpy as np
        b, t, e = x.shape
        h = Wq.shape[1] // e
        q = (x @ Wq + bq).reshape(b, t, h, e)
        k = (x @ Wk + bk).reshape(b, t, h, e)
        v = (x @ Wv + bv).reshape(b, t, h, e)
        scores = jnp.einsum('bihe,bjhe->bhij', q, k) / jnp.sqrt(jnp.asarray(e, jnp.float32))
        i = jnp.arange(t)[:, None]
        j = jnp.arange(t)[None, :]
        scores = jnp.where(j >= i, -jnp.inf, scores)
        scores = jnp.where(i == 0, 0.0, scores)
        att = jax.nn.softmax(scores, axis=-1)
        att = jnp.where(i == 0, 0.0, att)
        out = jnp.einsum('bhij,bjhe->bihe', att, v).reshape(b, t, h * e)
        return out @ Wu + bu

    def _L1_ffn_ref(x, U_i, V_i, b_i, U_f, V_f, b_f, U_c, V_c, b_c, U_o, V_o, b_o):
        import jax, jax.numpy as jnp
        import numpy as np
        from jax import lax
        B, T, _ = x.shape
        H = U_i.shape[1]
        xt = jnp.swapaxes(x, 0, 1)
        xi = xt @ U_i + b_i
        xf = xt @ U_f + b_f
        xg = xt @ U_c + b_c
        xo = xt @ U_o + b_o
        h0 = jnp.zeros((B, H), x.dtype)
        c0 = jnp.zeros((B, H), x.dtype)

        def step(carry, xs):
            h, c = carry
            xi_t, xf_t, xg_t, xo_t = xs
            i_t = jax.nn.sigmoid(xi_t + h @ V_i)
            f_t = jax.nn.sigmoid(xf_t + h @ V_f)
            g_t = jnp.tanh(xg_t + h @ V_c)
            o_t = jax.nn.sigmoid(xo_t + h @ V_o)
            c_new = h * c + i_t * g_t
            h_new = o_t * jnp.tanh(c_new)
            return ((h_new, c_new), h_new)
        (_, _), hs = lax.scan(step, (h0, c0), (xi, xf, xg, xo))
        return jnp.swapaxes(hs, 0, 1)
    h = _L0_tok_ref(x, L0_tok_W, L0_tok_b)
    h = jnp.concatenate([h, txt], axis=1)
    h = h + _L0_attn_ref(_layernorm(h, axis=-1), L0_attn_Win, L0_attn_bin_, L0_attn_Wout, L0_attn_bout, L0_attn_A, L0_attn_Bm, L0_attn_Cm, L0_attn_Dm)
    h = h + _L0_ffn_ref(_layernorm(h, axis=-1), L0_ffn_gate_w, L0_ffn_gate_b, L0_ffn_w1, L0_ffn_b1, L0_ffn_w2, L0_ffn_b2, L0_ffn_gamma, L0_ffn_beta)
    h = h + _L1_attn_ref(_layernorm(h, axis=-1), L1_attn_Wq, L1_attn_bq, L1_attn_Wk, L1_attn_bk, L1_attn_Wv, L1_attn_bv, L1_attn_Wu, L1_attn_bu)
    h = h + _L1_ffn_ref(_layernorm(h, axis=-1), L1_ffn_U_i, L1_ffn_V_i, L1_ffn_b_i, L1_ffn_U_f, L1_ffn_V_f, L1_ffn_b_f, L1_ffn_U_c, L1_ffn_V_c, L1_ffn_b_c, L1_ffn_U_o, L1_ffn_V_o, L1_ffn_b_o)
    return h

_drawn_inputs = setup_inputs


def setup_inputs(seed=0):
    import zlib

    import numpy as np

    out = dict(_drawn_inputs(seed))
    spreads = {'L0_attn_bin_': (0.0, 0.1),
     'L0_attn_bout': (0.0, 0.1),
     'L0_ffn_gate_b': (0.0, 0.1),
     'L0_ffn_b1': (0.0, 0.8),
     'L0_ffn_b2': (0.0, 0.1),
     'L0_ffn_gamma': (1.0, 0.2),
     'L0_ffn_beta': (0.0, 0.1),
     'L1_attn_bq': (0.0, 0.8),
     'L1_attn_bk': (0.0, 0.8),
     'L1_attn_bv': (0.0, 0.371),
     'L1_attn_bu': (0.0, 0.1)}
    factors = {'L0_tok_b': 8.0,
     'L0_attn_A': 3.687,
     'L0_ffn_w1': 7.243,
     'L0_ffn_w2': 5.368,
     'L1_attn_Wq': 8.0,
     'L1_attn_Wk': 8.0,
     'L1_attn_Wv': 5.762,
     'L1_ffn_U_i': 3.68,
     'L1_ffn_V_i': 8.0,
     'L1_ffn_b_i': 8.0,
     'L1_ffn_V_c': 7.674,
     'L1_ffn_b_c': 6.406,
     'L1_ffn_U_o': 3.556,
     'L1_ffn_V_o': 8.0,
     'L1_ffn_b_o': 8.0}
    for name, (base, spread) in spreads.items():
        noise = np.random.default_rng([zlib.crc32(name.encode()), seed]).standard_normal(out[name].shape)
        drawn = base * np.exp(spread * noise) if base else spread * noise
        out[name] = jnp.asarray(drawn.astype(out[name].dtype))
    for name, factor in factors.items():
        out[name] = (out[name] * factor).astype(out[name].dtype)
    return out
```

```python
from contextlib import ExitStack

import concourse.bass as bass
from concourse import mybir

F32 = mybir.dt.float32
F32R = mybir.dt.float32r
BF16 = mybir.dt.bfloat16
ALU = mybir.AluOpType
ACT = mybir.ActivationFunctionType
AX_X = mybir.AxisListType.X



def early_fusion(nc, x, txt, tok_W, tok_b, Win, bin_, Wout, bout, A, Bm, Cm, Dm,
                 gate_w, gate_b, w1, b1, w2, b2, gamma, beta,
                 Wq, bq, Wk, bk, Wv, bv, Wu, bu,
                 U_i, V_i, b_i, U_c, V_c, b_c, U_o, V_o, b_o, out):
    NB, TX, D, NF = x.shape
    TT = txt.shape[1]
    T = TX + TT
    NM = T // 2
    NK = NM // 2
    TOK = T * NB
    L = A.shape[0]
    HD = tok_W.shape[0]
    E, _, F = w1.shape
    NH = Wq.shape[1] // D
    NP = NH // 2
    EPS = 1e-5
    NEG = -1e30
    CH = 8
    NC = NM // CH
    KC = 4
    NJ = NK // KC
    QM = 4
    NQ = NM // QM
    GB = 4
    NG = NB // GB
    WBW = T // 2 + T - 1
    assert NB == 64 and D == 64 and F == 128 and T % 4 == 0 and NK % KC == 0

    with ExitStack() as ctx:
        def sb(name, shape, dt=F32):
            return ctx.enter_context(nc.sbuf_tensor(name, shape, dt))

        def sem(name):
            return ctx.enter_context(nc.semaphore(name))

        H = sb("H", [128, NM, D])
        X = sb("X", [128, NM, D])
        UT = sb("UT", [128, NK, 2, D])
        UF = sb("UF", [128, NK, 128])
        Y1 = sb("Y1", [128, NM * D])
        Y2 = sb("Y2", [128, NM * D])
        XC = sb("XC", [128, NM * D])
        BIG = sb("BIG", [128, 32 * D * NF])
        XS = sb("XS", [128, TOK], F32R)
        ident = sb("ident", [128, 128])
        identb = sb("identb", [128, 128], BF16)
        ii = sb("ii", [128, D], F32R)
        o128 = sb("o128", [128, 128])
        cD = sb("cD", [128, 1])
        mhalf = sb("mhalf", [128, 64])
        wtok = sb("wtok", [128, NF + 1])
        wm = sb("wm", [128, NF + 1])
        bds = sb("bds", [128, L + 2, 128])
        bdt = sb("bdt", [128, L + 2, 128])
        binr = sb("binr", [128, D])
        boutr = sb("boutr", [128, D])
        Am = sb("Am", [D, 2, L, D])
        Am2 = sb("Am2", [D, 2, L, D])
        Cs = sb("Cs", [D, L, D])
        Gk = sb("Gk", [D, L, T])
        BB = sb("BB", [D, L, 2, D])
        WQKh = sb("WQKh", [128, 2, NH * D], F32R)
        WQKl = sb("WQKl", [128, 2, NH * D], F32R)
        WB = sb("WB", [128, L, WBW + 1])
        lnab = sb("lnab", [128, L, 2])
        Cc = sb("Cc", [128, NK, 2])
        st = sb("st", [128, 4, NM])
        W1h = sb("W1h", [128, E, F], F32R)
        W1l = sb("W1l", [128, E, F], F32R)
        GWs = sb("GWs", [128, E])
        GWh = sb("GWh", [128, E], F32R)
        GWl = sb("GWl", [128, E], F32R)
        gbr = sb("gbr", [128, E])
        b1s = sb("b1s", [E, F])
        b1T = sb("b1T", [F, E])
        w2s = sb("w2s", [F, E, D])
        b2f = sb("b2f", [3 * E, 2, D])
        b2p = sb("b2p", [3 * E, 3, 2 * D], BF16)
        gs = sb("gs", [128, 8, NM])
        sel = sb("sel", [3 * E, E, F], BF16)
        rev = sb("rev", [128, E])
        gam = sb("gam", [128, D])
        bet = sb("bet", [128, D])
        XSg = sb("XSg", [128, 2, GB, T], F32R)
        mask = sb("mask", [T, NP, T], BF16)
        valid = sb("valid", [T, 1])
        Wvs = sb("Wvs", [D, NH * D])
        WvT = sb("WvT", [128, NP, D])
        Wus = sb("Wus", [128, NP, D])
        NPt = sb("NPt", [128, NP, D])
        bqk = sb("bqk", [128, 2, NP])
        bvs = sb("bvs", [128, NP])
        bus = sb("bus", [128, 2])
        am = sb("am", [T, 4, 4, NH])
        UIO = sb("UIO", [D + 1, 128])
        UG = sb("UG", [D + 1, 128])
        VIO = sb("VIO", [D, 128])
        VG = sb("VG", [D, 128])
        sems = {}

        def S(name):
            if name not in sems:
                sems[name] = sem(name)
            return sems[name]

        PS = ctx.enter_context(nc.psum_tensor("PS", [128, 8, 512], F32))

        W1s = Y1[:, 0:E * F].rearrange("p (e f) -> p e f", e=E)
        WQs = Y1[:, E * F:E * F + 2 * NH * D].rearrange("p (a c) -> p a c", a=2)
        GPT = UT[:, :, :, :].rearrange("p k h d -> p (k h d)").bitcast(BF16)[:, 0:NM * 3 * E]
        GP = UF[:, :, :].rearrange("p k c -> p (k c)").bitcast(BF16)
        PSb = PS[:, :, :].bitcast(BF16)
        MO = BIG[:, 0:TOK]
        Rb = Y2[:, 0:2048].rearrange("p (a c) -> p a c", a=4)
        Hb = XC[:, 0:2048].rearrange("p (a c) -> p a c", a=4)
        XF = BIG[0:D + 1, 0:TOK]
        AO = BIG[:, 0:TOK]
        QK = [t.rearrange("p (a c) -> p a c", a=2 * NP) for t in (UT[:, :, :, :].rearrange("p k h d -> p (k h d)"),
                                                                  UF[:, :, :].rearrange("p k c -> p (k c)"))]
        Pb = Y1[0:T, 0:4 * NH * T].rearrange("p (n a h j) -> p n a h j", n=4, a=2, h=NP)
        XT = XC[0:T, NP * GB * T:NP * GB * T + 2 * GB * D].rearrange("p (n b d) -> p n b d", n=2, b=GB)
        PT = Y2[0:T, 0:2 * NH * T].rearrange("p (n a c) -> p n a c", n=2, a=2)
        Zg = [t.rearrange("p (h b i) -> p h b i", h=NP, b=GB) for t in (Y2[:, 2 * NH * T:2 * NH * T + NP * GB * T],
                                                                        XC[:, 0:NP * GB * T])]
        UTf = UT[:, :, :, :].rearrange("p k h d -> p (k h d)")
        Tb = UTf[:, 0:256].rearrange("p (a c) -> p a c", a=2)
        TC = UTf[:, 256:320]
        Cb = UTf[0:D, 320:448].rearrange("p (a c) -> p a c", a=2)
        HC = UTf[0:D, 448:512]
        HB = UTf[0:D, 512:768].rearrange("p (a c) -> p a c", a=4)
        Yt = Y1[:, :].rearrange("p (m d) -> p m d", d=D)
        Xr = BIG[:, :].rearrange("p (m c) -> p m c", c=D * NF)

        def halves(t):
            return t[:, :, :].rearrange("p (k h) d -> p k h d", h=2)

        def view_km(t):
            return t[:, :, :].rearrange("p (h k) d -> p k h d", h=2)

        def ssm_scale(pool, l, j):
            n = l * NJ + j
            sj = slice(j * KC * 2, (j + 1) * KC * 2)
            pool.wait_ge(S("s_v"), n + 1)
            pool.tensor_tensor(st[:, 3, sj], st[:, 2, sj], mhalf[:, 0:KC * 2], ALU.pow).then_inc(S("s_r"), 1)
            pool.wait_ge(S("s_r"), n + 1)
            pool.tensor_tensor(ssm_cols(UT, j).rearrange("p (a d) -> p a d", d=D),
                               XC[:, j * 512:j * 512 + 512].rearrange("p (a d) -> p a d", d=D),
                               st[:, 3, sj].unsqueeze(2).to_broadcast([128, KC * 2, D]), ALU.mult).then_inc(S("s_un"), 1)

        def ssm_cols(t, j):
            return t[:, j * KC:(j + 1) * KC, :, :].rearrange("p k h d -> p (k h d)")

        def ln_dve(dve, p, src, ready):
            def front(c):
                n = p * NC + c + 1
                sc = slice(c * CH, (c + 1) * CH)
                ready(c)
                dve.tensor_reduce(st[:, 0, sc], src[:, sc, :], AX_X, ALU.add).then_inc(S("ln_s"), 1)
                dve.wait_ge(S("ln_s"), n)
                dve.tensor_scalar(st[:, 1, sc], st[:, 0, sc], -1.0 / D, None, ALU.mult).then_inc(S("ln_m"), 1)
                dve.wait_ge(S("ln_m"), n)
                dve.tensor_tensor(XC[:, c * 512:c * 512 + 512].rearrange("p (a d) -> p a d", d=D), src[:, sc, :],
                                  st[:, 1, sc].unsqueeze(2).to_broadcast([128, CH, D]), ALU.add).then_inc(S("ln_c"), 1)

            def back(c):
                n = p * NC + c + 1
                sc = slice(c * CH, (c + 1) * CH)
                dve.wait_ge(S("ln_q"), n)
                dve.tensor_reduce(st[:, 2, sc], Y2[:, c * 512:c * 512 + 512].rearrange("p (a d) -> p a d", d=D),
                                  AX_X, ALU.add).then_inc(S("ln_v0"), 1)
                dve.wait_ge(S("ln_v0"), n)
                dve.tensor_scalar(st[:, 2, sc], st[:, 2, sc], 1.0 / D, EPS, ALU.mult, ALU.add).then_inc(S("ln_v"), 1)

            for c in range(NC):
                front(c)
                if c:
                    back(c - 1)
            back(NC - 1)

        def ln_act(act, p):
            for c in range(NC):
                act.wait_ge(S("ln_c"), p * NC + c + 1)
                act.activation(Y2[:, c * 512:c * 512 + 512], XC[:, c * 512:c * 512 + 512], ACT.Square).then_inc(S("ln_q"), 1)

        def ln_pool(pool, p, dst, gamma_too=False):
            for c in range(NC):
                n = p * NC + c + 1
                sc = slice(c * CH, (c + 1) * CH)
                pool.wait_ge(S("ln_v"), n)
                pool.tensor_tensor(st[:, 3, sc], st[:, 2, sc], mhalf[:, 0:CH], ALU.pow).then_inc(S("ln_r"), 1)
                pool.wait_ge(S("ln_r"), n)
                pool.tensor_tensor(dst(c), XC[:, c * 512:c * 512 + 512].rearrange("p (a d) -> p a d", d=D),
                                   st[:, 3, sc].unsqueeze(2).to_broadcast([128, CH, D]), ALU.mult).then_inc(S("ln_o"), 1)
                if gamma_too:
                    pool.wait_ge(S("ln_o"), n)
                    pool.tensor_tensor(dst(c), dst(c), gam[:, :].unsqueeze(1).to_broadcast([128, CH, D]), ALU.mult).then_inc(S("f_g"), 1)

        def xcol(c, f):
            v = Xr[:, c * CH:(c + 1) * CH, :].rearrange("p m (i f) -> p (m i) f", f=NF)
            return v[:, :, f]

        def bank4(b):
            return PS[:, b, :].rearrange("p (k c) -> p k c", k=KC)

        def grant(eng, name, n):
            for _ in range(n):
                eng.nop().then_inc(S(name), 1)

        def XSp():
            return XS[:, :].rearrange("p (m a c) -> p m a c", a=2, c=128)

        def xs_pe(pe, r, lnp):
            for c in range(NC):
                pe.wait_ge(S("ln_o"), lnp * NC + c + 1)
                if c >= 2 or r:
                    pe.wait_ge(S("xs_l"), 2 * (r * NC + c - 1))
                for k in range(4):
                    last = pe.transpose(PS[:, 4 + c % 2, k * 128:k * 128 + 128],
                                        X[:, c * CH + 2 * k:c * CH + 2 * k + 2, :].rearrange("p m d -> p (m d)"), ident[:, :])
                last.then_inc(S("xs_tp"), 1)

        def xs_act(act, r):
            for c in range(NC):
                act.wait_ge(S("xs_tp"), r * NC + c + 1)
                for a in range(2):
                    act.activation(XSp()[0:64, 4 * c:4 * c + 4, a, :], bank4(4 + c % 2)[64 * a:64 * a + 64], ACT.Copy).then_inc(S("xs_h"), 1)

        def xs_dve(dve, r):
            for c in range(NC):
                for a in range(2):
                    dve.wait_ge(S("xs_h"), 2 * (r * NC + c) + a + 1)
                    dve.tensor_tensor(XSp()[64:128, 4 * c:4 * c + 4, a, :], bank4(4 + c % 2)[64 * a:64 * a + 64],
                                      XSp()[0:64, 4 * c:4 * c + 4, a, :].bitcast(F32), ALU.subtract).then_inc(S("xs_l"), 1)

        def has(d, k, first, drain):
            return not (first and k < d) and not (drain and k >= d)

        DRAIN = 4

        def att_loop(eng, step):
            for k in range(8):
                step(0, k, first=True)
            with eng.Fori(1, NB // 8 - 1) as i:
                for k in range(8):
                    step(i, k)
            for k in range(8):
                step(NB // 8 - 1, k, last=True)
            for k in range(DRAIN):
                step(NB // 8, k, drain=True)

        block = ctx.enter_context(nc.Block())

        @block.sync
        def _(sp):
            sp.dma_start(wtok[:, 0:NF], tok_W).then_inc(S("ld_tok"), 16)
            sp.dma_start(wtok[:, NF:NF + 1], tok_b.rearrange("(p a) -> p a", a=1)).then_inc(S("ld_tok"), 16)
            xv = x.rearrange("b (m s) i f -> s b m (i f)", s=2)
            for c in range(TX // 2 // CH):
                for s in range(2):
                    sp.dma_start(Xr[64 * s:64 * s + 64, c * CH:(c + 1) * CH, :],
                                 xv[s, :, c * CH:(c + 1) * CH, :]).then_inc(S("ld_x%d" % c), 16)
            tv = txt.rearrange("b (m s) d -> s b m d", s=2)
            for s in range(2):
                sp.dma_start(H[64 * s:64 * s + 64, TX // 2:NM, :], tv[s]).then_inc(S("ld_txt"), 16)
            for s in range(2):
                sp.dma_start(W1s[64 * s:64 * s + 64, :, :],
                             w1.rearrange("e h f -> h e f")).then_inc(S("ld_w1"), 16)
                sp.dma_start(GWs[64 * s:64 * s + 64, :], gate_w).then_inc(S("ld_w1"), 16)
                sp.dma_start(WQs[64 * s:64 * s + 64, 0, :], Wq).then_inc(S("ld_w1"), 16)
                sp.dma_start(WQs[64 * s:64 * s + 64, 1, :], Wk).then_inc(S("ld_w1"), 16)
            sp.dma_start(b1s[:, :], b1).then_inc(S("ld_moe"), 16)
            sp.dma_start(w2s[:, :, :], w2.rearrange("e f h -> f e h")).then_inc(S("ld_moe"), 16)
            for g in range(3):
                sp.dma_start(b2f[E * g:E * g + E, 0, :], b2).then_inc(S("ld_moe"), 16)
            for k in range(2):
                sp.dma_start(bqk[:, k, :], (bq, bk)[k].rearrange("(c p) -> p c", p=128), allow_slow_non_contiguous=True).then_inc(S("ld_at"), 16)
            sp.dma_start(bvs[:, :], bv.rearrange("(c p) -> p c", p=128), allow_slow_non_contiguous=True).then_inc(S("ld_at"), 16)
            sp.dma_start(bus[0:D, 0:1], bu.rearrange("(p a) -> p a", a=1)).then_inc(S("ld_at"), 16)
            sp.dma_start(Wvs[:, :], Wv).then_inc(S("ld_at"), 16)
            sp.dma_start(Wus[:, :, :], Wu.rearrange("(c p) o -> p c o", p=128)).then_inc(S("ld_at"), 16)
            for dst, lo, hi in ((UIO, (U_i, b_i), (U_o, b_o)), (UG, (U_c, b_c), (U_c, b_c)), (VIO, (V_i, None), (V_o, None)),
                                (VG, (V_c, None), (V_c, None))):
                for h, (w, b) in enumerate((lo, hi)):
                    sp.dma_start(dst[0:D, 64 * h:64 * h + 64], w).then_inc(S("ld_ls"), 16)
                    if b is not None:
                        sp.dma_start(dst[D:D + 1, 64 * h:64 * h + 64], b.rearrange("(a n) -> a n", a=1)).then_inc(S("ld_ls"), 16)
            for t, v, n in ((gbr, gate_b, E), (gam, gamma, D), (bet, beta, D)):
                sp.dma_start(t[:, :], v.rearrange("(a n) -> a n", a=1).to_broadcast([128, n])).then_inc(S("ld_moe"), 16)

            ov = out.rearrange("b (m s) d -> s b m d", s=2)
            with sp.Fori(0, T // 4) as i:
                sp.wait_ge(S("l_out"), 2 * i + 2)
                for h in range(2):
                    sp.dma_start(ov[h, :, bass.ds(2 * i, 2), :], X[64 * h:64 * h + 64, bass.ds(2 * i, 2), :]).then_inc(S("st"), 16)
            sp.wait_ge(S("st"), 16 * 2 * (T // 4))

        @block.gpsimd
        def _(pool):
            done = {}

            def seq(ins, name):
                done[name] = done.get(name, 0) + 1
                ins.then_inc(S(name), 1)
                pool.wait_ge(S(name), done[name])

            seq(pool.memset(bds[:, :, :], 0.0), "bds0")
            seq(pool.memset(ident[:, :], 0.0), "id0")
            seq(pool.affine_select(out=ident[:, :], in_=ident[:, :], compare_op=ALU.not_equal, fill=1.0,
                               base=0, pattern=[[-1, 128]], channel_multiplier=1), "ident")
            seq(pool.memset(o128[:, :], 1.0 / HD), "cst")
            seq(pool.memset(cD[:, :], 1.0 / D), "cst")
            seq(pool.memset(mhalf[:, :], -0.5), "cst")
            seq(pool.memset(WB[:, :, :], 0.0), "cst")
            seq(pool.memset(lnab[:, :, 0], 1.0 / D), "cst")
            seq(pool.memset(lnab[:, :, 1], EPS), "cst")
            seq(pool.memset(lnab[:, L - 1, 0:1], (1.0 + EPS) / D), "cst")
            seq(pool.memset(lnab[:, L - 1, 1:2], EPS * EPS), "cst")
            seq(pool.tensor_copy(identb[:, :], ident[:, :]), "identb")
            seq(pool.memset(sel[:, :, :], 0.0), "sel")
            for g in range(3):
                seq(pool.affine_select(out=sel[:, :, :], in_=sel[:, :, :], compare_op=ALU.not_equal, fill=1.0,
                                   base=-E * g, pattern=[[-1, E], [0, F]], channel_multiplier=1), "sel")
            seq(pool.memset(mask[:, :, :], 0.0), "mask")
            seq(pool.memset(valid[:, :], 1.0), "mask")
            seq(pool.affine_select(out=mask[:, :, :], in_=mask[:, :, :], compare_op=ALU.is_gt, fill=NEG, base=0,
                               pattern=[[0, NP], [-1, T]], channel_multiplier=1), "mask")
            seq(pool.affine_select(out=valid[:, :], in_=valid[:, :], compare_op=ALU.is_gt, fill=0.0, base=0,
                               pattern=[[0, 1]], channel_multiplier=1), "mask")
            for e in range(E):
                seq(pool.memset(rev[:, e:e + 1], float(E - e)), "rev")
            ln_pool(pool, 0, lambda c: halves(X)[:, c % (NC // 2) * CH:(c % (NC // 2) + 1) * CH, c // (NC // 2), :])
            for i, (w, h, lo) in enumerate(((W1s, W1h, W1l), (WQs, WQKh, WQKl), (GWs, GWh, GWl))):
                pool.wait_ge(S("whi"), i + 1)
                seq(pool.tensor_tensor(lo[:, :, :] if i < 2 else lo[:, :], w[:, :, :] if i < 2 else w[:, :],
                                   (h[:, :, :] if i < 2 else h[:, :]).bitcast(F32), ALU.subtract), "wlo")
            pool.wait_ge(S("ld_at"), 16 * 6)
            pool.wait_ge(S("ld_ls"), 16 * 12)
            for t, f in ((bqk[:, 0, :], D ** -0.5), (UIO[:, :], 0.5), (VIO[:, :], 0.25), (VG[:, :], 0.5)):
                seq(pool.tensor_scalar(t, t, f, None, ALU.mult), "wsc")
            pool.wait_ge(S("ld_moe"), 16 * 8)
            seq(pool.memset(b2p[:, :, D:2 * D], 0.0), "b2z")
            for i in range(3):
                seq(pool.tensor_copy(b2p[:, i, 0:D], b2f[:, i % 2, :]), "b2c")
                if i < 2:
                    seq(pool.tensor_tensor(b2f[:, (i + 1) % 2, :], b2f[:, i % 2, :], b2p[:, i, 0:D], ALU.subtract), "b2c")
            pool.wait_ge(S("ln_c"), NC)
            pool.wait_ge(S("ld_bd"), 16 * 8)
            seq(pool.tensor_tensor(H[:, :, :], H[:, :, :], boutr[:, :].unsqueeze(1).to_broadcast([128, NM, D]), ALU.add), "hb")
            with pool.Fori(0, L) as l:
                for j in range(NJ):
                    n = l * NJ + j
                    sl = slice(j * 512, j * 512 + 512)
                    pool.wait_ge(S("s_gelu"), n + 1)
                    pool.tensor_tensor(Y1[:, sl], Y2[:, sl], ssm_cols(UT, j), ALU.add).then_inc(S("s_y"), 1)
                    if j >= 2:
                        ssm_scale(pool, l, j - 2)
                ssm_scale(pool, l, NJ - 2)
                ssm_scale(pool, l, NJ - 1)
            ln_pool(pool, 1, lambda c: X[:, c * CH:(c + 1) * CH, :])
            pool.tensor_tensor(H[:, :, :], H[:, :, :], bet[:, :].unsqueeze(1).to_broadcast([128, NM, D]), ALU.add).then_inc(S("hb"), 1)
            ln_pool(pool, 2, lambda c: X[:, c * CH:(c + 1) * CH, :], gamma_too=True)
            ln_pool(pool, 3, lambda c: X[:, c * CH:(c + 1) * CH, :])
            pool.wait_ge(S("ln_o"), 4 * NC)

            def step(i, k, first=False, last=False, drain=False):
                B = 8 * i + k
                if not has(1, k, first, drain):
                    return
                pool.wait_ge(S("a_rv"), B)
                Pn = Pb[:, (k - 1) % 4, :, :, :].rearrange("p a h j -> p (a h) j")
                pool.tensor_tensor(Pn, Pn, am[:, (k - 1) % 4, 3, :].unsqueeze(2).to_broadcast([T, NH, T]), ALU.mult).then_inc(S("a_pn"), 1)

            att_loop(pool, step)
            pool.wait_ge(S("a_pn"), NB)
            pool.wait_ge(S("ao_tp"), NQ)
            pool.memset(BIG[D:D + 1, 0:TOK], 1.0).then_inc(S("ones"), 1)
            pool.wait_ge(S("ones"), 1)
            ln_pool(pool, 4, lambda c: X[:, c * CH:(c + 1) * CH, :])

        @block.scalar
        def _(act):
            act.dma_start(Am[:, 0, :, :], A.rearrange("l n m -> n l m")).then_inc(S("ld_a"), 16)
            act.dma_start(Cs[:, :, :], Cm.rearrange("l h n -> h l n")).then_inc(S("ld_a"), 16)
            for s in range(2):
                act.dma_start(BB[:, :, s, :], Bm.rearrange("l n h -> n l h")).then_inc(S("ld_a"), 16)
            act.wait_ge(S("bds0"), 1)
            for s in range(2):
                r = slice(64 * s, 64 * s + 64)
                act.dma_start(bds[r, 0, r], Win).then_inc(S("ld_bd"), 16)
                act.dma_start(bds[r, 1:L + 1, r], Dm.rearrange("l o i -> o l i")).then_inc(S("ld_bd"), 16)
                act.dma_start(bds[r, L + 1, r], Wout).then_inc(S("ld_bd"), 16)
            for t, v in ((binr, bin_), (boutr, bout)):
                act.dma_start(t[:, :], v.rearrange("(a n) -> a n", a=1).to_broadcast([128, D])).then_inc(S("ld_bd"), 16)
            nsq = (T - 1).bit_length() - 1
            for i in range(nsq + 1):
                act.wait_ge(S("p_kry"), i + 1)
                nxt = (Am if i == 0 else (Am2 if i % 2 else Am))
                act.activation(nxt[:, 1, :, :], PS[0:D, 1, 0:L * D].rearrange("p (l m) -> p l m", l=L), ACT.Copy).then_inc(S("p_at"), 1)
            act.wait_ge(S("p_wm"), 1)
            for c in range(TX // 2 // CH):
                act.wait_ge(S("ld_x%d" % c), 32)
                act.activation(H[:, c * CH:(c + 1) * CH, :].rearrange("p m d -> p (m d)"), xcol(c, 0), ACT.Identity,
                               bias=wm[:, NF:NF + 1], scale=wm[:, 0:1]).then_inc(S("tok0"), 1)
            ln_act(act, 0)
            for j in range(NJ):
                act.wait_ge(S("w_tp"), j + 1)
                act.activation(UF[:, j * KC:(j + 1) * KC, :], bank4(4 + j % 2), ACT.Copy).then_inc(S("w_x"), 1)
            for j in range(NJ):
                act.wait_ge(S("s_tp"), j + 1)
                act.activation(UF[:, j * KC:(j + 1) * KC, :], bank4(4 + j % 2), ACT.Copy).then_inc(S("s_uf"), 1)
            with act.Fori(0, L) as l:
                for w in range(NJ + 3):
                    if w < NJ:
                        sl = slice(w * 512, w * 512 + 512)
                        act.wait_ge(S("s_y1"), l * NJ + w + 1)
                        act.activation(Y2[:, sl], Y1[:, sl], ACT.Gelu).then_inc(S("s_gelu"), 1)
                    if 0 <= w - 1 < NJ:
                        j = w - 1
                        sl = slice(j * 512, j * 512 + 512)
                        act.wait_ge(S("s_c"), l * NJ + j + 1)
                        act.activation(Y2[:, sl], XC[:, sl], ACT.Square).then_inc(S("s_q"), 1)
                    if 0 <= w - 3 < NJ:
                        j = w - 3
                        act.wait_ge(S("s_tp"), l * NJ + NJ + j + 1)
                        act.activation(UF[:, j * KC:(j + 1) * KC, :], bank4(4 + j % 2), ACT.Copy).then_inc(S("s_uf"), 1)
            ln_act(act, 1)
            xs_act(act, 0)
            act.wait_ge(S("p_wvt"), 1)
            act.activation(WvT[:, :, :], PS[:, 7, 0:NP * D].rearrange("p (c d) -> p c d", d=D), ACT.Copy).then_inc(S("WvT"), 1)
            act.wait_ge(S("gchain"), 2 + 5 + 1 + 5 + 1)
            act.activation(gs[:, 4, :], gs[:, 3, :], ACT.Exp).then_inc(S("g_exp"), 1)
            for c in range(NC):
                act.wait_ge(S("gp_tp"), c + 1)
                act.activation(GP[0:3 * E, c * 1024:(c + 1) * 1024], PSb[0:3 * E, 2 + c % 2, :], ACT.Copy).then_inc(S("gp"), 1)
            with act.Fori(0, NQ // 2) as i:
                for qq in range(2):
                    for e in range(E):
                        n = i * 2 * E + qq * E + e
                        act.wait_ge(S("m_z"), n + 1)
                        act.wait_ge(S("m_h"), n + 1)
                        act.activation(Rb[:, e % 4, :], PS[:, e % 4, :], ACT.Relu, bias=b1T[:, e:e + 1]).then_inc(S("m_r"), 1)
                    act.wait_ge(S("m_d"), i * 2 * E + (qq + 1) * E + 4)
                    act.activation(MO[:, bass.ds(i * 1024 + qq * 512, 512)], PS[:, 6 + qq, :], ACT.Copy).then_inc(S("m_mo"), 1)
            ln_act(act, 2)
            ln_act(act, 3)
            xs_act(act, 1)

            def q_evac(g, par, tile):
                sc, bi = (D ** -0.5, bqk[:, 0, tile:tile + 1]) if tile < NP else (1.0, bqk[:, 1, tile - NP:tile - NP + 1])
                act.wait_ge(S("a_q"), 2 * NP * g + tile + 1)
                act.activation(QK[par][:, tile, :], PS[:, tile % 2, 0:GB * T], ACT.Identity, bias=bi, scale=sc).then_inc(S("q_ev"), 1)

            def step(i, k, first=False, last=False, drain=False):
                B, g, bb = 8 * i + k, 2 * i + k // 4, k % 4
                nextq = not drain and not (last and k >= 4)
                if (bb == 0 and not first) or (drain and k == 3):
                    og = g - 2 + k // 3 if drain else g - 2
                    act.wait_ge(S("a_o"), og + 1)
                    o = AO.rearrange("p (t b) -> p b t", b=NB)[:, bass.ds(og * GB, GB), :]
                    ps = PS[:, 1, 0:GB * T].rearrange("p (b t) -> p b t", b=GB)
                    act.activation(o[:, :, 1:T], ps[:, :, 1:T], ACT.Identity, bias=bus[:, 1:2]).then_inc(S("o_ev"), 1)
                    act.activation(o[:, :, 0:1], ps[:, :, 0:1], ACT.Identity, bias=bus[:, 0:1]).then_inc(S("o_ev"), 1)
                if bb == 1 and not drain:
                    act.wait_ge(S("a_xt"), g + 1)
                    if not first:
                        act.wait_ge(S("a_z"), 4 * g - 4)
                    act.activation(XT[:, (k // 4) % 2, :, :], PS[0:T, 1, 0:GB * D].rearrange("p (b d) -> p b d", d=D), ACT.Copy).then_inc(S("xt_ev"), 1)
                if nextq:
                    if bb == 0 and not (first and k == 0):
                        act.wait_ge(S("a_s"), 4 * g)
                    q_evac(g + 1, (k // 4 + 1) % 2, 2 * bb)
                if has(2, k, first, drain):
                    act.wait_ge(S("a_t"), B - 1)
                    if has(4, k, first, False):
                        act.wait_ge(S("a_z"), B - 3)
                    act.activation(PT[:, k % 2, :, :], PS[0:T, 6:8, 0:NP * T], ACT.Copy).then_inc(S("pt_ev"), 1)
                if nextq:
                    q_evac(g + 1, (k // 4 + 1) % 2, 2 * bb + 1)
                if has(3, k, first, drain):
                    zg, zb = (k - 3) // 4, (k - 3) % 4
                    act.wait_ge(S("a_z"), B - 2)
                    if zb == 0 and not first:
                        act.wait_ge(S("a_o"), 2 * i + zg - 1)
                    act.activation(Zg[zg % 2][:, :, zb, :], PS[:, 0, 0:NP * T].rearrange("p (h c) -> p h c", h=NP), ACT.Copy).then_inc(S("z_ev"), 1)
                if not drain:
                    act.wait_ge(S("a_sub"), B + 1)
                    Pn = Pb[:, k % 4, :, :, :].rearrange("p a h j -> p (a h j)")
                    act.activation(Pn, Pn, ACT.Exp).then_inc(S("a_e"), 1)

            for tile in range(2 * NP):
                q_evac(0, 0, tile)
            att_loop(act, step)
            ln_act(act, 4)
            act.wait_ge(S("ones"), 1)
            for q in range(NQ):
                act.wait_ge(S("x_tp"), q + 1)
                act.activation(XF[0:D, q * 512:(q + 1) * 512], PS[0:D, q % 2, :], ACT.Copy).then_inc(S("x_f"), 1)

            def gates(i, u, first=False):
                t = 4 * i + u
                act.wait_ge(S("l_v"), t + 1)
                act.activation(Tb[:, u % 2, :], PS[:, 2 + u % 2, 0:128], ACT.Tanh).then_inc(S("l_t"), 1)
                act.wait_ge(S("l_c"), t + 1)
                act.activation(TC[64:128, :], Cb[:, 1, :], ACT.Tanh).then_inc(S("l_tc"), 1)

            for u in range(4):
                gates(0, u)
            with act.Fori(1, T // 4) as i:
                for u in range(4):
                    gates(i, u)

        @block.vector
        def _(dve):
            dve.wait_ge(S("ident"), 1)
            for h in range(2):
                dve.tensor_copy(ii[64 * h:64 * h + 64, :], ident[64 * h:64 * h + 64, 64 * h:64 * h + 64]).then_inc(S("ii"), 1)
            dve.wait_ge(S("p_wmps"), 1)
            dve.tensor_copy(wm[:, :], PS[:, 0, 0:NF + 1]).then_inc(S("p_wm"), 1)
            for h in range(2):
                dve.wait_ge(S("p_bd"), h + 1)
                dve.tensor_copy(bdt[:, 3 * h:3 * h + 3, :], PS[:, 2 + h, 0:384].rearrange("p (a c) -> p a c", a=3)).then_inc(S("p_bdt"), 1)
            nsq = (T - 1).bit_length() - 1
            dve.wait_ge(S("p_g0"), 1)
            dve.tensor_copy(Gk[:, :, 0], PS[0:D, 4, 0:L]).then_inc(S("p_gk"), 1)
            for i in range(nsq + 1):
                m = 1 << i
                nm = min(m, T - m)
                dve.wait_ge(S("p_kry"), i + 2)
                dve.tensor_copy(Gk[:, :, m:m + nm], PS[0:D, 0, 0:L * nm].rearrange("p (l m) -> p l m", l=L)).then_inc(S("p_gk"), 1)
                if i < nsq:
                    nxt = Am2 if (i + 1) % 2 else Am
                    dve.tensor_copy(nxt[:, 0, :, :], PS[0:D, 2, 0:L * D].rearrange("p (l m) -> p l m", l=L)).then_inc(S("p_am"), 1)
            dve.wait_ge(S("p_w"), 1)
            dve.wait_ge(S("cst"), 8)
            pw = PS[:, 3, 0:L * T].rearrange("p (l t) -> p l t", l=L)
            dve.tensor_copy(WB[0:64, :, T // 2:T // 2 + T - 1], pw[0:64, :, 0:T - 1]).then_inc(S("p_wb"), 1)
            dve.tensor_copy(WB[64:128, :, T:T + T // 2 - 1], pw[64:128, :, 0:T // 2 - 1]).then_inc(S("p_wb"), 1)
            for c in range(TX // 2 // CH):
                dve.wait_ge(S("tok0"), c + 1)
                hc = H[:, c * CH:(c + 1) * CH, :].rearrange("p m d -> p (m d)")
                for f in range(1, NF):
                    if f > 1:
                        dve.wait_ge(S("tokf"), (NF - 1) * c + f - 1)
                    dve.scalar_tensor_tensor(hc, xcol(c, f), wm[:, f:f + 1], hc, ALU.mult, ALU.add).then_inc(S("tokf"), 1)

            def ready(c):
                if c < TX // 2 // CH:
                    dve.wait_ge(S("tokf"), (NF - 1) * (c + 1))
                else:
                    dve.wait_ge(S("ld_txt"), 32)
            ln_dve(dve, 0, H, ready)
            dve.wait_ge(S("ld_w1"), 16 * 8)
            dve.tensor_copy(W1h[:, :, :], W1s[:, :, :]).then_inc(S("whi"), 1)
            dve.tensor_copy(WQKh[:, :, :], WQs[:, :, :]).then_inc(S("whi"), 1)
            dve.tensor_copy(GWh[:, :], GWs[:, :]).then_inc(S("whi"), 1)
            dve.wait_ge(S("ld_bd"), 16 * 8)
            for j in range(NJ):
                dve.wait_ge(S("w_mm"), j + 1)
                dve.tensor_tensor(ssm_cols(UT, j).rearrange("p (a d) -> p a d", d=D),
                                  PS[:, j % 3, :].rearrange("p (a d) -> p a d", d=D),
                                  binr[:, :].unsqueeze(1).to_broadcast([128, KC * 2, D]), ALU.add).then_inc(S("w_u"), 1)
            dve.wait_ge(S("p_b1"), 1)
            dve.tensor_copy(b1T[:, :], PS[:, 7, 0:E]).then_inc(S("b1T"), 1)
            dve.wait_ge(S("wlo"), 3)
            with dve.Fori(0, L) as l:
                dve.wait_ge(S("s_cps"), l + 1)
                cps = PS[0:64, 6, 0:T].rearrange("p (h k s) -> p k h s", h=2, s=2)
                for s in range(2):
                    dve.tensor_copy(Cc[64 * s:64 * s + 64, :, :], cps[:, :, :, s]).then_inc(S("s_cc"), 1)
                dve.wait_ge(S("s_cc"), 2 * l + 2)

                def back(j):
                    n = l * NJ + j + 1
                    sj = slice(j * KC * 2, (j + 1) * KC * 2)
                    dve.wait_ge(S("s_q"), n)
                    dve.tensor_reduce(st[:, 2, sj], Y2[:, j * 512:j * 512 + 512].rearrange("p (a d) -> p a d", d=D),
                                      AX_X, ALU.add).then_inc(S("s_v0"), 1)
                    dve.wait_ge(S("s_v0"), n)
                    dve.tensor_scalar(st[:, 2, sj], st[:, 2, sj], lnab[:, bass.ds(l, 1), 0], lnab[:, bass.ds(l, 1), 1],
                                      ALU.mult, ALU.add).then_inc(S("s_v"), 1)

                for w in range(NJ + 2):
                    if w < NJ:
                        dve.wait_ge(S("s_du"), l * NJ + w + 1)
                        dve.tensor_tensor(Y1[:, w * 512:w * 512 + 512].rearrange("p (a d) -> p a d", d=D),
                                          PS[:, w % 3, :].rearrange("p (a d) -> p a d", d=D),
                                          Cc[:, w * KC:(w + 1) * KC, :].rearrange("p k h -> p (k h)").unsqueeze(2).to_broadcast([128, KC * 2, D]),
                                          ALU.add).then_inc(S("s_y1"), 1)
                    if 0 <= w - 1 < NJ:
                        j = w - 1
                        n = l * NJ + j + 1
                        sj = slice(j * KC * 2, (j + 1) * KC * 2)
                        y = Y1[:, j * 512:j * 512 + 512].rearrange("p (a d) -> p a d", d=D)
                        dve.wait_ge(S("s_y"), n)
                        dve.tensor_reduce(st[:, 0, sj], y, AX_X, ALU.add).then_inc(S("s_s"), 1)
                        dve.wait_ge(S("s_s"), n)
                        dve.tensor_scalar(st[:, 1, sj], st[:, 0, sj], -1.0 / D, None, ALU.mult).then_inc(S("s_m"), 1)
                        dve.wait_ge(S("s_m"), n)
                        dve.tensor_tensor(XC[:, j * 512:j * 512 + 512].rearrange("p (a d) -> p a d", d=D), y,
                                          st[:, 1, sj].unsqueeze(2).to_broadcast([128, KC * 2, D]), ALU.add).then_inc(S("s_c"), 1)
                    if 0 <= w - 2 < NJ:
                        back(w - 2)
            dve.wait_ge(S("hb"), 1)
            for j in range(NJ):
                dve.wait_ge(S("o_mm"), j + 1)
                hv = view_km(H)[:, j * KC:(j + 1) * KC, :, :]
                dve.tensor_tensor(hv, PS[:, j % 3, :].rearrange("p (k h d) -> p k h d", h=2, d=D), hv, ALU.add).then_inc(S("o_h"), 1)
            ln_dve(dve, 1, H, lambda c: dve.wait_ge(S("o_h"), 2 * (c % (NC // 2)) + 2))
            xs_dve(dve, 0)
            dve.wait_ge(S("p_np"), 1)
            dve.memset(bus[D:128, :], 0.0).then_inc(S("bus0"), 1)
            dve.tensor_copy(NPt[:, :, :], PS[:, 6, 0:NP * D].rearrange("p (c d) -> p c d", d=D)).then_inc(S("NPt"), 1)
            dve.tensor_tensor(bus[0:D, 1:2], PS[0:D, 6, NP * D:NP * D + 1], bus[0:D, 0:1], ALU.add).then_inc(S("NPt"), 1)
            nch = [0]

            def link(ins):
                nch[0] += 1
                ins.then_inc(S("gchain"), 1)
                dve.wait_ge(S("gchain"), nch[0])

            def g3(i):
                return Y1[:, NM * E * i:NM * E * (i + 1)].rearrange("p (m e) -> p m e", e=E)

            def bm(i):
                return gs[:, i, :].unsqueeze(2).to_broadcast([128, NM, E])

            revb = rev[:, :].unsqueeze(1).to_broadcast([128, NM, E])
            LG, SC, K1, K2 = g3(0), g3(1), g3(2), g3(3)
            dve.wait_ge(S("ld_moe"), 16 * 8)
            dve.wait_ge(S("rev"), E)
            for h, (a, b) in enumerate(((0, 32), (32, NM))):
                dve.wait_ge(S("gt_mm"), h + 1)
                link(dve.tensor_tensor(LG[:, a:b, :], PS[:, h, 0:(b - a) * E].rearrange("p (m e) -> p m e", e=E),
                                       gbr[:, :].unsqueeze(1).to_broadcast([128, b - a, E]), ALU.add))
            for r, K in ((0, K1), (1, K2)):
                link(dve.tensor_reduce(gs[:, r, :], LG, AX_X, ALU.max))
                link(dve.tensor_tensor(SC, LG, bm(r), ALU.is_equal))
                link(dve.tensor_tensor(SC, SC, revb, ALU.mult))
                link(dve.tensor_reduce(gs[:, 2, :], SC, AX_X, ALU.max))
                link(dve.tensor_tensor(K, revb, bm(2), ALU.is_equal))
                if r == 0:
                    link(dve.scalar_tensor_tensor(LG, K, -3e38, LG, ALU.mult, ALU.add))
            link(dve.tensor_tensor(gs[:, 3, :], gs[:, 1, :], gs[:, 0, :], ALU.subtract))
            dve.wait_ge(S("g_exp"), 1)
            link(dve.tensor_scalar(gs[:, 5, :], gs[:, 4, :], 1.0, None, ALU.add))
            link(dve.reciprocal(gs[:, 6, :], gs[:, 5, :]))
            link(dve.tensor_tensor(gs[:, 7, :], gs[:, 4, :], gs[:, 6, :], ALU.mult))
            link(dve.tensor_tensor(K1, K1, bm(6), ALU.mult))
            link(dve.tensor_tensor(K2, K2, bm(7), ALU.mult))
            link(dve.tensor_tensor(LG, K1, K2, ALU.add))
            gp = GPT.rearrange("p (m g e) -> p m g e", g=3, e=E)
            link(dve.tensor_copy(gp[:, :, 0, :], LG))
            link(dve.tensor_tensor(SC, LG, gp[:, :, 0, :], ALU.subtract))
            link(dve.tensor_copy(gp[:, :, 1, :], SC))
            link(dve.tensor_tensor(K1, SC, gp[:, :, 1, :], ALU.subtract))
            dve.tensor_copy(gp[:, :, 2, :], K1).then_inc(S("g_gp"), 1)
            with dve.Fori(0, NQ // 2) as i:
                for qq in range(2):
                    for e in range(E):
                        n = i * 2 * E + qq * E + e
                        dve.wait_ge(S("m_r"), n + 5)
                        dve.wait_ge(S("m_g"), n + 1)
                        dve.wait_ge(S("m_d"), n + 1)
                        dve.tensor_tensor(Hb[:, e % 4, :], PS[:, 4 + e % 2, :], Rb[:, e % 4, :], ALU.mult).then_inc(S("m_h"), 1)

            def moe_sum(c):
                for q in (2 * c, 2 * c + 1):
                    dve.wait_ge(S("mo_tp"), q + 1)
                    ps = PS[:, 4 + q % 2, :].rearrange("p (m a d) -> p m a d", a=2, d=D)
                    y = Yt[:, q * QM:(q + 1) * QM, :]
                    dve.tensor_tensor(y, ps[:, :, 0, :], X[:, q * QM:(q + 1) * QM, :], ALU.add).then_inc(S("mo_y"), 1)
                    dve.wait_ge(S("mo_y"), 2 * q + 1)
                    dve.tensor_tensor(y, ps[:, :, 1, :], y, ALU.add).then_inc(S("mo_y"), 1)
                dve.wait_ge(S("mo_y"), 4 * c + 4)

            dve.wait_ge(S("hb"), 2)
            ln_dve(dve, 2, Yt, moe_sum)

            def residual(c):
                sc = slice(c * CH, (c + 1) * CH)
                dve.wait_ge(S("f_g"), c + 1)
                dve.tensor_tensor(H[:, sc, :], H[:, sc, :], X[:, sc, :], ALU.add).then_inc(S("f_h"), 1)
                dve.wait_ge(S("f_h"), c + 1)

            ln_dve(dve, 3, H, residual)
            xs_dve(dve, 1)

            xsb = XS[:, :].rearrange("p (t b) -> p b t", b=NB)

            def step(i, k, first=False, last=False, drain=False):
                B, g, bb = 8 * i + k, 2 * i + k // 4, k % 4
                gp = (k // 4) % 2
                if bb == 2 and not drain and not last:
                    dve.wait_ge(S("a_q"), 2 * NP * g + 2 * NP)
                    dve.wait_ge(S("a_xt"), g + 1)
                    dve.tensor_copy(XSg[:, gp, :, :], xsb[:, bass.ds(GB * g + 2 * GB, GB), :]).then_inc(S("a_st"), 1)
                if has(1, k, first, drain):
                    s1 = am[:, (k - 1) % 4, :, :]
                    dve.wait_ge(S("a_e"), B)
                    dve.tensor_reduce(s1[:, 1, :], Pb[:, (k - 1) % 4, :, :, :].rearrange("p a h j -> p (a h) j"),
                                      AX_X, ALU.add).then_inc(S("a_sm"), 1)
                    dve.wait_ge(S("a_sm"), B)
                    dve.reciprocal(s1[:, 2, :], s1[:, 1, :]).then_inc(S("a_rc"), 1)
                    dve.wait_ge(S("a_rc"), B)
                    dve.tensor_scalar(s1[:, 3, :], s1[:, 2, :], valid[:, 0:1], None, ALU.mult).then_inc(S("a_rv"), 1)
                if drain:
                    return
                ps = PS[0:T, 2 + 2 * (k % 2):4 + 2 * (k % 2), 0:NP * T].rearrange("p a (h j) -> p a h j", h=NP)
                dve.wait_ge(S("a_s"), B + 1)
                dve.tensor_reduce(am[:, k % 4, 0, :], ps, AX_X, ALU.max).then_inc(S("a_mx"), 1)
                dve.wait_ge(S("a_mx"), B + 1)
                if not (first and k < 4):
                    dve.wait_ge(S("a_t"), B - 3)
                mx = am[:, k % 4, 0, :].rearrange("p (a h) -> p a h", a=2)
                for a in range(2):
                    dve.tensor_tensor(Pb[:, k % 4, a, :, :], ps[:, a, :, :], mx[:, a, :].unsqueeze(2).to_broadcast([T, NP, T]),
                                      ALU.subtract).then_inc(S("a_sub%d" % a if a == 0 else "a_sub"), 1)

            dve.wait_ge(S("mask"), 4)
            dve.wait_ge(S("xs_l"), 4 * NC)
            for g in range(2):
                dve.tensor_copy(XSg[:, g, :, :], xsb[:, g * GB:(g + 1) * GB, :]).then_inc(S("a_st"), 1)
            att_loop(dve, step)

            def att_residual(c):
                for a in range(2):
                    for q in (2 * c, 2 * c + 1):
                        ps = PS[:, 4 + q % 4, :].rearrange("p (m a d) -> p m a d", a=2, d=D)
                        hc = H[:, q * QM:(q + 1) * QM, :]
                        if a == 0:
                            dve.wait_ge(S("ao_tp"), q + 1)
                        else:
                            dve.wait_ge(S("a_h"), 4 * c + q % 2 + 1)
                        dve.tensor_tensor(hc, ps[:, :, a, :], hc, ALU.add).then_inc(S("a_h"), 1)
                dve.wait_ge(S("a_h"), 4 * c + 4)

            ln_dve(dve, 4, H, att_residual)

            def cell(i, u, first=False):
                t = 4 * i + u
                tb = Tb[:, u % 2, :]
                if not first and u % 2 == 0:
                    dve.wait_ge(S("l_tp"), 2 * i + u // 2 - 1)
                dve.wait_ge(S("l_t"), t + 1)
                dve.scalar_tensor_tensor(Cb[:, 0, :], tb[0:64, 0:64], 1.0, tb[0:64, 64:128], ALU.add, ALU.mult).then_inc(S("l_a"), 1)
                dve.wait_ge(S("l_a"), t + 1)
                if first and u == 0:
                    dve.tensor_scalar(Cb[:, 1, :], Cb[:, 0, :], 0.5, None, ALU.mult).then_inc(S("l_c"), 1)
                else:
                    dve.wait_ge(S("l_hc"), t)
                    dve.scalar_tensor_tensor(Cb[:, 1, :], Cb[:, 0, :], 0.5, HC[:, :], ALU.mult, ALU.add).then_inc(S("l_c"), 1)
                dve.wait_ge(S("l_tc"), t + 1)
                dve.scalar_tensor_tensor(HB[:, u, :], tb[64:128, 0:64], 1.0, TC[64:128, :], ALU.add, ALU.mult).then_inc(S("l_h"), 1)
                dve.wait_ge(S("l_h"), t + 1)
                dve.scalar_tensor_tensor(HC[:, :], HB[:, u, :], 0.5, Cb[:, 1, :], ALU.mult, ALU.mult).then_inc(S("l_hc"), 1)
                if u % 2 == 0 and not (first and u == 0):
                    output(2 * i + u // 2 - 1, (u // 2 - 1) % 2)

            def output(m, par):
                dve.wait_ge(S("l_tp"), m + 1)
                dve.scalar_tensor_tensor(X[:, bass.ds(m, 1), :].rearrange("p a d -> p (a d)"), PS[:, 4 + par, 0:D], 0.5,
                                         H[:, bass.ds(m, 1), :].rearrange("p a d -> p (a d)"), ALU.mult, ALU.add).then_inc(S("l_out"), 1)

            for u in range(4):
                cell(0, u, first=True)
            with dve.Fori(1, T // 4) as i:
                for u in range(4):
                    cell(i, u)
            output(NM - 1, 1)

        @block.tensor
        def _(pe):
            pe.wait_ge(S("cst"), 1)
            pe.wait_ge(S("ld_tok"), 32)
            pe.matmul(PS[:, 0, 0:NF + 1], o128[:, :], wtok[:, :], start=True, stop=True).then_inc(S("p_wmps"), 1)
            pe.wait_ge(S("ident"), 1)
            pe.wait_ge(S("ld_a"), 64)
            for l in range(L):
                last = pe.transpose(PS[0:D, 1, l * D:l * D + D], Am[:, 0, l, :], ident[0:D, 0:D])
            last.then_inc(S("p_kry"), 1)
            pe.wait_ge(S("cst"), 2)
            for l in range(L):
                last = pe.matmul(PS[0:D, 4, l:l + 1], Cs[:, l, :], cD[0:D, :], start=True, stop=True)
            last.then_inc(S("p_g0"), 1)
            pe.wait_ge(S("ld_bd"), 16 * 8)
            for h in range(2):
                for a in range(3):
                    last = pe.transpose(PS[:, 2 + h, a * 128:a * 128 + 128], bds[:, 3 * h + a, :], ident[:, :])
                last.then_inc(S("p_bd"), 1)
            nsq = (T - 1).bit_length() - 1
            pe.wait_ge(S("p_bdt"), 2)
            pe.wait_ge(S("p_wm"), 1)
            for i in range(nsq + 1):
                m = 1 << i
                nm = min(m, T - m)
                cur = Am if i % 2 == 0 else Am2
                pe.wait_ge(S("p_gk"), i + 1)
                if i:
                    pe.wait_ge(S("p_am"), i)
                pe.wait_ge(S("p_at"), i + 1)
                for l in range(L):
                    last = pe.matmul(PS[0:D, 0, l * nm:l * nm + nm], cur[:, 0, l, :], Gk[:, l, 0:nm], start=True, stop=True)
                if i < nsq:
                    for l in range(L):
                        pe.matmul(PS[0:D, 2, l * D:l * D + D], cur[:, 1, l, :], cur[:, 0, l, :], start=True, stop=True)
                    for l in range(L):
                        last = pe.matmul(PS[0:D, 1, l * D:l * D + D], cur[:, 0, l, :], cur[:, 1, l, :], start=True, stop=True)
                last.then_inc(S("p_kry"), 1)
            pe.wait_ge(S("p_gk"), nsq + 2)
            for l in range(L):
                last = pe.matmul(PS[:, 3, l * T:l * T + T], BB[:, l, :, :].rearrange("p a b -> p (a b)"), Gk[:, l, :], start=True, stop=True)
            last.then_inc(S("p_w"), 1)
            pe.wait_ge(S("ld_moe"), 16 * 8)
            pe.transpose(PS[:, 7, 0:E], b1s[:, :], ident[0:E, 0:E]).then_inc(S("p_b1"), 1)
            xk = halves(X)
            for j in range(NJ):
                pe.wait_ge(S("ln_o"), NC)
                if j >= 2:
                    pe.wait_ge(S("w_x"), j - 1)
                for k in range(KC):
                    last = pe.transpose(PS[:, 4 + j % 2, k * 128:k * 128 + 128], xk[:, j * KC + k, :, :].rearrange("p h d -> p (h d)"), ident[:, :])
                last.then_inc(S("w_tp"), 1)
                if j == 0:
                    pe.wait_ge(S("p_gk"), nsq + 2)
            for j in range(NJ):
                pe.wait_ge(S("w_x"), j + 1)
                if j >= 3:
                    pe.wait_ge(S("w_u"), j - 2)
                for k in range(KC):
                    last = pe.matmul(PS[:, j % 3, k * 128:k * 128 + 128], UF[:, j * KC + k, :], bdt[:, 0, :], start=True, stop=True)
                last.then_inc(S("w_mm"), 1)
            for j in range(NJ):
                pe.wait_ge(S("w_u"), j + 1)
                if j < 2:
                    pe.wait_ge(S("w_x"), NJ - 1 + j)
                if j >= 2:
                    pe.wait_ge(S("s_uf"), j - 1)
                for k in range(KC):
                    last = pe.transpose(PS[:, 4 + j % 2, k * 128:k * 128 + 128], UT[:, j * KC + k, :, :].rearrange("p h d -> p (h d)"), ident[:, :])
                last.then_inc(S("s_tp"), 1)
            pe.wait_ge(S("p_wb"), 2)
            with pe.Fori(0, L) as l:
                for tt in range(T // 2):
                    if tt % (2 * KC) == 0:
                        pe.wait_ge(S("s_uf"), l * NJ + tt // (2 * KC) + 1)
                    o = T // 2 - 1 - tt
                    last = pe.matmul(PS[0:64, 6, 0:T], UF[:, tt // 2, 64 * (tt % 2):64 * (tt % 2) + 64],
                                     WB[:, bass.ds(l, 1), o:o + T].rearrange("p a t -> p (a t)"), start=(tt == 0), stop=(tt == T // 2 - 1))
                last.then_inc(S("s_cps"), 1)
                for j in range(NJ):
                    if j >= 3:
                        pe.wait_ge(S("s_y1"), l * NJ + j - 2)
                    for k in range(KC):
                        last = pe.matmul(PS[:, j % 3, k * 128:k * 128 + 128], UF[:, j * KC + k, :],
                                         bdt[:, bass.ds(l + 1, 1), :].rearrange("p a t -> p (a t)"), start=True, stop=True)
                    last.then_inc(S("s_du"), 1)
                for j in range(NJ):
                    pe.wait_ge(S("s_un"), l * NJ + j + 1)
                    pe.wait_ge(S("s_uf"), l * NJ + NJ + j - 1)
                    for k in range(KC):
                        last = pe.transpose(PS[:, 4 + j % 2, k * 128:k * 128 + 128], UT[:, j * KC + k, :, :].rearrange("p h d -> p (h d)"), ident[:, :])
                    last.then_inc(S("s_tp"), 1)
            for j in range(NJ):
                pe.wait_ge(S("s_uf"), L * NJ + j + 1)
                if j < 3:
                    pe.wait_ge(S("s_y1"), L * NJ - 2 + j)
                else:
                    pe.wait_ge(S("o_h"), j - 2)
                for k in range(KC):
                    last = pe.matmul(PS[:, j % 3, k * 128:k * 128 + 128], UF[:, j * KC + k, :], bdt[:, L + 1, :], start=True, stop=True)
                last.then_inc(S("o_mm"), 1)
            xs_pe(pe, 0, 1)
            pe.wait_ge(S("ld_at"), 16 * 6)
            for c in range(NP):
                last = pe.transpose(PS[:, 7, c * D:(c + 1) * D], Wvs[:, c * 128:(c + 1) * 128], ident[0:D, 0:D])
            last.then_inc(S("p_wvt"), 1)
            pe.wait_ge(S("WvT"), 1)
            for c in range(NP):
                for a in range(2):
                    r = slice(64 * a, 64 * a + 64)
                    pe.matmul(PS[r, 6, c * D:(c + 1) * D], WvT[r, c, :], Wus[r, c, :], start=True, stop=True)
            for c in range(NP):
                last = pe.matmul(PS[0:D, 6, NP * D:NP * D + 1], Wus[:, c, :], bvs[:, c:c + 1], start=(c == 0), stop=(c == NP - 1))
            last.then_inc(S("p_np"), 1)
            pe.wait_ge(S("wlo"), 3)
            pe.wait_ge(S("o_h"), NJ)
            for m in range(NM):
                if m % CH == 0:
                    pe.wait_ge(S("xs_l"), 2 * (m // CH) + 2)
                o = PS[:, m // 32, (m % 32) * E:(m % 32 + 1) * E]
                pe.matmul(o, XS[:, m * 128:(m + 1) * 128], GWh[:, :], start=True, stop=False)
                last = pe.matmul(o, XS[:, m * 128:(m + 1) * 128], GWl[:, :], start=False, stop=True)
                if m in (31, NM - 1):
                    last.then_inc(S("gt_mm"), 1)
            pe.wait_ge(S("g_gp"), 1)
            pe.wait_ge(S("identb"), 1)
            for c in range(NC):
                if c >= 2:
                    pe.wait_ge(S("gp"), c - 1)
                for k in range(8):
                    last = pe.transpose(PSb[0:3 * E, 2 + c % 2, k * 128:(k + 1) * 128],
                                        GPT[:, (c * 8 + k) * 3 * E:(c * 8 + k + 1) * 3 * E], identb[:, :])
                last.then_inc(S("gp_tp"), 1)
            pe.wait_ge(S("gp"), NC)
            pe.wait_ge(S("b2c"), 5)
            pe.wait_ge(S("b2z"), 1)
            pe.wait_ge(S("sel"), 4)
            pe.wait_ge(S("ld_moe"), 16 * 8)
            grant(pe, "m_r", 4)
            grant(pe, "m_h", 4)
            grant(pe, "m_d", 4)
            grant(pe, "m_mo", 2)
            with pe.Fori(0, NQ // 2) as i:
                for qq in range(2):
                    col = i * 1024 + qq * 512
                    acc = PS[:, 6 + qq, :]

                    def down(e):
                        pe.wait_ge(S("m_h"), i * 2 * E + qq * E + e + 5)
                        pe.matmul(acc[64 * (e % 2):64 * (e % 2) + 64], w2s[:, e, :], Hb[:, e % 4, :],
                                  start=False, stop=(e >= E - 2)).then_inc(S("m_d"), 1)

                    for e in range(E):
                        n = i * 2 * E + qq * E + e
                        if e == 0:
                            pe.wait_ge(S("m_mo"), i * 2 + qq + 1)
                        pe.wait_ge(S("m_h"), n + 3)
                        pe.wait_ge(S("m_r"), n + 1)
                        pe.matmul(PS[:, e % 4, :], W1h[:, e, :], XS[:, bass.ds(col, 512)], start=True, stop=False)
                        pe.matmul(PS[:, e % 4, :], W1l[:, e, :], XS[:, bass.ds(col, 512)], start=False, stop=True).then_inc(S("m_z"), 1)
                        if e == 0:
                            for g in range(3):
                                pe.matmul(acc, b2p[:, g, :], GP[0:3 * E, bass.ds(col, 512)], start=(g == 0), stop=False)
                        pe.matmul(PS[:, 4 + e % 2, :], sel[:, e, :], GP[0:3 * E, bass.ds(col, 512)], start=True, stop=True).then_inc(S("m_g"), 1)
                        if e % 2 and e >= 3:
                            down(e - 3)
                            down(e - 2)
                    down(E - 2)
                    down(E - 1)
            for q in range(NQ):
                pe.wait_ge(S("m_mo"), 2 + q + 1)
                if q >= 2:
                    pe.wait_ge(S("mo_y"), 2 * (q - 1))
                else:
                    pe.wait_ge(S("m_h"), 4 + NQ * E)
                for k in range(QM):
                    m = q * QM + k
                    last = pe.transpose(PS[:, 4 + q % 2, k * 128:(k + 1) * 128], MO[:, m * 128:(m + 1) * 128], ident[:, :])
                last.then_inc(S("mo_tp"), 1)
            xs_pe(pe, 1, 3)

            def q_tile(par, tile):
                W = (WQKh, WQKl)
                for a in range(2):
                    last = pe.matmul(PS[:, tile % 2, 0:GB * T], W[a][:, tile // NP, (tile % NP) * 128:(tile % NP + 1) * 128],
                                     XSg[:, par, :, :].rearrange("p b t -> p (b t)"), start=(a == 0), stop=(a == 1))
                last.then_inc(S("a_q"), 1)

            def step(i, k, first=False, last=False, drain=False):
                B, g, bb = 8 * i + k, 2 * i + k // 4, k % 4
                gp = (k // 4) % 2
                nq = 2 * NP
                if not drain:
                    if bb == 0:
                        pe.wait_ge(S("q_ev"), nq * g + nq)
                    if has(2, k, first, False):
                        pe.wait_ge(S("a_sub"), B - 1)
                    for a in range(2):
                        pe.matmul(PS[0:T, 2 + 2 * (k % 2) + a, 0:NP * T], identb[0:T, 0:T],
                                  mask[:, :, :].rearrange("p h j -> p (h j)"), start=True, stop=False)
                    for h in range(NP):
                        for a in range(2):
                            r = slice(64 * a, 64 * a + 64)
                            mm = pe.matmul(PS[0:T, 2 + 2 * (k % 2) + a, h * T:(h + 1) * T], QK[gp][r, h, bb * T:(bb + 1) * T],
                                           QK[gp][r, NP + h, bb * T:(bb + 1) * T], start=False, stop=(h == NP - 1))
                    mm.then_inc(S("a_s"), 1)
                nextq = not drain and not (last and k >= 4)
                if (bb == 0 and not first) or (drain and k == 3):
                    og = g - 2 + k // 3 if drain else g - 2
                    pe.wait_ge(S("z_ev"), 4 * og + 4)
                    if drain:
                        if k == 0:
                            pe.wait_ge(S("xt_ev"), g)
                        else:
                            pe.wait_ge(S("o_ev"), 2 * g - 2)
                    for h in range(NP):
                        r = slice(64 * (h % 2), 64 * (h % 2) + 64)
                        mm = pe.matmul(PS[r, 1, 0:GB * T], NPt[:, h, :], Zg[(k // 4 + k // 3 * drain) % 2][:, h, :, :].rearrange("p b t -> p (b t)"),
                                       start=(h < 2), stop=(h >= NP - 2))
                    mm.then_inc(S("a_o"), 1)
                if bb == 1 and not drain:
                    if nextq:
                        pe.wait_ge(S("q_ev"), nq * (g + 1) + 2)
                    else:
                        pe.wait_ge(S("o_ev"), 2 * g - 2)
                    for b in range(GB):
                        mm = pe.matmul(PS[0:T, 1, b * D:(b + 1) * D], XSg[:, gp, b, :], ii[:, :], start=True, stop=True)
                    mm.then_inc(S("a_xt"), 1)
                if nextq:
                    if bb == 0:
                        pe.wait_ge(S("a_st"), g + 2)
                    if has(4, k, first, False):
                        pe.wait_ge(S("z_ev"), B - 3)
                    elif k:
                        pe.wait_ge(S("q_ev"), nq * (g + 1) + 2 * bb - 1)
                    q_tile(1 - gp, 2 * bb)
                if has(2, k, first, drain):
                    pe.wait_ge(S("a_pn"), B - 1)
                    if has(3, k, first, False):
                        pe.wait_ge(S("pt_ev"), B - 2)
                    for h in range(NP):
                        for a in range(2):
                            mm = pe.transpose(PS[0:T, 6 + a, h * T:(h + 1) * T], Pb[:, (k - 2) % 4, a, h, :], ident[0:T, 0:T])
                    mm.then_inc(S("a_t"), 1)
                if nextq:
                    if bb == 0 and not first:
                        pe.wait_ge(S("o_ev"), 2 * g - 2)
                    if bb == 1:
                        pe.wait_ge(S("xt_ev"), g + 1)
                    if bb >= 2:
                        pe.wait_ge(S("q_ev"), nq * (g + 1) + 2 * bb)
                    q_tile(1 - gp, 2 * bb + 1)
                if has(3, k, first, drain):
                    zg = (k - 3) // 4
                    pe.wait_ge(S("pt_ev"), B - 2)
                    if nextq:
                        pe.wait_ge(S("q_ev"), nq * (g + 1) + 2 * bb + 1)
                    elif has(4, k, first, False):
                        pe.wait_ge(S("z_ev"), B - 3)
                    for a in range(2):
                        mm = pe.matmul(PS[64 * a:64 * a + 64, 0, 0:NP * T], XT[:, zg % 2, (k - 3) % 4, :],
                                       PT[:, (k - 3) % 2, a, :], start=True, stop=True)
                    mm.then_inc(S("a_z"), 1)

            pe.wait_ge(S("a_st"), 1)
            pe.wait_ge(S("wsc"), 4)
            pe.wait_ge(S("mask"), 4)
            pe.wait_ge(S("ii"), 2)
            pe.wait_ge(S("NPt"), 2)
            pe.wait_ge(S("bus0"), 1)
            for tile in range(2 * NP):
                if tile >= 2:
                    pe.wait_ge(S("q_ev"), tile - 1)
                q_tile(0, tile)
            att_loop(pe, step)
            for q in range(NQ):
                pe.wait_ge(S("o_ev"), 2 * NG)
                if q >= 4:
                    pe.wait_ge(S("a_h"), 4 * (q // 2 - 2) + 3 + q % 2)
                for k in range(QM):
                    m = q * QM + k
                    mm = pe.transpose(PS[:, 4 + q % 4, k * 128:(k + 1) * 128], AO[:, m * 128:(m + 1) * 128], ident[:, :])
                mm.then_inc(S("ao_tp"), 1)
            for q in range(NQ):
                pe.wait_ge(S("ln_o"), 4 * NC + q // 2 + 1)
                if q >= 2:
                    pe.wait_ge(S("x_f"), q - 1)
                for k in range(4):
                    mm = pe.transpose(PS[0:D, q % 2, k * 128:(k + 1) * 128], X[:, 4 * q + k, :], ident[:, :])
                mm.then_inc(S("x_tp"), 1)

            def gates_x(i, u, first=False):
                xt = XF[:, bass.ds(256 * i + 64 * u, 64)]
                bank = PS[:, 2 + u % 2, :]
                if not (first and u < 2):
                    pe.wait_ge(S("l_t"), 4 * i + u - 1)
                if u % 2 == 0 and not first:
                    pe.wait_ge(S("l_out"), 2 * i + u // 2 - 2)
                pe.matmul(bank[:, 0:64], UIO[:, :], xt, start=True, stop=False, skip_group_check=True)
                n = 128 if first and u < 2 else 64
                mm = pe.matmul(bank[0:n, 64:128], UG[:, 0:n], xt, start=False, stop=(first and u == 0), skip_group_check=True)
                if first and u == 0:
                    mm.then_inc(S("l_v"), 1)

            def gates_h(i, u, first=False):
                bank = PS[:, 2 + u % 2, :]
                pe.wait_ge(S("l_h"), 4 * i + u)
                pe.nop().then_inc(S("l_hp"), 1)
                hp = HB[:, (u - 1) % 4, :]
                for h in range(2):
                    r = slice(64 * h, 64 * h + 64)
                    pe.matmul(bank[r, 0:64], VIO[:, r], hp, start=False, stop=True, skip_group_check=True)
                pe.matmul(bank[0:64, 64:128], VG[:, 0:64], hp, start=False, stop=True, skip_group_check=True).then_inc(S("l_v"), 1)
                if u % 2 == 0:
                    out_tp((u // 2 - 1) % 2)

            def out_tp(par):
                pe.transpose(PS[:, 4 + par, 0:D], HB[:, 2 * par:2 * par + 2, :].rearrange("p a b -> p (a b)"), ident[0:D, 0:D]).then_inc(S("l_tp"), 1)

            pe.wait_ge(S("x_f"), NQ)
            pe.wait_ge(S("a_h"), 4 * NC)
            gates_x(0, 0, first=True)
            for u in range(1, 4):
                gates_x(0, u, first=True)
                gates_h(0, u, first=True)
            with pe.Fori(1, T // 4) as i:
                for u in range(4):
                    gates_x(i, u)
                    gates_h(i, u)
            pe.wait_ge(S("l_out"), NM - 2)
            pe.wait_ge(S("l_h"), T)
            out_tp(1)


_INS = ["x", "txt", "L0_tok_W", "L0_tok_b", "L0_attn_Win", "L0_attn_bin_", "L0_attn_Wout", "L0_attn_bout",
        "L0_attn_A", "L0_attn_Bm", "L0_attn_Cm", "L0_attn_Dm",
        "L0_ffn_gate_w", "L0_ffn_gate_b", "L0_ffn_w1", "L0_ffn_b1", "L0_ffn_w2", "L0_ffn_b2",
        "L0_ffn_gamma", "L0_ffn_beta",
        "L1_attn_Wq", "L1_attn_bq", "L1_attn_Wk", "L1_attn_bk", "L1_attn_Wv", "L1_attn_bv",
        "L1_attn_Wu", "L1_attn_bu",
        "L1_ffn_U_i", "L1_ffn_V_i", "L1_ffn_b_i", "L1_ffn_U_c", "L1_ffn_V_c", "L1_ffn_b_c",
        "L1_ffn_U_o", "L1_ffn_V_o", "L1_ffn_b_o"]


def kernel(**inputs):
    import numpy as np
    import concourse.bacc as bacc
    from concourse.bass_utils import run_bass_kernel_spmd

    nc = bacc.Bacc("TRN2", target_bir_lowering=False, num_devices=1)
    arrays, args = {}, []
    for name in _INS:
        a = np.ascontiguousarray(inputs[name])
        arrays["in_" + name] = a
        args.append(nc.dram_tensor("in_" + name, a.shape, mybir.dt.from_np(a.dtype), kind="ExternalInput").ap())
    b, tx, d, _ = inputs["x"].shape
    shape = (b, tx + inputs["txt"].shape[1], d)
    out = nc.dram_tensor("out_0", shape, F32, kind="ExternalOutput").ap()
    early_fusion(nc, *args, out)
    r = run_bass_kernel_spmd(nc, [arrays], core_ids=[0])
    return r.results[0]["out_0"]
```

```python
from contextlib import ExitStack

import concourse.bass as bass
from concourse import mybir

F32 = mybir.dt.float32
F32R = mybir.dt.float32r
BF16 = mybir.dt.bfloat16
ALU = mybir.AluOpType
ACT = mybir.ActivationFunctionType
AX_X = mybir.AxisListType.X



def early_fusion(nc, x, txt, tok_W, tok_b, Win, bin_, Wout, bout, A, Bm, Cm, Dm,
                 gate_w, gate_b, w1, b1, w2, b2, gamma, beta,
                 Wq, bq, Wk, bk, Wv, bv, Wu, bu,
                 U_i, V_i, b_i, U_c, V_c, b_c, U_o, V_o, b_o, out):
    NB, TX, D, NF = x.shape
    TT = txt.shape[1]
    T = TX + TT
    NM = T // 2
    NK = NM // 2
    TOK = T * NB
    L = A.shape[0]
    HD = tok_W.shape[0]
    E, _, F = w1.shape
    NH = Wq.shape[1] // D
    NP = NH // 2
    EPS = 1e-5
    NEG = -1e30
    CH = 8
    NC = NM // CH
    KC = 4
    NJ = NK // KC
    QM = 4
    NQ = NM // QM
    GB = 4
    NG = NB // GB
    WBW = T // 2 + T - 1
    assert NB == 64 and D == 64 and F == 128 and T % 4 == 0 and NK % KC == 0

    with ExitStack() as ctx:
        def sb(name, shape, dt=F32):
            return ctx.enter_context(nc.sbuf_tensor(name, shape, dt))

        def sem(name):
            return ctx.enter_context(nc.semaphore(name))

        H = sb("H", [128, NM, D])
        X = sb("X", [128, NM, D])
        UT = sb("UT", [128, NK, 2, D])
        UF = sb("UF", [128, NK, 128])
        Y1 = sb("Y1", [128, NM * D])
        Y2 = sb("Y2", [128, NM * D])
        XC = sb("XC", [128, NM * D])
        BIG = sb("BIG", [128, 32 * D * NF])
        XS = sb("XS", [128, TOK], F32R)
        ident = sb("ident", [128, 128])
        identb = sb("identb", [128, 128], BF16)
        ii = sb("ii", [128, D], F32R)
        o128 = sb("o128", [128, 128])
        cD = sb("cD", [128, 1])
        mhalf = sb("mhalf", [128, 64])
        wtok = sb("wtok", [128, NF + 1])
        wm = sb("wm", [128, NF + 1])
        bds = sb("bds", [128, L + 2, 128])
        bdt = sb("bdt", [128, L + 2, 128])
        binr = sb("binr", [128, D])
        boutr = sb("boutr", [128, D])
        Am = sb("Am", [D, 2, L, D])
        Am2 = sb("Am2", [D, 2, L, D])
        Cs = sb("Cs", [D, L, D])
        Gk = sb("Gk", [D, L, T])
        BB = sb("BB", [D, L, 2, D])
        WQKh = sb("WQKh", [128, 2, NH * D], F32R)
        WQKl = sb("WQKl", [128, 2, NH * D], F32R)
        WB = sb("WB", [128, L, WBW + 1])
        scr = sb("scr", [128, 1])
        lnab = sb("lnab", [128, L, 2])
        Cc = sb("Cc", [128, NK, 2])
        st = sb("st", [128, 4, NM])
        W1h = sb("W1h", [128, E, F], F32R)
        W1l = sb("W1l", [128, E, F], F32R)
        GWs = sb("GWs", [128, E])
        GWhl = sb("GWhl", [128, 2, E], F32R)
        gbr = sb("gbr", [128, E])
        b1s = sb("b1s", [E, F])
        b1T = sb("b1T", [F, E])
        w2s = sb("w2s", [F, E, D])
        b2f = sb("b2f", [3 * E, 2, D])
        b2p = sb("b2p", [3 * E, 3, 2 * D], BF16)
        gs = sb("gs", [128, 8, NM])
        sel = sb("sel", [3 * E, E, F], BF16)
        rev = sb("rev", [128, E])
        gam = sb("gam", [128, D])
        bet = sb("bet", [128, D])
        XSg = sb("XSg", [128, 2, GB, T], F32R)
        mask = sb("mask", [T, NP, T], BF16)
        valid = sb("valid", [T, 1])
        Wvs = sb("Wvs", [D, NH * D])
        WvT = sb("WvT", [128, NP, D])
        Wus = sb("Wus", [128, NP, D])
        NPt = sb("NPt", [128, NP, D])
        bqk = sb("bqk", [128, 2, NP])
        bvs = sb("bvs", [128, NP])
        bus = sb("bus", [128, 2])
        am = sb("am", [T, 4, 4, NH])
        UIO = sb("UIO", [D + 1, 128])
        UG = sb("UG", [D + 1, 128])
        VIO = sb("VIO", [D, 128])
        VG = sb("VG", [D, D])
        sems = {}

        def S(name):
            if name not in sems:
                sems[name] = sem(name)
            return sems[name]

        PS = ctx.enter_context(nc.psum_tensor("PS", [128, 8, 512], F32))

        W1s = Y1[:, 0:E * F].rearrange("p (e f) -> p e f", e=E)
        WQs = Y1[:, E * F:E * F + 2 * NH * D].rearrange("p (a c) -> p a c", a=2)
        GPT = UT[:, :, :, :].rearrange("p k h d -> p (k h d)").bitcast(BF16)[:, 0:NM * 3 * E]
        GP = UF[:, :, :].rearrange("p k c -> p (k c)").bitcast(BF16)
        PSb = PS[:, :, :].bitcast(BF16)
        MO = BIG[:, 0:2 * 512]
        Rb = Y2[:, 0:2048].rearrange("p (a c) -> p a c", a=4)
        Hb = XC[:, 0:2048].rearrange("p (a c) -> p a c", a=4)
        XF = BIG[0:D + 1, 0:TOK]
        AO = BIG[:, 0:TOK]
        QK = [t.rearrange("p (a c) -> p a c", a=2 * NP) for t in (UT[:, :, :, :].rearrange("p k h d -> p (k h d)"),
                                                                  UF[:, :, :].rearrange("p k c -> p (k c)"))]
        Pb = Y1[0:T, 0:4 * NH * T].rearrange("p (n a h j) -> p n a h j", n=4, a=2, h=NP)
        XT = XC[0:T, NP * GB * T:NP * GB * T + 2 * GB * D].rearrange("p (n b d) -> p n b d", n=2, b=GB)
        PT = Y2[0:T, 0:2 * NH * T].rearrange("p (n a c) -> p n a c", n=2, a=2)
        Zg = [t.rearrange("p (h b i) -> p h b i", h=NP, b=GB) for t in (Y2[:, 2 * NH * T:2 * NH * T + NP * GB * T],
                                                                        XC[:, 0:NP * GB * T])]
        UTf = UT[:, :, :, :].rearrange("p k h d -> p (k h d)")
        Tb = UTf[:, 0:256].rearrange("p (a c) -> p a c", a=2)
        TC = UTf[:, 256:320]
        Cb = UTf[0:D, 320:448].rearrange("p (a c) -> p a c", a=2)
        HC = UTf[0:D, 448:512]
        HB = UTf[0:D, 512:768].rearrange("p (a c) -> p a c", a=4)
        Ysum = Y1[:, 0:512].rearrange("p (m d) -> p m d", d=D)
        Ygam = Y1[:, 512:1024].rearrange("p (m d) -> p m d", d=D)
        Ynrm = Y1[:, 1024:1536].rearrange("p (m d) -> p m d", d=D)
        Ycen = XC[:, 2048:3072].rearrange("p (r m d) -> p r m d", r=2, d=D)
        Ysqr = Y2[:, 2048:3072].rearrange("p (r m d) -> p r m d", r=2, d=D)
        Xr = BIG[:, :].rearrange("p (m c) -> p m c", c=D * NF)

        def halves(t):
            return t[:, :, :].rearrange("p (k h) d -> p k h d", h=2)

        def view_km(t):
            return t[:, :, :].rearrange("p (h k) d -> p k h d", h=2)

        def ssm_scale(pool, l, j):
            n = l * NJ + j
            sj = slice(j * KC * 2, (j + 1) * KC * 2)
            pool.wait_ge(S("s_v"), n + 1)
            pool.tensor_tensor(st[:, 3, sj], st[:, 2, sj], mhalf[:, 0:KC * 2], ALU.pow).then_inc(S("s_r"), 1)
            pool.wait_ge(S("s_r"), n + 1)
            pool.tensor_tensor(ssm_cols(UT, j).rearrange("p (a d) -> p a d", d=D),
                               XC[:, j * 512:j * 512 + 512].rearrange("p (a d) -> p a d", d=D),
                               st[:, 3, sj].unsqueeze(2).to_broadcast([128, KC * 2, D]), ALU.mult).then_inc(S("s_un"), 1)

        def ssm_cols(t, j):
            return t[:, j * KC:(j + 1) * KC, :, :].rearrange("p k h d -> p (k h d)")

        def ln_dve(dve, p, src, ready, order=range(NC), between=None):
            def front(i, c):
                n = p * NC + i + 1
                sc = slice(c * CH, (c + 1) * CH)
                ready(c)
                dve.tensor_reduce(st[:, 0, sc], src[:, sc, :], AX_X, ALU.add).then_inc(S("ln_s"), 1)
                dve.wait_ge(S("ln_s"), n)
                dve.scalar_tensor_tensor(XC[:, c * 512:c * 512 + 512].rearrange("p (a d) -> p a d", d=D),
                                         st[:, 0, sc].unsqueeze(2).to_broadcast([128, CH, D]), -1.0 / D, src[:, sc, :],
                                         ALU.mult, ALU.add).then_inc(S("ln_c"), 1)

            def back(i, c):
                n = p * NC + i + 1
                sc = slice(c * CH, (c + 1) * CH)
                dve.wait_ge(S("ln_q"), n)
                dve.tensor_reduce(st[:, 2, sc], Y2[:, c * 512:c * 512 + 512].rearrange("p (a d) -> p a d", d=D),
                                  AX_X, ALU.add).then_inc(S("ln_v0"), 1)
                dve.wait_ge(S("ln_v0"), n)
                dve.tensor_scalar(st[:, 2, sc], st[:, 2, sc], 1.0 / D, EPS, ALU.mult, ALU.add).then_inc(S("ln_v"), 1)

            for i, c in enumerate(order):
                front(i, c)
                if i:
                    back(i - 1, order[i - 1])
                if between:
                    between(i)
            back(NC - 1, order[NC - 1])

        def ln_act(act, p, order=range(NC), between=None):
            for i, c in enumerate(order):
                act.wait_ge(S("ln_c"), p * NC + i + 1)
                act.activation(Y2[:, c * 512:c * 512 + 512], XC[:, c * 512:c * 512 + 512], ACT.Square).then_inc(S("ln_q"), 1)
                if between:
                    between(i)

        def ln_pool(pool, p, dst, order=range(NC)):
            for i, c in enumerate(order):
                n = p * NC + i + 1
                sc = slice(c * CH, (c + 1) * CH)
                pool.wait_ge(S("ln_v"), n)
                pool.tensor_tensor(st[:, 3, sc], st[:, 2, sc], mhalf[:, 0:CH], ALU.pow).then_inc(S("ln_r"), 1)
                pool.wait_ge(S("ln_r"), n)
                pool.tensor_tensor(dst(c), XC[:, c * 512:c * 512 + 512].rearrange("p (a d) -> p a d", d=D),
                                   st[:, 3, sc].unsqueeze(2).to_broadcast([128, CH, D]), ALU.mult).then_inc(S("ln_o"), 1)

        def ln_no(j, r):
            return 2 * NC + 2 * j + r + 1

        def ln_part(r):
            return slice(r * CH, (r + 1) * CH)

        FOLD = [c + h * (NC // 2) for c in range(NC // 2) for h in range(2)]
        XFOLD = [c for c in FOLD if c < TX // 2 // CH]
        nsq = (T - 1).bit_length() - 1

        def xcol(c, f):
            v = Xr[:, c * CH:(c + 1) * CH, :].rearrange("p m (i f) -> p (m i) f", f=NF)
            return v[:, :, f]

        def bank4(b):
            return PS[:, b, :].rearrange("p (k c) -> p k c", k=KC)

        def grant(eng, name, n):
            for _ in range(n):
                eng.nop().then_inc(S(name), 1)

        def XSp():
            return XS[:, :].rearrange("p (m a c) -> p m a c", a=2, c=128)

        def xs_pe(pe, lnp, after):
            for c in range(NC):
                pe.wait_ge(S("ln_o"), lnp * NC + c + 1)
                if c >= 2:
                    pe.wait_ge(S("xs_l"), 2 * (c - 1))
                for k in range(4):
                    last = pe.transpose(PS[:, 4 + c % 2, k * 128:k * 128 + 128],
                                        X[:, c * CH + 2 * k:c * CH + 2 * k + 2, :].rearrange("p m d -> p (m d)"), ident[:, :])
                last.then_inc(S("xs_tp"), 1)
                if c:
                    after(c - 1)
            after(NC - 1)

        def xs_act(act):
            for c in range(NC):
                act.wait_ge(S("xs_tp"), c + 1)
                for a in range(2):
                    act.activation(XSp()[0:64, 4 * c:4 * c + 4, a, :], bank4(4 + c % 2)[64 * a:64 * a + 64], ACT.Copy).then_inc(S("xs_h"), 1)

        def xs_dve(dve):
            for c in range(NC):
                for a in range(2):
                    dve.wait_ge(S("xs_h"), 2 * c + a + 1)
                    dve.tensor_tensor(XSp()[64:128, 4 * c:4 * c + 4, a, :], bank4(4 + c % 2)[64 * a:64 * a + 64],
                                      XSp()[0:64, 4 * c:4 * c + 4, a, :].bitcast(F32), ALU.subtract).then_inc(S("xs_l"), 1)

        def has(d, k, first, drain):
            return not (first and k < d) and not (drain and k >= d)

        DRAIN = 4

        def att_loop(eng, step):
            for k in range(8):
                step(0, k, first=True)
            with eng.Fori(1, NB // 8 - 1) as i:
                for k in range(8):
                    step(i, k)
            for k in range(8):
                step(NB // 8 - 1, k, last=True)
            for k in range(DRAIN):
                step(NB // 8, k, drain=True)

        block = ctx.enter_context(nc.Block())

        @block.sync
        def _(sp):
            sp.dma_start(wtok[:, 0:NF], tok_W).then_inc(S("ld_tok"), 16)
            sp.dma_start(wtok[:, NF:NF + 1], tok_b.rearrange("(p a) -> p a", a=1)).then_inc(S("ld_tok"), 16)
            xv = x.rearrange("b (m s) i f -> s b m (i f)", s=2)
            for c in XFOLD:
                for s in range(2):
                    sp.dma_start(Xr[64 * s:64 * s + 64, c * CH:(c + 1) * CH, :],
                                 xv[s, :, c * CH:(c + 1) * CH, :]).then_inc(S("ld_x%d" % c), 16)
            tv = txt.rearrange("b (m s) d -> s b m d", s=2)
            for s in range(2):
                sp.dma_start(H[64 * s:64 * s + 64, TX // 2:NM, :], tv[s]).then_inc(S("ld_txt"), 16)
            sp.wait_ge(S("bds0"), 1)
            for s in range(2):
                r = slice(64 * s, 64 * s + 64)
                sp.dma_start(bds[r, 0, r], Win).then_inc(S("ld_bd"), 16)
                sp.dma_start(bds[r, 1:L + 1, r], Dm.rearrange("l o i -> o l i")).then_inc(S("ld_bd"), 16)
                sp.dma_start(bds[r, L + 1, r], Wout).then_inc(S("ld_bd"), 16)
            sp.dma_start(binr[:, :], bin_.rearrange("(a n) -> a n", a=1).to_broadcast([128, D])).then_inc(S("ld_bd"), 16)
            sp.dma_start(boutr[:, :], bout.rearrange("(a n) -> a n", a=1).to_broadcast([128, D])).then_inc(S("ld_bd"), 16)
            for s in range(2):
                sp.dma_start(W1s[64 * s:64 * s + 64, :, :],
                             w1.rearrange("e h f -> h e f")).then_inc(S("ld_w1"), 16)
                sp.dma_start(GWs[64 * s:64 * s + 64, :], gate_w).then_inc(S("ld_w1"), 16)
                sp.dma_start(WQs[64 * s:64 * s + 64, 0, :], Wq).then_inc(S("ld_w1"), 16)
                sp.dma_start(WQs[64 * s:64 * s + 64, 1, :], Wk).then_inc(S("ld_w1"), 16)
            sp.dma_start(b1s[:, :], b1).then_inc(S("ld_moe"), 16)
            sp.dma_start(w2s[:, :, :], w2.rearrange("e f h -> f e h")).then_inc(S("ld_moe"), 16)
            for g in range(3):
                sp.dma_start(b2f[E * g:E * g + E, 0, :], b2).then_inc(S("ld_moe"), 16)
            for k in range(2):
                sp.dma_start(bqk[:, k, :], (bq, bk)[k].rearrange("(c p) -> p c", p=128), allow_slow_non_contiguous=True).then_inc(S("ld_at"), 16)
            sp.dma_start(bvs[:, :], bv.rearrange("(c p) -> p c", p=128), allow_slow_non_contiguous=True).then_inc(S("ld_at"), 16)
            sp.dma_start(bus[0:D, 0:1], bu.rearrange("(p a) -> p a", a=1)).then_inc(S("ld_at"), 16)
            sp.dma_start(Wvs[:, :], Wv).then_inc(S("ld_at"), 16)
            sp.dma_start(Wus[:, :, :], Wu.rearrange("(c p) o -> p c o", p=128)).then_inc(S("ld_at"), 16)
            for dst, lo, hi in ((UIO, (U_i, b_i), (U_o, b_o)), (UG, (U_c, b_c), (U_c, b_c)), (VIO, (V_i, None), (V_o, None)),
                                (VG, (V_c, None), None)):
                for h, (w, b) in enumerate((lo, hi) if hi else (lo,)):
                    sp.dma_start(dst[0:D, 64 * h:64 * h + 64], w).then_inc(S("ld_ls"), 16)
                    if b is not None:
                        sp.dma_start(dst[D:D + 1, 64 * h:64 * h + 64], b.rearrange("(a n) -> a n", a=1)).then_inc(S("ld_ls"), 16)
            for t, v, n in ((gbr, gate_b, E), (gam, gamma, D), (bet, beta, D)):
                sp.dma_start(t[:, :], v.rearrange("(a n) -> a n", a=1).to_broadcast([128, n])).then_inc(S("ld_moe"), 16)

            ov = out.rearrange("b (m s) d -> s b m d", s=2)
            with sp.Fori(0, T // 4) as i:
                sp.wait_ge(S("l_out"), 2 * i + 2)
                for h in range(2):
                    sp.dma_start(ov[h, :, bass.ds(2 * i, 2), :], X[64 * h:64 * h + 64, bass.ds(2 * i, 2), :]).then_inc(S("st"), 16)
            sp.wait_ge(S("st"), 16 * 2 * (T // 4))

        @block.gpsimd
        def _(pool):
            done = {}

            def seq(ins, name):
                done[name] = done.get(name, 0) + 1
                ins.then_inc(S(name), 1)
                pool.wait_ge(S(name), done[name])

            seq(pool.memset(bds[:, :, :], 0.0), "bds0")
            seq(pool.memset(ident[:, :], 0.0), "id0")
            seq(pool.affine_select(out=ident[:, :], in_=ident[:, :], compare_op=ALU.not_equal, fill=1.0,
                               base=0, pattern=[[-1, 128]], channel_multiplier=1), "ident")
            seq(pool.memset(o128[:, :], 1.0 / HD), "cst")
            seq(pool.memset(cD[:, :], 1.0 / D), "cst")
            seq(pool.memset(mhalf[:, :], -0.5), "cst")
            seq(pool.memset(WB[:, :, :], 0.0), "cst")
            seq(pool.memset(lnab[:, :, 0], 1.0 / D), "cst")
            seq(pool.memset(lnab[:, :, 1], EPS), "cst")
            seq(pool.memset(lnab[:, L - 1, 0:1], (1.0 + EPS) / D), "cst")
            seq(pool.memset(lnab[:, L - 1, 1:2], EPS * EPS), "cst")
            seq(pool.tensor_copy(identb[:, :], ident[:, :]), "identb")
            seq(pool.memset(sel[:, :, :], 0.0), "sel")
            for g in range(3):
                seq(pool.affine_select(out=sel[:, :, :], in_=sel[:, :, :], compare_op=ALU.not_equal, fill=1.0,
                                   base=-E * g, pattern=[[-1, E], [0, F]], channel_multiplier=1), "sel")
            seq(pool.memset(mask[:, :, :], 0.0), "mask")
            seq(pool.memset(valid[:, :], 1.0), "mask")
            seq(pool.affine_select(out=mask[:, :, :], in_=mask[:, :, :], compare_op=ALU.is_gt, fill=NEG, base=0,
                               pattern=[[0, NP], [-1, T]], channel_multiplier=1), "mask")
            seq(pool.affine_select(out=valid[:, :], in_=valid[:, :], compare_op=ALU.is_gt, fill=0.0, base=0,
                               pattern=[[0, 1]], channel_multiplier=1), "mask")
            for e in range(E):
                seq(pool.memset(rev[:, e:e + 1], float(E - e)), "rev")
            ln_pool(pool, 0, lambda c: halves(X)[:, c % (NC // 2) * CH:(c % (NC // 2) + 1) * CH, c // (NC // 2), :], order=FOLD)
            for i, (w, h, lo) in enumerate(((W1s, W1h, W1l), (WQs, WQKh, WQKl), (GWs, GWhl[:, 0, :], GWhl[:, 1, :]))):
                pool.wait_ge(S("whi"), i + 1)
                seq(pool.tensor_tensor(lo[:, :, :] if i < 2 else lo, w[:, :, :] if i < 2 else w[:, :],
                                   (h[:, :, :] if i < 2 else h).bitcast(F32), ALU.subtract), "wlo")
            pool.wait_ge(S("ld_at"), 16 * 6)
            pool.wait_ge(S("ld_ls"), 16 * 11)
            for t, f in ((bqk[:, 0, :], D ** -0.5), (UIO[:, :], 0.5), (VIO[:, :], 0.25), (VG[:, :], 0.5)):
                seq(pool.tensor_scalar(t, t, f, None, ALU.mult), "wsc")
            pool.wait_ge(S("ld_moe"), 16 * 8)
            seq(pool.memset(b2p[:, :, D:2 * D], 0.0), "b2z")
            for i in range(3):
                seq(pool.tensor_copy(b2p[:, i, 0:D], b2f[:, i % 2, :]), "b2c")
                if i < 2:
                    seq(pool.tensor_tensor(b2f[:, (i + 1) % 2, :], b2f[:, i % 2, :], b2p[:, i, 0:D], ALU.subtract), "b2c")
            pool.wait_ge(S("ln_c"), NC)
            pool.wait_ge(S("ld_bd"), 16 * 8)
            pool.tensor_tensor(H[:, :, :], H[:, :, :], boutr[:, :].unsqueeze(1).to_broadcast([128, NM, D]), ALU.add).then_inc(S("hb"), 1)
            with pool.Fori(0, L) as l:
                for j in range(NJ):
                    ssm_scale(pool, l, j)
            ln_pool(pool, 1, lambda c: X[:, c * CH:(c + 1) * CH, :])
            pool.wait_ge(S("ln_c"), 2 * NC)
            pool.tensor_tensor(H[:, :, :], H[:, :, :], bet[:, :].unsqueeze(1).to_broadcast([128, NM, D]), ALU.add).then_inc(S("hb"), 1)
            with pool.Fori(0, NC) as j:
                for r, dst in ((0, Ygam), (1, Ynrm)):
                    pool.wait_ge(S("ln_v"), ln_no(j, r))
                    pool.tensor_tensor(st[:, 3, ln_part(r)], st[:, 2, ln_part(r)], mhalf[:, 0:CH], ALU.pow).then_inc(S("ln_r"), 1)
                    pool.wait_ge(S("ln_r"), ln_no(j, r))
                    pool.tensor_tensor(dst, Ycen[:, r, :, :], st[:, 3, ln_part(r)].unsqueeze(2).to_broadcast([128, CH, D]),
                                       ALU.mult).then_inc(S("ln_o"), 1)
                    if r == 0:
                        pool.wait_ge(S("ln_o"), ln_no(j, r))
                        pool.tensor_tensor(dst, dst, gam[:, :].unsqueeze(1).to_broadcast([128, CH, D]), ALU.mult).then_inc(S("f_g"), 1)
            pool.wait_ge(S("ln_o"), 4 * NC)

            def step(i, k, first=False, last=False, drain=False):
                B = 8 * i + k
                if not has(1, k, first, drain):
                    return
                pool.wait_ge(S("a_rv"), B)
                Pn = Pb[:, (k - 1) % 4, :, :, :].rearrange("p a h j -> p (a h) j")
                pool.tensor_tensor(Pn, Pn, am[:, (k - 1) % 4, 3, :].unsqueeze(2).to_broadcast([T, NH, T]), ALU.mult).then_inc(S("a_pn"), 1)

            att_loop(pool, step)
            pool.wait_ge(S("a_pn"), NB)
            pool.wait_ge(S("ao_tp"), NQ)
            pool.memset(BIG[D:D + 1, 0:TOK], 1.0).then_inc(S("ones"), 1)
            pool.wait_ge(S("ones"), 1)
            ln_pool(pool, 4, lambda c: X[:, c * CH:(c + 1) * CH, :])

        @block.scalar
        def _(act):
            act.dma_start(Am[:, 0, :, :], A.rearrange("l n m -> n l m")).then_inc(S("ld_a"), 16)
            act.dma_start(Cs[:, :, :], Cm.rearrange("l h n -> h l n")).then_inc(S("ld_a"), 16)
            for s in range(2):
                act.dma_start(BB[:, :, s, :], Bm.rearrange("l n h -> n l h")).then_inc(S("ld_a"), 16)
            def power(i):
                act.wait_ge(S("p_kry"), i + 1)
                nxt = (Am if i == 0 else (Am2 if i % 2 else Am))
                act.activation(nxt[:, 1, :, :], PS[0:D, 1, 0:L * D].rearrange("p (l m) -> p l m", l=L), ACT.Copy).then_inc(S("p_at"), 1)

            power(0)
            act.wait_ge(S("p_wm"), 1)
            for i, c in enumerate(XFOLD):
                act.wait_ge(S("ld_x%d" % c), 32)
                act.activation(H[:, c * CH:(c + 1) * CH, :].rearrange("p m d -> p (m d)"), xcol(c, 0), ACT.Identity,
                               bias=wm[:, NF:NF + 1], scale=wm[:, 0:1]).then_inc(S("tok0"), 1)
                power(i + 1)
            ln_act(act, 0, FOLD, lambda i: power(i + 1 + len(XFOLD)) if i + 1 + len(XFOLD) <= nsq else None)
            for j in range(NJ):
                act.wait_ge(S("w_tp"), j + 1)
                act.activation(UF[:, j * KC:(j + 1) * KC, :], bank4(4 + j % 2), ACT.Copy).then_inc(S("w_x"), 1)
            for j in range(NJ):
                act.wait_ge(S("s_tp"), j + 1)
                act.activation(UF[:, j * KC:(j + 1) * KC, :], bank4(4 + j % 2), ACT.Copy).then_inc(S("s_uf"), 1)
            with act.Fori(0, L) as l:
                act.activation(scr[:, :], mhalf[:, 0:1], ACT.Gelu)
                for w in range(NJ + 3):
                    if w < NJ:
                        sl = slice(w * 512, w * 512 + 512)
                        if w == 0:
                            act.wait_ge(S("s_cc"), 2 * l + 2)
                        act.wait_ge(S("s_du"), l * NJ + w + 1)
                        for a in range(2 * KC):
                            last = act.activation(Y2[:, sl][:, a * D:(a + 1) * D], PS[:, w % 3, a * D:(a + 1) * D], ACT.Gelu,
                                                bias=Cc[:, w * KC + a // 2, a % 2:a % 2 + 1])
                        last.then_inc(S("s_gelu"), 1)
                    if 0 <= w - 1 < NJ:
                        j = w - 1
                        sl = slice(j * 512, j * 512 + 512)
                        act.wait_ge(S("s_c"), l * NJ + j + 1)
                        act.activation(Y2[:, sl], XC[:, sl], ACT.Square).then_inc(S("s_q"), 1)
                    if 0 <= w - 3 < NJ:
                        j = w - 3
                        act.wait_ge(S("s_tp"), l * NJ + NJ + j + 1)
                        act.activation(UF[:, j * KC:(j + 1) * KC, :], bank4(4 + j % 2), ACT.Copy).then_inc(S("s_uf"), 1)
            ln_act(act, 1)
            xs_act(act)
            act.wait_ge(S("p_wvt"), 1)
            act.activation(WvT[:, :, :], PS[:, 7, 0:NP * D].rearrange("p (c d) -> p c d", d=D), ACT.Copy).then_inc(S("WvT"), 1)
            act.wait_ge(S("gchain"), 2 + 5 + 1 + 5 + 1)
            act.activation(gs[:, 4, :], gs[:, 3, :], ACT.Exp).then_inc(S("g_exp"), 1)
            for c in range(NC):
                act.wait_ge(S("gp_tp"), c + 1)
                act.activation(GP[0:3 * E, c * 1024:(c + 1) * 1024], PSb[0:3 * E, 2 + c % 2, :], ACT.Copy).then_inc(S("gp"), 1)
            def square(j, r):
                act.wait_ge(S("ln_c"), ln_no(j, r))
                act.activation(Ysqr[:, r, :, :], Ycen[:, r, :, :], ACT.Square).then_inc(S("ln_q"), 1)

            def hi_part(j, a):
                if a == 0:
                    act.wait_ge(S("xs_tp"), NC + j + 1)
                act.activation(XSp()[0:64, bass.ds(4 * j, 4), a, :], bank4(2)[64 * a:64 * a + 64], ACT.Copy).then_inc(S("xs_h"), 1)

            def experts(i, first=False):
                for qq in range(2):
                    for e in range(E):
                        n = i * 2 * E + qq * E + e
                        act.wait_ge(S("m_z"), n + 1)
                        act.wait_ge(S("m_h"), n + 1)
                        act.activation(Rb[:, e % 4, :], PS[:, e % 2, :], ACT.Relu, bias=b1T[:, e:e + 1]).then_inc(S("m_r"), 1)
                        if e == 2 and not (first and qq == 0):
                            act.wait_ge(S("m_d"), i * 2 * E + qq * E + 4)
                            act.activation(MO[:, (1 - qq) * 512:(2 - qq) * 512], PS[:, 7 - qq, :], ACT.Copy).then_inc(S("m_mo"), 1)
                        if not first:
                            if (qq, e) in ((0, 11), (1, 4)):
                                square(i - 1, qq)
                            if (qq, e) in ((1, 11), (1, 12)):
                                hi_part(i - 1, e - 11)

            experts(0, first=True)
            with act.Fori(1, NC) as i:
                experts(i)
            act.wait_ge(S("m_d"), NQ * E + 4)
            act.activation(MO[:, 512:1024], PS[:, 7, :], ACT.Copy).then_inc(S("m_mo"), 1)
            for r in range(2):
                square(NC - 1, r)
            for a in range(2):
                hi_part(NC - 1, a)

            def q_evac(g, par, tile):
                sc, bi = (D ** -0.5, bqk[:, 0, tile:tile + 1]) if tile < NP else (1.0, bqk[:, 1, tile - NP:tile - NP + 1])
                act.wait_ge(S("a_q"), 2 * NP * g + tile + 1)
                act.activation(QK[par][:, tile, :], PS[:, tile % 2, 0:GB * T], ACT.Identity, bias=bi, scale=sc).then_inc(S("q_ev"), 1)

            def step(i, k, first=False, last=False, drain=False):
                B, g, bb = 8 * i + k, 2 * i + k // 4, k % 4
                nextq = not drain and not (last and k >= 4)
                if (bb == 0 and not first) or (drain and k == 3):
                    og = g - 2 + k // 3 if drain else g - 2
                    act.wait_ge(S("a_o"), og + 1)
                    o = AO.rearrange("p (t b) -> p b t", b=NB)[:, bass.ds(og * GB, GB), :]
                    ps = PS[:, 1, 0:GB * T].rearrange("p (b t) -> p b t", b=GB)
                    act.activation(o[:, :, 1:T], ps[:, :, 1:T], ACT.Identity, bias=bus[:, 1:2]).then_inc(S("o_ev"), 1)
                    act.activation(o[:, :, 0:1], ps[:, :, 0:1], ACT.Identity, bias=bus[:, 0:1]).then_inc(S("o_ev"), 1)
                if bb == 1 and not drain:
                    act.wait_ge(S("a_xt"), g + 1)
                    if not first:
                        act.wait_ge(S("a_z"), 4 * g - 4)
                    act.activation(XT[:, (k // 4) % 2, :, :], PS[0:T, 1, 0:GB * D].rearrange("p (b d) -> p b d", d=D), ACT.Copy).then_inc(S("xt_ev"), 1)
                if nextq:
                    if bb == 0 and not (first and k == 0):
                        act.wait_ge(S("a_s"), 4 * g)
                    q_evac(g + 1, (k // 4 + 1) % 2, 2 * bb)
                if has(2, k, first, drain):
                    act.wait_ge(S("a_t"), B - 1)
                    if has(4, k, first, False):
                        act.wait_ge(S("a_z"), B - 3)
                    act.activation(PT[:, k % 2, :, :], PS[0:T, 6:8, 0:NP * T], ACT.Copy).then_inc(S("pt_ev"), 1)
                if nextq:
                    q_evac(g + 1, (k // 4 + 1) % 2, 2 * bb + 1)
                if has(3, k, first, drain):
                    zg, zb = (k - 3) // 4, (k - 3) % 4
                    act.wait_ge(S("a_z"), B - 2)
                    if zb == 0 and not first:
                        act.wait_ge(S("a_o"), 2 * i + zg - 1)
                    act.activation(Zg[zg % 2][:, :, zb, :], PS[:, 0, 0:NP * T].rearrange("p (h c) -> p h c", h=NP), ACT.Copy).then_inc(S("z_ev"), 1)
                if not drain:
                    act.wait_ge(S("a_sub"), B + 1)
                    Pn = Pb[:, k % 4, :, :, :].rearrange("p a h j -> p (a h j)")
                    act.activation(Pn, Pn, ACT.Exp).then_inc(S("a_e"), 1)

            for tile in range(2 * NP):
                q_evac(0, 0, tile)
            att_loop(act, step)
            ln_act(act, 4)
            act.wait_ge(S("ones"), 1)
            for q in range(NQ):
                act.wait_ge(S("x_tp"), q + 1)
                act.activation(XF[0:D, q * 512:(q + 1) * 512], PS[0:D, q % 2, :], ACT.Copy).then_inc(S("x_f"), 1)

            def gates(i, u, first=False):
                t = 4 * i + u
                act.wait_ge(S("l_v"), t + 1)
                act.activation(Tb[:, u % 2, :], PS[:, 2 + u % 2, 0:128], ACT.Tanh).then_inc(S("l_t"), 1)
                act.wait_ge(S("l_c"), t + 1)
                act.activation(TC[64:128, :], Cb[:, 1, :], ACT.Tanh).then_inc(S("l_tc"), 1)

            for u in range(4):
                gates(0, u)
            with act.Fori(1, T // 4) as i:
                for u in range(4):
                    gates(i, u)

        @block.vector
        def _(dve):
            dve.wait_ge(S("ident"), 1)
            for h in range(2):
                dve.tensor_copy(ii[64 * h:64 * h + 64, :], ident[64 * h:64 * h + 64, 64 * h:64 * h + 64]).then_inc(S("ii"), 1)
            dve.wait_ge(S("p_wmps"), 1)
            dve.tensor_copy(wm[:, :], PS[:, 0, 0:NF + 1]).then_inc(S("p_wm"), 1)
            dve.wait_ge(S("p_g0"), 1)
            dve.tensor_copy(Gk[:, :, 0], PS[0:D, 4, 0:L]).then_inc(S("p_gk"), 1)

            def krylov(i):
                m = 1 << i
                nm = min(m, T - m)
                dve.wait_ge(S("p_kry"), i + 2)
                dve.tensor_copy(Gk[:, :, m:m + nm], PS[0:D, 0, 0:L * nm].rearrange("p (l m) -> p l m", l=L)).then_inc(S("p_gk"), 1)
                if i < nsq:
                    nxt = Am2 if (i + 1) % 2 else Am
                    dve.tensor_copy(nxt[:, 0, :, :], PS[0:D, 2, 0:L * D].rearrange("p (l m) -> p l m", l=L)).then_inc(S("p_am"), 1)

            for i, c in enumerate(XFOLD):
                dve.wait_ge(S("tok0"), i + 1)
                hc = H[:, c * CH:(c + 1) * CH, :].rearrange("p m d -> p (m d)")
                for f in range(1, NF):
                    if f > 1:
                        dve.wait_ge(S("tokf"), (NF - 1) * i + f - 1)
                    dve.scalar_tensor_tensor(hc, xcol(c, f), wm[:, f:f + 1], hc, ALU.mult, ALU.add).then_inc(S("tokf"), 1)
                krylov(i)

            def ready(c):
                if c in XFOLD:
                    dve.wait_ge(S("tokf"), (NF - 1) * (XFOLD.index(c) + 1))
                else:
                    dve.wait_ge(S("ld_txt"), 32)
            ln_dve(dve, 0, H, ready, FOLD, lambda i: krylov(i + len(XFOLD)) if i + len(XFOLD) <= nsq else None)
            dve.wait_ge(S("p_w"), 1)
            dve.wait_ge(S("cst"), 8)
            pw = PS[:, 3, 0:L * T].rearrange("p (l t) -> p l t", l=L)
            dve.tensor_copy(WB[0:64, :, T // 2:T // 2 + T - 1], pw[0:64, :, 0:T - 1]).then_inc(S("p_wb"), 1)
            dve.tensor_copy(WB[64:128, :, T:T + T // 2 - 1], pw[64:128, :, 0:T // 2 - 1]).then_inc(S("p_wb"), 1)
            for h in range(2):
                dve.wait_ge(S("p_bd"), h + 1)
                dve.tensor_copy(bdt[:, 3 * h:3 * h + 3, :], PS[:, 6 + h, 0:384].rearrange("p (a c) -> p a c", a=3)).then_inc(S("p_bdt"), 1)
            dve.wait_ge(S("ld_w1"), 16 * 8)
            dve.tensor_copy(W1h[:, :, :], W1s[:, :, :]).then_inc(S("whi"), 1)
            dve.tensor_copy(WQKh[:, :, :], WQs[:, :, :]).then_inc(S("whi"), 1)
            dve.tensor_copy(GWhl[:, 0, :], GWs[:, :]).then_inc(S("whi"), 1)
            dve.wait_ge(S("ld_bd"), 16 * 8)
            for j in range(NJ):
                dve.wait_ge(S("w_mm"), j + 1)
                dve.tensor_tensor(ssm_cols(UT, j).rearrange("p (a d) -> p a d", d=D),
                                  PS[:, j % 3, :].rearrange("p (a d) -> p a d", d=D),
                                  binr[:, :].unsqueeze(1).to_broadcast([128, KC * 2, D]), ALU.add).then_inc(S("w_u"), 1)
            dve.wait_ge(S("p_b1"), 1)
            dve.tensor_copy(b1T[:, :], PS[:, 7, 0:E]).then_inc(S("b1T"), 1)
            dve.wait_ge(S("wlo"), 3)
            with dve.Fori(0, L) as l:
                dve.wait_ge(S("s_cps"), l + 1)
                cps = PS[0:64, 6, 0:T].rearrange("p (h k s) -> p k h s", h=2, s=2)
                for s in range(2):
                    dve.tensor_copy(Cc[64 * s:64 * s + 64, :, :], cps[:, :, :, s]).then_inc(S("s_cc"), 1)
                dve.wait_ge(S("s_cc"), 2 * l + 2)

                def back(j):
                    n = l * NJ + j + 1
                    sj = slice(j * KC * 2, (j + 1) * KC * 2)
                    dve.wait_ge(S("s_q"), n)
                    dve.tensor_reduce(st[:, 2, sj], Y2[:, j * 512:j * 512 + 512].rearrange("p (a d) -> p a d", d=D),
                                      AX_X, ALU.add).then_inc(S("s_v0"), 1)
                    dve.wait_ge(S("s_v0"), n)
                    dve.tensor_scalar(st[:, 2, sj], st[:, 2, sj], lnab[:, bass.ds(l, 1), 0], lnab[:, bass.ds(l, 1), 1],
                                      ALU.mult, ALU.add).then_inc(S("s_v"), 1)

                for j in range(NJ):
                    n = l * NJ + j + 1
                    sj = slice(j * KC * 2, (j + 1) * KC * 2)
                    y = Y1[:, j * 512:j * 512 + 512]
                    y3 = y.rearrange("p (a d) -> p a d", d=D)
                    dve.wait_ge(S("s_gelu"), n)
                    dve.tensor_tensor(y, Y2[:, j * 512:j * 512 + 512], ssm_cols(UT, j), ALU.add).then_inc(S("s_y"), 1)
                    if j:
                        back(j - 1)
                    dve.wait_ge(S("s_y"), n)
                    dve.tensor_reduce(st[:, 0, sj], y3, AX_X, ALU.add).then_inc(S("s_s"), 1)
                    dve.wait_ge(S("s_s"), n)
                    dve.scalar_tensor_tensor(XC[:, j * 512:j * 512 + 512].rearrange("p (a d) -> p a d", d=D),
                                             st[:, 0, sj].unsqueeze(2).to_broadcast([128, KC * 2, D]), -1.0 / D, y3,
                                             ALU.mult, ALU.add).then_inc(S("s_c"), 1)
                back(NJ - 1)
            dve.wait_ge(S("hb"), 1)
            for j in range(NJ):
                dve.wait_ge(S("o_mm"), j + 1)
                hv = view_km(H)[:, j * KC:(j + 1) * KC, :, :]
                dve.tensor_tensor(hv, PS[:, j % 3, :].rearrange("p (k h d) -> p k h d", h=2, d=D), hv, ALU.add).then_inc(S("o_h"), 1)
            ln_dve(dve, 1, H, lambda c: dve.wait_ge(S("o_h"), 2 * (c % (NC // 2)) + 2))
            xs_dve(dve)
            dve.wait_ge(S("p_np"), 1)
            dve.memset(bus[D:128, :], 0.0).then_inc(S("bus0"), 1)
            dve.tensor_copy(NPt[:, :, :], PS[:, 6, 0:NP * D].rearrange("p (c d) -> p c d", d=D)).then_inc(S("NPt"), 1)
            dve.tensor_tensor(bus[0:D, 1:2], PS[0:D, 6, NP * D:NP * D + 1], bus[0:D, 0:1], ALU.add).then_inc(S("NPt"), 1)
            nch = [0]

            def link(ins):
                nch[0] += 1
                ins.then_inc(S("gchain"), 1)
                dve.wait_ge(S("gchain"), nch[0])

            def g3(i):
                return Y1[:, NM * E * i:NM * E * (i + 1)].rearrange("p (m e) -> p m e", e=E)

            def bm(i):
                return gs[:, i, :].unsqueeze(2).to_broadcast([128, NM, E])

            revb = rev[:, :].unsqueeze(1).to_broadcast([128, NM, E])
            LG, SC, K1, K2 = g3(0), g3(1), g3(2), g3(3)
            dve.wait_ge(S("ld_moe"), 16 * 8)
            dve.wait_ge(S("rev"), E)
            dve.wait_ge(S("gt_mm"), NC)
            lps = PS[:, 0:NM // 16, :].rearrange("p b (m a e) -> p (b m) a e", a=2, e=E)
            link(dve.tensor_tensor(LG, lps[:, :, 1, :], gbr[:, :].unsqueeze(1).to_broadcast([128, NM, E]), ALU.add))
            link(dve.tensor_tensor(LG, lps[:, :, 0, :], LG, ALU.add))
            for r, K in ((0, K1), (1, K2)):
                link(dve.tensor_reduce(gs[:, r, :], LG, AX_X, ALU.max))
                link(dve.tensor_tensor(SC, LG, bm(r), ALU.is_equal))
                link(dve.tensor_tensor(SC, SC, revb, ALU.mult))
                link(dve.tensor_reduce(gs[:, 2, :], SC, AX_X, ALU.max))
                link(dve.tensor_tensor(K, revb, bm(2), ALU.is_equal))
                if r == 0:
                    link(dve.scalar_tensor_tensor(LG, K, -3e38, LG, ALU.mult, ALU.add))
            link(dve.tensor_tensor(gs[:, 3, :], gs[:, 1, :], gs[:, 0, :], ALU.subtract))
            dve.wait_ge(S("g_exp"), 1)
            link(dve.tensor_scalar(gs[:, 5, :], gs[:, 4, :], 1.0, None, ALU.add))
            link(dve.reciprocal(gs[:, 6, :], gs[:, 5, :]))
            link(dve.tensor_tensor(gs[:, 7, :], gs[:, 4, :], gs[:, 6, :], ALU.mult))
            link(dve.tensor_tensor(K1, K1, bm(6), ALU.mult))
            link(dve.tensor_tensor(K2, K2, bm(7), ALU.mult))
            link(dve.tensor_tensor(LG, K1, K2, ALU.add))
            gp = GPT.rearrange("p (m g e) -> p m g e", g=3, e=E)
            link(dve.tensor_copy(gp[:, :, 0, :], LG))
            link(dve.tensor_tensor(SC, LG, gp[:, :, 0, :], ALU.subtract))
            link(dve.tensor_copy(gp[:, :, 1, :], SC))
            link(dve.tensor_tensor(K1, SC, gp[:, :, 1, :], ALU.subtract))
            dve.tensor_copy(gp[:, :, 2, :], K1).then_inc(S("g_gp"), 1)
            def settle(j, k):
                def step(*ks):
                    return k in ks
                if step(0, 1, 2, 3):
                    q, odd = k // 2, k % 2
                    ps = PS[:, 2 + q, :].rearrange("p (m a d) -> p m a d", a=2, d=D)[:, :, odd, :]
                    y = Ysum[:, q * QM:(q + 1) * QM, :]
                    if odd:
                        dve.wait_ge(S("mo_y"), 4 * j + k)
                        dve.tensor_tensor(y, ps, y, ALU.add).then_inc(S("mo_y"), 1)
                    else:
                        dve.wait_ge(S("mo_tp"), 2 * j + q + 1)
                        dve.tensor_tensor(y, ps, X[:, bass.ds(j * CH + q * QM, QM), :], ALU.add).then_inc(S("mo_y"), 1)
                if step(8):
                    dve.wait_ge(S("f_g"), j + 1)
                    h = H[:, bass.ds(j * CH, CH), :]
                    dve.tensor_tensor(h, h, Ygam, ALU.add).then_inc(S("f_h"), 1)
                    dve.wait_ge(S("f_h"), j + 1)
                r = 0 if k < 8 else 1
                src = H[:, bass.ds(j * CH, CH), :] if r else Ysum
                if step(4, 9):
                    if not r:
                        dve.wait_ge(S("mo_y"), 4 * j + 4)
                    dve.tensor_reduce(st[:, 0, ln_part(r)], src, AX_X, ALU.add).then_inc(S("ln_s"), 1)
                if step(5, 10):
                    dve.wait_ge(S("ln_s"), ln_no(j, r))
                    dve.scalar_tensor_tensor(Ycen[:, r, :, :], st[:, 0, ln_part(r)].unsqueeze(2).to_broadcast([128, CH, D]), -1.0 / D,
                                             src, ALU.mult, ALU.add).then_inc(S("ln_c"), 1)
                if step(6, 11):
                    dve.wait_ge(S("ln_q"), ln_no(j, r))
                    dve.tensor_reduce(st[:, 2, ln_part(r)], Ysqr[:, r, :, :], AX_X, ALU.add).then_inc(S("ln_v0"), 1)
                if step(7, 12):
                    dve.wait_ge(S("ln_v0"), ln_no(j, r))
                    dve.tensor_scalar(st[:, 2, ln_part(r)], st[:, 2, ln_part(r)], 1.0 / D, EPS, ALU.mult, ALU.add).then_inc(S("ln_v"), 1)
                if step(13, 14):
                    a = k - 13
                    dve.wait_ge(S("xs_h"), 2 * (NC + j) + a + 1)
                    dve.tensor_tensor(XSp()[64:128, bass.ds(4 * j, 4), a, :], bank4(2)[64 * a:64 * a + 64],
                                      XSp()[0:64, bass.ds(4 * j, 4), a, :].bitcast(F32), ALU.subtract).then_inc(S("xs_l"), 1)

            SETTLE = [(0, e) for e in (5, 6, 7, 8, 9, 10, 12, 13)] + [(1, e) for e in (1, 2, 3, 5, 6, 12, 13)]

            def experts(i, first=False):
                for qq in range(2):
                    for e in range(E):
                        n = i * 2 * E + qq * E + e
                        dve.wait_ge(S("m_r"), n + 5)
                        dve.wait_ge(S("m_g"), n + 1)
                        dve.wait_ge(S("m_d"), n + 1)
                        dve.tensor_tensor(Hb[:, e % 4, :], PS[:, 4 + e % 2, :], Rb[:, e % 4, :], ALU.mult).then_inc(S("m_h"), 1)
                        if not first and (qq, e) in SETTLE:
                            settle(i - 1, SETTLE.index((qq, e)))

            experts(0, first=True)
            dve.wait_ge(S("hb"), 2)
            with dve.Fori(1, NC) as i:
                experts(i)
            for k in range(len(SETTLE)):
                settle(NC - 1, k)

            xsb = XS[:, :].rearrange("p (t b) -> p b t", b=NB)

            def step(i, k, first=False, last=False, drain=False):
                B, g, bb = 8 * i + k, 2 * i + k // 4, k % 4
                gp = (k // 4) % 2
                if bb == 2 and not drain and not last:
                    dve.wait_ge(S("a_q"), 2 * NP * g + 2 * NP)
                    dve.wait_ge(S("a_xt"), g + 1)
                    dve.tensor_copy(XSg[:, gp, :, :], xsb[:, bass.ds(GB * g + 2 * GB, GB), :]).then_inc(S("a_st"), 1)
                if has(1, k, first, drain):
                    s1 = am[:, (k - 1) % 4, :, :]
                    dve.wait_ge(S("a_e"), B)
                    dve.tensor_reduce(s1[:, 1, :], Pb[:, (k - 1) % 4, :, :, :].rearrange("p a h j -> p (a h) j"),
                                      AX_X, ALU.add).then_inc(S("a_sm"), 1)
                    dve.wait_ge(S("a_sm"), B)
                    dve.reciprocal(s1[:, 2, :], s1[:, 1, :]).then_inc(S("a_rc"), 1)
                    dve.wait_ge(S("a_rc"), B)
                    dve.tensor_scalar(s1[:, 3, :], s1[:, 2, :], valid[:, 0:1], None, ALU.mult).then_inc(S("a_rv"), 1)
                if drain:
                    return
                ps = PS[0:T, 2 + 2 * (k % 2):4 + 2 * (k % 2), 0:NP * T].rearrange("p a (h j) -> p a h j", h=NP)
                dve.wait_ge(S("a_s"), B + 1)
                dve.tensor_reduce(am[:, k % 4, 0, :], ps, AX_X, ALU.max).then_inc(S("a_mx"), 1)
                dve.wait_ge(S("a_mx"), B + 1)
                if not (first and k < 4):
                    dve.wait_ge(S("a_t"), B - 3)
                mx = am[:, k % 4, 0, :].rearrange("p (a h) -> p a h", a=2)
                for a in range(2):
                    dve.tensor_tensor(Pb[:, k % 4, a, :, :], ps[:, a, :, :], mx[:, a, :].unsqueeze(2).to_broadcast([T, NP, T]),
                                      ALU.subtract).then_inc(S("a_sub%d" % a if a == 0 else "a_sub"), 1)

            dve.wait_ge(S("mask"), 4)
            dve.wait_ge(S("xs_l"), 4 * NC)
            for g in range(2):
                dve.tensor_copy(XSg[:, g, :, :], xsb[:, g * GB:(g + 1) * GB, :]).then_inc(S("a_st"), 1)
            att_loop(dve, step)

            def att_residual(c):
                for a in range(2):
                    for q in (2 * c, 2 * c + 1):
                        ps = PS[:, 4 + q % 4, :].rearrange("p (m a d) -> p m a d", a=2, d=D)
                        hc = H[:, q * QM:(q + 1) * QM, :]
                        if a == 0:
                            dve.wait_ge(S("ao_tp"), q + 1)
                        else:
                            dve.wait_ge(S("a_h"), 4 * c + q % 2 + 1)
                        dve.tensor_tensor(hc, ps[:, :, a, :], hc, ALU.add).then_inc(S("a_h"), 1)
                dve.wait_ge(S("a_h"), 4 * c + 4)

            ln_dve(dve, 4, H, att_residual)

            def cell(i, u, first=False):
                t = 4 * i + u
                tb = Tb[:, u % 2, :]
                if not first and u % 2 == 0:
                    dve.wait_ge(S("l_tp"), 2 * i + u // 2 - 1)
                dve.wait_ge(S("l_t"), t + 1)
                dve.scalar_tensor_tensor(Cb[:, 0, :], tb[0:64, 0:64], 1.0, tb[0:64, 64:128], ALU.add, ALU.mult).then_inc(S("l_a"), 1)
                dve.wait_ge(S("l_a"), t + 1)
                if first and u == 0:
                    dve.tensor_scalar(Cb[:, 1, :], Cb[:, 0, :], 0.5, None, ALU.mult).then_inc(S("l_c"), 1)
                else:
                    dve.wait_ge(S("l_hc"), t)
                    dve.scalar_tensor_tensor(Cb[:, 1, :], Cb[:, 0, :], 0.5, HC[:, :], ALU.mult, ALU.add).then_inc(S("l_c"), 1)
                dve.wait_ge(S("l_tc"), t + 1)
                dve.scalar_tensor_tensor(HB[:, u, :], tb[64:128, 0:64], 1.0, TC[64:128, :], ALU.add, ALU.mult).then_inc(S("l_h"), 1)
                dve.wait_ge(S("l_h"), t + 1)
                dve.scalar_tensor_tensor(HC[:, :], HB[:, u, :], 0.5, Cb[:, 1, :], ALU.mult, ALU.mult).then_inc(S("l_hc"), 1)
                if u % 2 == 0 and not (first and u == 0):
                    output(2 * i + u // 2 - 1, (u // 2 - 1) % 2)

            def output(m, par):
                dve.wait_ge(S("l_tp"), m + 1)
                dve.scalar_tensor_tensor(X[:, bass.ds(m, 1), :].rearrange("p a d -> p (a d)"), PS[:, 4 + par, 0:D], 0.5,
                                         H[:, bass.ds(m, 1), :].rearrange("p a d -> p (a d)"), ALU.mult, ALU.add).then_inc(S("l_out"), 1)

            for u in range(4):
                cell(0, u, first=True)
            with dve.Fori(1, T // 4) as i:
                for u in range(4):
                    cell(i, u)
            output(NM - 1, 1)

        @block.tensor
        def _(pe):
            pe.wait_ge(S("cst"), 1)
            pe.wait_ge(S("ld_tok"), 32)
            pe.matmul(PS[:, 0, 0:NF + 1], o128[:, :], wtok[:, :], start=True, stop=True).then_inc(S("p_wmps"), 1)
            pe.wait_ge(S("ident"), 1)
            pe.wait_ge(S("ld_a"), 64)
            for l in range(L):
                last = pe.transpose(PS[0:D, 1, l * D:l * D + D], Am[:, 0, l, :], ident[0:D, 0:D])
            last.then_inc(S("p_kry"), 1)
            pe.wait_ge(S("cst"), 2)
            for l in range(L):
                last = pe.matmul(PS[0:D, 4, l:l + 1], Cs[:, l, :], cD[0:D, :], start=True, stop=True)
            last.then_inc(S("p_g0"), 1)
            for i in range(nsq + 1):
                m = 1 << i
                nm = min(m, T - m)
                cur = Am if i % 2 == 0 else Am2
                pe.wait_ge(S("p_gk"), i + 1)
                if i:
                    pe.wait_ge(S("p_am"), i)
                pe.wait_ge(S("p_at"), i + 1)
                for l in range(L):
                    last = pe.matmul(PS[0:D, 0, l * nm:l * nm + nm], cur[:, 0, l, :], Gk[:, l, 0:nm], start=True, stop=True)
                if i < nsq:
                    for l in range(L):
                        pe.matmul(PS[0:D, 2, l * D:l * D + D], cur[:, 1, l, :], cur[:, 0, l, :], start=True, stop=True)
                    for l in range(L):
                        last = pe.matmul(PS[0:D, 1, l * D:l * D + D], cur[:, 0, l, :], cur[:, 1, l, :], start=True, stop=True)
                last.then_inc(S("p_kry"), 1)
            pe.wait_ge(S("p_gk"), nsq + 2)
            for l in range(L):
                last = pe.matmul(PS[:, 3, l * T:l * T + T], BB[:, l, :, :].rearrange("p a b -> p (a b)"), Gk[:, l, :], start=True, stop=True)
            last.then_inc(S("p_w"), 1)
            pe.wait_ge(S("ld_bd"), 16 * 8)
            for h in range(2):
                for a in range(3):
                    last = pe.transpose(PS[:, 6 + h, a * 128:a * 128 + 128], bds[:, 3 * h + a, :], ident[:, :])
                last.then_inc(S("p_bd"), 1)
            pe.wait_ge(S("p_bdt"), 2)
            pe.wait_ge(S("ld_moe"), 16 * 8)
            pe.transpose(PS[:, 7, 0:E], b1s[:, :], ident[0:E, 0:E]).then_inc(S("p_b1"), 1)
            xk = halves(X)
            for j in range(NJ):
                pe.wait_ge(S("ln_o"), 2 * (j * KC // CH) + 2)
                if j >= 2:
                    pe.wait_ge(S("w_x"), j - 1)
                for k in range(KC):
                    last = pe.transpose(PS[:, 4 + j % 2, k * 128:k * 128 + 128], xk[:, j * KC + k, :, :].rearrange("p h d -> p (h d)"), ident[:, :])
                last.then_inc(S("w_tp"), 1)
                if j == 0:
                    pe.wait_ge(S("p_gk"), nsq + 2)
            for j in range(NJ):
                pe.wait_ge(S("w_x"), j + 1)
                if j >= 3:
                    pe.wait_ge(S("w_u"), j - 2)
                for k in range(KC):
                    last = pe.matmul(PS[:, j % 3, k * 128:k * 128 + 128], UF[:, j * KC + k, :], bdt[:, 0, :], start=True, stop=True)
                last.then_inc(S("w_mm"), 1)
            def toeplitz(l, j):
                pe.wait_ge(S("s_uf"), l * NJ + j + 1)
                for tt in range(2 * KC * j, 2 * KC * (j + 1)):
                    o = T // 2 - 1 - tt
                    mm = pe.matmul(PS[0:64, 6, 0:T], UF[:, tt // 2, 64 * (tt % 2):64 * (tt % 2) + 64],
                                   WB[:, bass.ds(l, 1), o:o + T].rearrange("p a t -> p (a t)"), start=(tt == 0), stop=(tt == T // 2 - 1))
                if j == NJ - 1:
                    mm.then_inc(S("s_cps"), 1)

            def du(l, j):
                if j >= 3:
                    pe.wait_ge(S("s_gelu"), l * NJ + j - 2)
                for k in range(KC):
                    mm = pe.matmul(PS[:, j % 3, k * 128:k * 128 + 128], UF[:, j * KC + k, :],
                                   bdt[:, bass.ds(l + 1, 1), :].rearrange("p a t -> p (a t)"), start=True, stop=True)
                mm.then_inc(S("s_du"), 1)

            def feature_major(j):
                for k in range(KC):
                    mm = pe.transpose(PS[:, 4 + j % 2, k * 128:k * 128 + 128], UT[:, j * KC + k, :, :].rearrange("p h d -> p (h d)"), ident[:, :])
                mm.then_inc(S("s_tp"), 1)

            for j in range(NJ):
                pe.wait_ge(S("w_u"), j + 1)
                if j < 2:
                    pe.wait_ge(S("w_x"), NJ - 1 + j)
                if j >= 2:
                    pe.wait_ge(S("s_uf"), j - 1)
                feature_major(j)
                if j == 0:
                    pe.wait_ge(S("p_wb"), 2)
                else:
                    toeplitz(0, j - 1)
            pe.wait_ge(S("w_u"), NJ)
            for j in range(3):
                du(0, j)
            toeplitz(0, NJ - 1)

            def layer(l, last=False):
                for j in range(3, NJ):
                    du(l, j)
                for j in range(NJ):
                    pe.wait_ge(S("s_un"), l * NJ + j + 1)
                    pe.wait_ge(S("s_uf"), l * NJ + NJ + j - 1)
                    feature_major(j)
                    if not last and j:
                        toeplitz(l + 1, j - 1)
                        if j >= NJ - 3:
                            pe.wait_ge(S("s_gelu"), l * NJ + j + 1)
                            du(l + 1, j - (NJ - 3))
                if not last:
                    toeplitz(l + 1, NJ - 1)

            with pe.Fori(0, L - 1) as l:
                layer(l)
            layer(L - 1, last=True)
            for j in range(NJ):
                pe.wait_ge(S("s_uf"), L * NJ + j + 1)
                if j < 3:
                    pe.wait_ge(S("s_gelu"), L * NJ - 2 + j)
                else:
                    pe.wait_ge(S("o_h"), j - 2)
                for k in range(KC):
                    last = pe.matmul(PS[:, j % 3, k * 128:k * 128 + 128], UF[:, j * KC + k, :], bdt[:, L + 1, :], start=True, stop=True)
                last.then_inc(S("o_mm"), 1)
            def logits(c):
                if c == 0:
                    pe.wait_ge(S("wlo"), 3)
                    pe.wait_ge(S("o_h"), NJ)
                pe.wait_ge(S("xs_l"), 2 * c + 2)
                for m in range(c * CH, (c + 1) * CH):
                    last = pe.matmul(PS[:, m // 16, (m % 16) * 2 * E:(m % 16 + 1) * 2 * E], XS[:, m * 128:(m + 1) * 128],
                                     GWhl[:, :, :].rearrange("p a e -> p (a e)"), start=True, stop=True)
                last.then_inc(S("gt_mm"), 1)

            xs_pe(pe, 1, logits)
            pe.wait_ge(S("ld_at"), 16 * 6)
            for c in range(NP):
                last = pe.transpose(PS[:, 7, c * D:(c + 1) * D], Wvs[:, c * 128:(c + 1) * 128], ident[0:D, 0:D])
            last.then_inc(S("p_wvt"), 1)
            pe.wait_ge(S("WvT"), 1)
            for c in range(NP):
                for a in range(2):
                    r = slice(64 * a, 64 * a + 64)
                    pe.matmul(PS[r, 6, c * D:(c + 1) * D], WvT[r, c, :], Wus[r, c, :], start=True, stop=True)
            for c in range(NP):
                last = pe.matmul(PS[0:D, 6, NP * D:NP * D + 1], Wus[:, c, :], bvs[:, c:c + 1], start=(c == 0), stop=(c == NP - 1))
            last.then_inc(S("p_np"), 1)
            pe.wait_ge(S("g_gp"), 1)
            pe.wait_ge(S("identb"), 1)
            for c in range(NC):
                if c >= 2:
                    pe.wait_ge(S("gp"), c - 1)
                for k in range(8):
                    last = pe.transpose(PSb[0:3 * E, 2 + c % 2, k * 128:(k + 1) * 128],
                                        GPT[:, (c * 8 + k) * 3 * E:(c * 8 + k + 1) * 3 * E], identb[:, :])
                last.then_inc(S("gp_tp"), 1)
            pe.wait_ge(S("b2c"), 5)
            pe.wait_ge(S("b2z"), 1)
            pe.wait_ge(S("sel"), 4)
            pe.wait_ge(S("ld_moe"), 16 * 8)
            grant(pe, "m_r", 4)
            grant(pe, "m_h", 4)
            grant(pe, "m_d", 4)
            grant(pe, "m_mo", 2)
            def sums_out(j):
                pe.wait_ge(S("m_mo"), 2 * j + 4)
                pe.wait_ge(S("xs_l"), 2 * (NC + j))
                for q in range(2):
                    for k in range(QM):
                        last = pe.transpose(PS[:, 2 + q, k * 128:(k + 1) * 128], MO[:, q * 512 + k * 128:q * 512 + (k + 1) * 128], ident[:, :])
                    last.then_inc(S("mo_tp"), 1)

            def norm_out(j):
                pe.wait_ge(S("ln_o"), ln_no(j, 1))
                for k in range(4):
                    last = pe.transpose(PS[:, 2, k * 128:k * 128 + 128], Ynrm[:, 2 * k:2 * k + 2, :].rearrange("p m d -> p (m d)"), ident[:, :])
                last.then_inc(S("xs_tp"), 1)

            def experts(i, first=False):
                for qq in range(2):
                    col = i * 1024 + qq * 512

                    def down(q, e):
                        pe.wait_ge(S("m_h"), i * 2 * E + q * E + e + 5)
                        pe.matmul(PS[64 * (e % 2):64 * (e % 2) + 64, 6 + q % 2, :], w2s[:, e, :], Hb[:, e % 4, :],
                                  start=False, stop=(e >= E - 2)).then_inc(S("m_d"), 1)

                    for e in range(E):
                        n = i * 2 * E + qq * E + e
                        if e == 0:
                            pe.wait_ge(S("gp"), i + 1)
                            pe.wait_ge(S("m_mo"), i * 2 + qq + 1)
                        pe.wait_ge(S("m_h"), n + 3)
                        pe.wait_ge(S("m_r"), n + 1)
                        pe.matmul(PS[:, e % 2, :], W1h[:, e, :], XS[:, bass.ds(col, 512)], start=True, stop=False)
                        pe.matmul(PS[:, e % 2, :], W1l[:, e, :], XS[:, bass.ds(col, 512)], start=False, stop=True).then_inc(S("m_z"), 1)
                        if e == 0:
                            for g in range(3):
                                pe.matmul(PS[:, 6 + qq, :], b2p[:, g, :], GP[0:3 * E, bass.ds(col, 512)], start=(g == 0), stop=False)
                        pe.matmul(PS[:, 4 + e % 2, :], sel[:, e, :], GP[0:3 * E, bass.ds(col, 512)], start=True, stop=True).then_inc(S("m_g"), 1)
                        if e % 2 and not (first and qq == 0 and e == 1):
                            down(qq if e > 1 else qq - 1, (e - 3) % E)
                            down(qq if e > 1 else qq - 1, (e - 2) % E)
                        if not first and (qq, e) == (0, 4):
                            sums_out(i - 1)
                        if not first and (qq, e) == (1, 10):
                            norm_out(i - 1)

            experts(0, first=True)
            with pe.Fori(1, NC) as i:
                experts(i)
            for e in (E - 2, E - 1):
                pe.wait_ge(S("m_h"), NQ * E - E + e + 5)
                pe.matmul(PS[64 * (e % 2):64 * (e % 2) + 64, 6 + (NQ - 1) % 2, :], w2s[:, e, :], Hb[:, e % 4, :],
                          start=False, stop=True).then_inc(S("m_d"), 1)
            sums_out(NC - 1)
            norm_out(NC - 1)

            def q_tile(par, tile):
                W = (WQKh, WQKl)
                for a in range(2):
                    last = pe.matmul(PS[:, tile % 2, 0:GB * T], W[a][:, tile // NP, (tile % NP) * 128:(tile % NP + 1) * 128],
                                     XSg[:, par, :, :].rearrange("p b t -> p (b t)"), start=(a == 0), stop=(a == 1))
                last.then_inc(S("a_q"), 1)

            def step(i, k, first=False, last=False, drain=False):
                B, g, bb = 8 * i + k, 2 * i + k // 4, k % 4
                gp = (k // 4) % 2
                nq = 2 * NP
                if not drain:
                    if bb == 0:
                        pe.wait_ge(S("q_ev"), nq * g + nq)
                    if has(2, k, first, False):
                        pe.wait_ge(S("a_sub"), B - 1)
                    for a in range(2):
                        pe.matmul(PS[0:T, 2 + 2 * (k % 2) + a, 0:NP * T], identb[0:T, 0:T],
                                  mask[:, :, :].rearrange("p h j -> p (h j)"), start=True, stop=False)
                    for h in range(NP):
                        for a in range(2):
                            r = slice(64 * a, 64 * a + 64)
                            mm = pe.matmul(PS[0:T, 2 + 2 * (k % 2) + a, h * T:(h + 1) * T], QK[gp][r, h, bb * T:(bb + 1) * T],
                                           QK[gp][r, NP + h, bb * T:(bb + 1) * T], start=False, stop=(h == NP - 1))
                    mm.then_inc(S("a_s"), 1)
                nextq = not drain and not (last and k >= 4)
                if (bb == 0 and not first) or (drain and k == 3):
                    og = g - 2 + k // 3 if drain else g - 2
                    pe.wait_ge(S("z_ev"), 4 * og + 4)
                    if drain:
                        if k == 0:
                            pe.wait_ge(S("xt_ev"), g)
                        else:
                            pe.wait_ge(S("o_ev"), 2 * g - 2)
                    for h in range(NP):
                        r = slice(64 * (h % 2), 64 * (h % 2) + 64)
                        mm = pe.matmul(PS[r, 1, 0:GB * T], NPt[:, h, :], Zg[(k // 4 + k // 3 * drain) % 2][:, h, :, :].rearrange("p b t -> p (b t)"),
                                       start=(h < 2), stop=(h >= NP - 2))
                    mm.then_inc(S("a_o"), 1)
                if bb == 1 and not drain:
                    if nextq:
                        pe.wait_ge(S("q_ev"), nq * (g + 1) + 2)
                    else:
                        pe.wait_ge(S("o_ev"), 2 * g - 2)
                    for b in range(GB):
                        mm = pe.matmul(PS[0:T, 1, b * D:(b + 1) * D], XSg[:, gp, b, :], ii[:, :], start=True, stop=True)
                    mm.then_inc(S("a_xt"), 1)
                if nextq:
                    if bb == 0:
                        pe.wait_ge(S("a_st"), g + 2)
                    if has(4, k, first, False):
                        pe.wait_ge(S("z_ev"), B - 3)
                    elif k:
                        pe.wait_ge(S("q_ev"), nq * (g + 1) + 2 * bb - 1)
                    q_tile(1 - gp, 2 * bb)
                if has(2, k, first, drain):
                    pe.wait_ge(S("a_pn"), B - 1)
                    if has(3, k, first, False):
                        pe.wait_ge(S("pt_ev"), B - 2)
                    for h in range(NP):
                        for a in range(2):
                            mm = pe.transpose(PS[0:T, 6 + a, h * T:(h + 1) * T], Pb[:, (k - 2) % 4, a, h, :], ident[0:T, 0:T])
                    mm.then_inc(S("a_t"), 1)
                if nextq:
                    if bb == 0 and not first:
                        pe.wait_ge(S("o_ev"), 2 * g - 2)
                    if bb == 1:
                        pe.wait_ge(S("xt_ev"), g + 1)
                    if bb >= 2:
                        pe.wait_ge(S("q_ev"), nq * (g + 1) + 2 * bb)
                    q_tile(1 - gp, 2 * bb + 1)
                if has(3, k, first, drain):
                    zg = (k - 3) // 4
                    pe.wait_ge(S("pt_ev"), B - 2)
                    if nextq:
                        pe.wait_ge(S("q_ev"), nq * (g + 1) + 2 * bb + 1)
                    elif has(4, k, first, False):
                        pe.wait_ge(S("z_ev"), B - 3)
                    for a in range(2):
                        mm = pe.matmul(PS[64 * a:64 * a + 64, 0, 0:NP * T], XT[:, zg % 2, (k - 3) % 4, :],
                                       PT[:, (k - 3) % 2, a, :], start=True, stop=True)
                    mm.then_inc(S("a_z"), 1)

            pe.wait_ge(S("a_st"), 1)
            pe.wait_ge(S("wsc"), 4)
            pe.wait_ge(S("mask"), 4)
            pe.wait_ge(S("ii"), 2)
            pe.wait_ge(S("NPt"), 2)
            pe.wait_ge(S("bus0"), 1)
            for tile in range(2 * NP):
                if tile >= 2:
                    pe.wait_ge(S("q_ev"), tile - 1)
                q_tile(0, tile)
            att_loop(pe, step)
            for q in range(NQ):
                pe.wait_ge(S("o_ev"), 2 * NG)
                if q >= 4:
                    pe.wait_ge(S("a_h"), 4 * (q // 2 - 2) + 3 + q % 2)
                for k in range(QM):
                    m = q * QM + k
                    mm = pe.transpose(PS[:, 4 + q % 4, k * 128:(k + 1) * 128], AO[:, m * 128:(m + 1) * 128], ident[:, :])
                mm.then_inc(S("ao_tp"), 1)
            for q in range(NQ):
                pe.wait_ge(S("ln_o"), 4 * NC + q // 2 + 1)
                if q >= 2:
                    pe.wait_ge(S("x_f"), q - 1)
                for k in range(4):
                    mm = pe.transpose(PS[0:D, q % 2, k * 128:(k + 1) * 128], X[:, 4 * q + k, :], ident[:, :])
                mm.then_inc(S("x_tp"), 1)

            def gates_x(i, u, first=False):
                xt = XF[:, bass.ds(256 * i + 64 * u, 64)]
                bank = PS[:, 2 + u % 2, :]
                if not (first and u < 2):
                    pe.wait_ge(S("l_t"), 4 * i + u - 1)
                if u % 2 == 0 and not first:
                    pe.wait_ge(S("l_out"), 2 * i + u // 2 - 2)
                pe.matmul(bank[:, 0:64], UIO[:, :], xt, start=True, stop=False, skip_group_check=True)
                n = 128 if first and u < 2 else 64
                mm = pe.matmul(bank[0:n, 64:128], UG[:, 0:n], xt, start=False, stop=(first and u == 0), skip_group_check=True)
                if first and u == 0:
                    mm.then_inc(S("l_v"), 1)

            def gates_h(i, u, first=False):
                bank = PS[:, 2 + u % 2, :]
                pe.wait_ge(S("l_h"), 4 * i + u)
                pe.nop().then_inc(S("l_hp"), 1)
                hp = HB[:, (u - 1) % 4, :]
                for h in range(2):
                    r = slice(64 * h, 64 * h + 64)
                    pe.matmul(bank[r, 0:64], VIO[:, r], hp, start=False, stop=True, skip_group_check=True)
                pe.matmul(bank[0:64, 64:128], VG[:, :], hp, start=False, stop=True, skip_group_check=True).then_inc(S("l_v"), 1)
                if u % 2 == 0:
                    out_tp((u // 2 - 1) % 2)

            def out_tp(par):
                pe.transpose(PS[:, 4 + par, 0:D], HB[:, 2 * par:2 * par + 2, :].rearrange("p a b -> p (a b)"), ident[0:D, 0:D]).then_inc(S("l_tp"), 1)

            pe.wait_ge(S("x_f"), NQ)
            pe.wait_ge(S("a_h"), 4 * NC)
            gates_x(0, 0, first=True)
            for u in range(1, 4):
                gates_x(0, u, first=True)
                gates_h(0, u, first=True)
            with pe.Fori(1, T // 4) as i:
                for u in range(4):
                    gates_x(i, u)
                    gates_h(i, u)
            pe.wait_ge(S("l_out"), NM - 2)
            pe.wait_ge(S("l_h"), T)
            out_tp(1)


_INS = ["x", "txt", "L0_tok_W", "L0_tok_b", "L0_attn_Win", "L0_attn_bin_", "L0_attn_Wout", "L0_attn_bout",
        "L0_attn_A", "L0_attn_Bm", "L0_attn_Cm", "L0_attn_Dm",
        "L0_ffn_gate_w", "L0_ffn_gate_b", "L0_ffn_w1", "L0_ffn_b1", "L0_ffn_w2", "L0_ffn_b2",
        "L0_ffn_gamma", "L0_ffn_beta",
        "L1_attn_Wq", "L1_attn_bq", "L1_attn_Wk", "L1_attn_bk", "L1_attn_Wv", "L1_attn_bv",
        "L1_attn_Wu", "L1_attn_bu",
        "L1_ffn_U_i", "L1_ffn_V_i", "L1_ffn_b_i", "L1_ffn_U_c", "L1_ffn_V_c", "L1_ffn_b_c",
        "L1_ffn_U_o", "L1_ffn_V_o", "L1_ffn_b_o"]


def kernel(**inputs):
    import numpy as np
    import concourse.bacc as bacc
    from concourse.bass_utils import run_bass_kernel_spmd

    nc = bacc.Bacc("TRN2", target_bir_lowering=False, num_devices=1)
    arrays, args = {}, []
    for name in _INS:
        a = np.ascontiguousarray(inputs[name])
        arrays["in_" + name] = a
        args.append(nc.dram_tensor("in_" + name, a.shape, mybir.dt.from_np(a.dtype), kind="ExternalInput").ap())
    b, tx, d, _ = inputs["x"].shape
    shape = (b, tx + inputs["txt"].shape[1], d)
    out = nc.dram_tensor("out_0", shape, F32, kind="ExternalOutput").ap()
    early_fusion(nc, *args, out)
    r = run_bass_kernel_spmd(nc, [arrays], core_ids=[0])
    return r.results[0]["out_0"]
```

```python
from contextlib import ExitStack

import concourse.bass as bass
from concourse import mybir

F32 = mybir.dt.float32
F32R = mybir.dt.float32r
BF16 = mybir.dt.bfloat16
ALU = mybir.AluOpType
ACT = mybir.ActivationFunctionType
AX_X = mybir.AxisListType.X



def early_fusion(nc, x, txt, tok_W, tok_b, Win, bin_, Wout, bout, A, Bm, Cm, Dm,
                 gate_w, gate_b, w1, b1, w2, b2, gamma, beta,
                 Wq, bq, Wk, bk, Wv, bv, Wu, bu,
                 U_i, V_i, b_i, U_c, V_c, b_c, U_o, V_o, b_o, out):
    NB, TX, D, NF = x.shape
    TT = txt.shape[1]
    T = TX + TT
    NM = T // 2
    NK = NM // 2
    TOK = T * NB
    L = A.shape[0]
    HD = tok_W.shape[0]
    E, _, F = w1.shape
    NH = Wq.shape[1] // D
    NP = NH // 2
    EPS = 1e-5
    NEG = -1e30
    CH = 8
    NC = NM // CH
    KC = 4
    NJ = NK // KC
    QM = 4
    NQ = NM // QM
    GB = 4
    NG = NB // GB
    WBW = T // 2 + T - 1
    assert NB == 64 and D == 64 and F == 128 and T % 4 == 0 and NK % KC == 0

    with ExitStack() as ctx:
        def sb(name, shape, dt=F32):
            return ctx.enter_context(nc.sbuf_tensor(name, shape, dt))

        def sem(name):
            return ctx.enter_context(nc.semaphore(name))

        H = sb("H", [128, NM, D])
        X = sb("X", [128, NM, D])
        UT = sb("UT", [128, NK, 2, D])
        UF = sb("UF", [128, NK, 128])
        Y1 = sb("Y1", [128, NM * D])
        Y2 = sb("Y2", [128, NM * D])
        XC = sb("XC", [128, NM * D])
        BIG = sb("BIG", [128, 32 * D * NF])
        XS = sb("XS", [128, TOK], F32R)
        ident = sb("ident", [128, 128])
        identb = sb("identb", [128, 128], BF16)
        ii = sb("ii", [128, D], F32R)
        o128 = sb("o128", [128, 128])
        cD = sb("cD", [128, 1])
        mhalf = sb("mhalf", [128, 64])
        wtok = sb("wtok", [128, NF + 1])
        wm = sb("wm", [128, NF + 1])
        bds = sb("bds", [128, L + 2, 128])
        bdt = sb("bdt", [128, L + 2, 128])
        binr = sb("binr", [128, D])
        boutr = sb("boutr", [128, D])
        Am = sb("Am", [D, 2, L, D])
        Am2 = sb("Am2", [D, 2, L, D])
        Cs = sb("Cs", [D, L, D])
        Gk = sb("Gk", [D, L, T])
        BB = sb("BB", [D, L, 2, D])
        WQKh = sb("WQKh", [128, 2, NH * D], F32R)
        WQKl = sb("WQKl", [128, 2, NH * D], F32R)
        WB = sb("WB", [128, L, WBW + 1])
        scr = sb("scr", [128, 1])
        lnab = sb("lnab", [128, L, 2])
        Cc = sb("Cc", [128, NK, 2])
        st = sb("st", [128, 4, NM])
        W1h = sb("W1h", [128, E, F], F32R)
        W1l = sb("W1l", [128, E, F], F32R)
        GWs = sb("GWs", [128, E])
        GWhl = sb("GWhl", [128, 2, E], F32R)
        gbr = sb("gbr", [128, E])
        b1s = sb("b1s", [E, F])
        b1T = sb("b1T", [F, E])
        w2s = sb("w2s", [F, E, D])
        b2f = sb("b2f", [3 * E, 2, D])
        b2p = sb("b2p", [3 * E, 3, 2 * D], BF16)
        gs = sb("gs", [128, 8, NM])
        sel = sb("sel", [3 * E, E, F], BF16)
        rev = sb("rev", [128, E])
        gam = sb("gam", [128, D])
        bet = sb("bet", [128, D])
        XSg = sb("XSg", [128, 2, GB, T], F32R)
        mask = sb("mask", [T, NP, T], BF16)
        valid = sb("valid", [T, 1])
        Wvs = sb("Wvs", [D, NH * D])
        WvT = sb("WvT", [128, NP, D])
        Wus = sb("Wus", [128, NP, D])
        NPt = sb("NPt", [128, NP, D])
        bqk = sb("bqk", [128, 2, NP])
        bvs = sb("bvs", [128, NP])
        bus = sb("bus", [128, 2])
        am = sb("am", [T, 4, 4, NH])
        UIO = sb("UIO", [D + 1, 128])
        UG = sb("UG", [D + 1, D])
        VIO = sb("VIO", [D, 128])
        VG = sb("VG", [D, D])
        sems = {}

        def S(name):
            if name not in sems:
                sems[name] = sem(name)
            return sems[name]

        PS = ctx.enter_context(nc.psum_tensor("PS", [128, 8, 512], F32))

        W1s = Y1[:, 0:E * F].rearrange("p (e f) -> p e f", e=E)
        WQs = Y1[:, E * F:E * F + 2 * NH * D].rearrange("p (a c) -> p a c", a=2)
        GPT = UT[:, :, :, :].rearrange("p k h d -> p (k h d)").bitcast(BF16)[:, 0:NM * 3 * E]
        GP = UF[:, :, :].rearrange("p k c -> p (k c)").bitcast(BF16)
        PSb = PS[:, :, :].bitcast(BF16)
        MO = BIG[:, 0:2 * 512]
        Rb = Y2[:, 0:2048].rearrange("p (a c) -> p a c", a=4)
        Hb = XC[:, 0:2048].rearrange("p (a c) -> p a c", a=4)
        XF = BIG[0:D + 1, 0:TOK]
        CW = 1024
        Xcen, Xsqr, Xnrm = [t[:, 0:512].rearrange("p (m d) -> p m d", d=D) for t in (XC, Y2, Y1)]
        AO = BIG[:, 0:TOK]
        QK = [t.rearrange("p (a c) -> p a c", a=2 * NP) for t in (UT[:, :, :, :].rearrange("p k h d -> p (k h d)"),
                                                                  UF[:, :, :].rearrange("p k c -> p (k c)"))]
        Pb = Y1[0:T, 0:4 * NH * T].rearrange("p (n a h j) -> p n a h j", n=4, a=2, h=NP)
        XT = XC[0:T, NP * GB * T:NP * GB * T + 2 * GB * D].rearrange("p (n b d) -> p n b d", n=2, b=GB)
        PT = Y2[0:T, 0:2 * NH * T].rearrange("p (n a c) -> p n a c", n=2, a=2)
        Zg = [t.rearrange("p (h b i) -> p h b i", h=NP, b=GB) for t in (Y2[:, 2 * NH * T:2 * NH * T + NP * GB * T],
                                                                        XC[:, 0:NP * GB * T])]
        UTf = UT[:, :, :, :].rearrange("p k h d -> p (k h d)")
        Tb = UTf[:, 0:256].rearrange("p (a c) -> p a c", a=2)
        TC = UTf[:, 256:320]
        Cb = UTf[0:D, 320:448].rearrange("p (a c) -> p a c", a=2)
        HC = UTf[0:D, 448:512]
        HB = UTf[0:D, 512:768].rearrange("p (a c) -> p a c", a=4)
        Ysum = Y1[:, 0:512].rearrange("p (m d) -> p m d", d=D)
        Ygam = Y1[:, 512:1024].rearrange("p (m d) -> p m d", d=D)
        Ynrm = Y1[:, 1024:1536].rearrange("p (m d) -> p m d", d=D)
        Ycen = XC[:, 2048:3072].rearrange("p (r m d) -> p r m d", r=2, d=D)
        Ysqr = Y2[:, 2048:3072].rearrange("p (r m d) -> p r m d", r=2, d=D)
        Xr = BIG[:, :].rearrange("p (m c) -> p m c", c=D * NF)

        def halves(t):
            return t[:, :, :].rearrange("p (k h) d -> p k h d", h=2)

        def view_km(t):
            return t[:, :, :].rearrange("p (h k) d -> p k h d", h=2)

        def ssm_scale(pool, l, j):
            n = l * NJ + j
            sj = slice(j * KC * 2, (j + 1) * KC * 2)
            pool.wait_ge(S("s_v"), n + 1)
            pool.tensor_tensor(st[:, 3, sj], st[:, 2, sj], mhalf[:, 0:KC * 2], ALU.pow).then_inc(S("s_r"), 1)
            pool.wait_ge(S("s_r"), n + 1)
            pool.tensor_tensor(ssm_cols(UT, j).rearrange("p (a d) -> p a d", d=D),
                               XC[:, j * 512:j * 512 + 512].rearrange("p (a d) -> p a d", d=D),
                               st[:, 3, sj].unsqueeze(2).to_broadcast([128, KC * 2, D]), ALU.mult).then_inc(S("s_un"), 1)

        def ssm_cols(t, j):
            return t[:, j * KC:(j + 1) * KC, :, :].rearrange("p k h d -> p (k h d)")

        def ln_dve(dve, p, src, ready, order=range(NC), between=None):
            def front(i, c):
                n = p * NC + i + 1
                sc = slice(c * CH, (c + 1) * CH)
                ready(c)
                dve.tensor_reduce(st[:, 0, sc], src[:, sc, :], AX_X, ALU.add).then_inc(S("ln_s"), 1)
                dve.wait_ge(S("ln_s"), n)
                dve.scalar_tensor_tensor(XC[:, c * 512:c * 512 + 512].rearrange("p (a d) -> p a d", d=D),
                                         st[:, 0, sc].unsqueeze(2).to_broadcast([128, CH, D]), -1.0 / D, src[:, sc, :],
                                         ALU.mult, ALU.add).then_inc(S("ln_c"), 1)

            def back(i, c):
                n = p * NC + i + 1
                sc = slice(c * CH, (c + 1) * CH)
                dve.wait_ge(S("ln_q"), n)
                dve.tensor_reduce(st[:, 2, sc], Y2[:, c * 512:c * 512 + 512].rearrange("p (a d) -> p a d", d=D),
                                  AX_X, ALU.add).then_inc(S("ln_v0"), 1)
                dve.wait_ge(S("ln_v0"), n)
                dve.tensor_scalar(st[:, 2, sc], st[:, 2, sc], 1.0 / D, EPS, ALU.mult, ALU.add).then_inc(S("ln_v"), 1)

            for i, c in enumerate(order):
                front(i, c)
                if i:
                    back(i - 1, order[i - 1])
                if between:
                    between(i)
            back(NC - 1, order[NC - 1])

        def ln_act(act, p, order=range(NC), between=None):
            for i, c in enumerate(order):
                act.wait_ge(S("ln_c"), p * NC + i + 1)
                act.activation(Y2[:, c * 512:c * 512 + 512], XC[:, c * 512:c * 512 + 512], ACT.Square).then_inc(S("ln_q"), 1)
                if between:
                    between(i)

        def ln_pool(pool, p, dst, order=range(NC)):
            for i, c in enumerate(order):
                n = p * NC + i + 1
                sc = slice(c * CH, (c + 1) * CH)
                pool.wait_ge(S("ln_v"), n)
                pool.tensor_tensor(st[:, 3, sc], st[:, 2, sc], mhalf[:, 0:CH], ALU.pow).then_inc(S("ln_r"), 1)
                pool.wait_ge(S("ln_r"), n)
                pool.tensor_tensor(dst(c), XC[:, c * 512:c * 512 + 512].rearrange("p (a d) -> p a d", d=D),
                                   st[:, 3, sc].unsqueeze(2).to_broadcast([128, CH, D]), ALU.mult).then_inc(S("ln_o"), 1)

        def ln_no(j, r):
            return 2 * NC + 2 * j + r + 1

        def ln_last(c):
            return 4 * NC + c + 1

        def ln_part(r):
            return slice(r * CH, (r + 1) * CH)

        FOLD = [c + h * (NC // 2) for c in range(NC // 2) for h in range(2)]
        XFOLD = [c for c in FOLD if c < TX // 2 // CH]
        nsq = (T - 1).bit_length() - 1

        def xcol(c, f):
            v = Xr[:, c * CH:(c + 1) * CH, :].rearrange("p m (i f) -> p (m i) f", f=NF)
            return v[:, :, f]

        def bank4(b):
            return PS[:, b, :].rearrange("p (k c) -> p k c", k=KC)

        def grant(eng, name, n):
            for _ in range(n):
                eng.nop().then_inc(S(name), 1)

        def XSp():
            return XS[:, :].rearrange("p (m a c) -> p m a c", a=2, c=128)

        def xs_pe(pe, lnp, after):
            for c in range(NC):
                pe.wait_ge(S("ln_o"), lnp * NC + c + 1)
                if c >= 2:
                    pe.wait_ge(S("xs_l"), 2 * (c - 1))
                for k in range(4):
                    last = pe.transpose(PS[:, 4 + c % 2, k * 128:k * 128 + 128],
                                        X[:, c * CH + 2 * k:c * CH + 2 * k + 2, :].rearrange("p m d -> p (m d)"), ident[:, :])
                last.then_inc(S("xs_tp"), 1)
                if c:
                    after(c - 1)
            after(NC - 1)

        def xs_act(act, after):
            for c in range(NC):
                act.wait_ge(S("xs_tp"), c + 1)
                for a in range(2):
                    act.activation(XSp()[0:64, 4 * c:4 * c + 4, a, :], bank4(4 + c % 2)[64 * a:64 * a + 64], ACT.Copy).then_inc(S("xs_h"), 1)
                after(c)

        def xs_dve(dve, after):
            for c in range(NC):
                for a in range(2):
                    dve.wait_ge(S("xs_h"), 2 * c + a + 1)
                    dve.tensor_tensor(XSp()[64:128, 4 * c:4 * c + 4, a, :], bank4(4 + c % 2)[64 * a:64 * a + 64],
                                      XSp()[0:64, 4 * c:4 * c + 4, a, :].bitcast(F32), ALU.subtract).then_inc(S("xs_l"), 1)
                after(c)

        GPART = ((0, 2 * CH), (2 * CH, NM))
        GOPS, GEXP = 25, 14

        def gates_done(p, k):
            return GOPS * p + k

        def has(d, k, first, drain):
            return not (first and k < d) and not (drain and k >= d)

        DRAIN = 4

        def att_loop(eng, step):
            for k in range(8):
                step(0, k, first=True)
            with eng.Fori(1, NB // 8 - 1) as i:
                for k in range(8):
                    step(i, k)
            for k in range(8):
                step(NB // 8 - 1, k, last=True)
            for k in range(DRAIN):
                step(NB // 8, k, drain=True)

        block = ctx.enter_context(nc.Block())

        @block.sync
        def _(sp):
            sp.dma_start(wtok[:, 0:NF], tok_W).then_inc(S("ld_tok"), 16)
            sp.dma_start(wtok[:, NF:NF + 1], tok_b.rearrange("(p a) -> p a", a=1)).then_inc(S("ld_tok"), 16)
            xv = x.rearrange("b (m s) i f -> s b m (i f)", s=2)
            for c in XFOLD:
                for s in range(2):
                    sp.dma_start(Xr[64 * s:64 * s + 64, c * CH:(c + 1) * CH, :],
                                 xv[s, :, c * CH:(c + 1) * CH, :]).then_inc(S("ld_x%d" % c), 16)
            tv = txt.rearrange("b (m s) d -> s b m d", s=2)
            for s in range(2):
                sp.dma_start(H[64 * s:64 * s + 64, TX // 2:NM, :], tv[s]).then_inc(S("ld_txt"), 16)
            sp.wait_ge(S("bds0"), 1)
            for s in range(2):
                r = slice(64 * s, 64 * s + 64)
                sp.dma_start(bds[r, 0, r], Win).then_inc(S("ld_bd"), 16)
                sp.dma_start(bds[r, 1:L + 1, r], Dm.rearrange("l o i -> o l i")).then_inc(S("ld_bd"), 16)
                sp.dma_start(bds[r, L + 1, r], Wout).then_inc(S("ld_bd"), 16)
            sp.dma_start(binr[:, :], bin_.rearrange("(a n) -> a n", a=1).to_broadcast([128, D])).then_inc(S("ld_bd"), 16)
            sp.dma_start(boutr[:, :], bout.rearrange("(a n) -> a n", a=1).to_broadcast([128, D])).then_inc(S("ld_bd"), 16)
            for s in range(2):
                sp.dma_start(W1s[64 * s:64 * s + 64, :, :],
                             w1.rearrange("e h f -> h e f")).then_inc(S("ld_w1"), 16)
                sp.dma_start(GWs[64 * s:64 * s + 64, :], gate_w).then_inc(S("ld_w1"), 16)
                sp.dma_start(WQs[64 * s:64 * s + 64, 0, :], Wq).then_inc(S("ld_w1"), 16)
                sp.dma_start(WQs[64 * s:64 * s + 64, 1, :], Wk).then_inc(S("ld_w1"), 16)
            sp.dma_start(b1s[:, :], b1).then_inc(S("ld_moe"), 16)
            sp.dma_start(w2s[:, :, :], w2.rearrange("e f h -> f e h")).then_inc(S("ld_moe"), 16)
            for g in range(3):
                sp.dma_start(b2f[E * g:E * g + E, 0, :], b2).then_inc(S("ld_moe"), 16)
            for k in range(2):
                sp.dma_start(bqk[:, k, :], (bq, bk)[k].rearrange("(c p) -> p c", p=128), allow_slow_non_contiguous=True).then_inc(S("ld_at"), 16)
            sp.dma_start(bvs[:, :], bv.rearrange("(c p) -> p c", p=128), allow_slow_non_contiguous=True).then_inc(S("ld_at"), 16)
            sp.dma_start(bus[0:D, 0:1], bu.rearrange("(p a) -> p a", a=1)).then_inc(S("ld_at"), 16)
            sp.dma_start(Wvs[:, :], Wv).then_inc(S("ld_at"), 16)
            sp.dma_start(Wus[:, :, :], Wu.rearrange("(c p) o -> p c o", p=128)).then_inc(S("ld_at"), 16)
            for dst, lo, hi in ((UIO, (U_i, b_i), (U_o, b_o)), (UG, (U_c, b_c), None), (VIO, (V_i, None), (V_o, None)),
                                (VG, (V_c, None), None)):
                for h, (w, b) in enumerate((lo, hi) if hi else (lo,)):
                    sp.dma_start(dst[0:D, 64 * h:64 * h + 64], w).then_inc(S("ld_ls"), 16)
                    if b is not None:
                        sp.dma_start(dst[D:D + 1, 64 * h:64 * h + 64], b.rearrange("(a n) -> a n", a=1)).then_inc(S("ld_ls"), 16)
            for t, v, n in ((gbr, gate_b, E), (gam, gamma, D), (bet, beta, D)):
                sp.dma_start(t[:, :], v.rearrange("(a n) -> a n", a=1).to_broadcast([128, n])).then_inc(S("ld_moe"), 16)

            ov = out.rearrange("b (m s) d -> s b m d", s=2)
            with sp.Fori(0, T // 4) as i:
                sp.wait_ge(S("l_out"), 2 * i + 2)
                for h in range(2):
                    sp.dma_start(ov[h, :, bass.ds(2 * i, 2), :], X[64 * h:64 * h + 64, bass.ds(2 * i, 2), :]).then_inc(S("st"), 16)
            sp.wait_ge(S("st"), 16 * 2 * (T // 4))

        @block.gpsimd
        def _(pool):
            done = {}

            def seq(ins, name):
                done[name] = done.get(name, 0) + 1
                ins.then_inc(S(name), 1)
                pool.wait_ge(S(name), done[name])

            seq(pool.memset(bds[:, :, :], 0.0), "bds0")
            seq(pool.memset(ident[:, :], 0.0), "id0")
            seq(pool.affine_select(out=ident[:, :], in_=ident[:, :], compare_op=ALU.not_equal, fill=1.0,
                               base=0, pattern=[[-1, 128]], channel_multiplier=1), "ident")
            seq(pool.memset(o128[:, :], 1.0 / HD), "cst")
            seq(pool.memset(cD[:, :], 1.0 / D), "cst")
            seq(pool.memset(mhalf[:, :], -0.5), "cst")
            seq(pool.memset(WB[:, :, :], 0.0), "cst")
            seq(pool.memset(lnab[:, :, 0], 1.0 / D), "cst")
            seq(pool.memset(lnab[:, :, 1], EPS), "cst")
            seq(pool.memset(lnab[:, L - 1, 0:1], (1.0 + EPS) / D), "cst")
            seq(pool.memset(lnab[:, L - 1, 1:2], EPS * EPS), "cst")
            seq(pool.tensor_copy(identb[:, :], ident[:, :]), "identb")
            seq(pool.memset(sel[:, :, :], 0.0), "sel")
            for g in range(3):
                seq(pool.affine_select(out=sel[:, :, :], in_=sel[:, :, :], compare_op=ALU.not_equal, fill=1.0,
                                   base=-E * g, pattern=[[-1, E], [0, F]], channel_multiplier=1), "sel")
            seq(pool.memset(mask[:, :, :], 0.0), "mask")
            seq(pool.memset(valid[:, :], 1.0), "mask")
            seq(pool.affine_select(out=mask[:, :, :], in_=mask[:, :, :], compare_op=ALU.is_gt, fill=NEG, base=0,
                               pattern=[[0, NP], [-1, T]], channel_multiplier=1), "mask")
            seq(pool.affine_select(out=valid[:, :], in_=valid[:, :], compare_op=ALU.is_gt, fill=0.0, base=0,
                               pattern=[[0, 1]], channel_multiplier=1), "mask")
            for e in range(E):
                seq(pool.memset(rev[:, e:e + 1], float(E - e)), "rev")
            ln_pool(pool, 0, lambda c: halves(X)[:, c % (NC // 2) * CH:(c % (NC // 2) + 1) * CH, c // (NC // 2), :], order=FOLD)
            for i, (w, h, lo) in enumerate(((W1s, W1h, W1l), (WQs, WQKh, WQKl), (GWs, GWhl[:, 0, :], GWhl[:, 1, :]))):
                pool.wait_ge(S("whi"), i + 1)
                seq(pool.tensor_tensor(lo[:, :, :] if i < 2 else lo, w[:, :, :] if i < 2 else w[:, :],
                                   (h[:, :, :] if i < 2 else h).bitcast(F32), ALU.subtract), "wlo")
            pool.wait_ge(S("ld_at"), 16 * 6)
            pool.wait_ge(S("ld_ls"), 16 * 9)
            for t, f in ((bqk[:, 0, :], D ** -0.5), (UIO[:, :], 0.5), (VIO[:, :], 0.25), (VG[:, :], 0.5)):
                seq(pool.tensor_scalar(t, t, f, None, ALU.mult), "wsc")
            pool.wait_ge(S("ld_moe"), 16 * 8)
            seq(pool.memset(b2p[:, :, D:2 * D], 0.0), "b2z")
            for i in range(3):
                seq(pool.tensor_copy(b2p[:, i, 0:D], b2f[:, i % 2, :]), "b2c")
                if i < 2:
                    seq(pool.tensor_tensor(b2f[:, (i + 1) % 2, :], b2f[:, i % 2, :], b2p[:, i, 0:D], ALU.subtract), "b2c")
            pool.wait_ge(S("ln_c"), NC)
            pool.wait_ge(S("ld_bd"), 16 * 8)
            pool.tensor_tensor(H[:, :, :], H[:, :, :], boutr[:, :].unsqueeze(1).to_broadcast([128, NM, D]), ALU.add).then_inc(S("hb"), 1)
            with pool.Fori(0, L) as l:
                for j in range(NJ):
                    ssm_scale(pool, l, j)
            ln_pool(pool, 1, lambda c: X[:, c * CH:(c + 1) * CH, :])
            pool.wait_ge(S("ln_c"), 2 * NC)
            pool.tensor_tensor(H[:, :, :], H[:, :, :], bet[:, :].unsqueeze(1).to_broadcast([128, NM, D]), ALU.add).then_inc(S("hb"), 1)
            def power(j, r):
                pool.wait_ge(S("ln_v"), ln_no(j, r))
                pool.tensor_tensor(st[:, 3, ln_part(r)], st[:, 2, ln_part(r)], mhalf[:, 0:CH], ALU.pow).then_inc(S("ln_r"), 1)

            with pool.Fori(0, NC - 1) as j:
                for r, dst in ((0, Ygam), (1, Ynrm)):
                    power(j, r)
                    pool.wait_ge(S("ln_r"), ln_no(j, r))
                    pool.tensor_tensor(dst, Ycen[:, r, :, :], st[:, 3, ln_part(r)].unsqueeze(2).to_broadcast([128, CH, D]),
                                       ALU.mult).then_inc(S("ln_o"), 1)
                    if r == 0:
                        pool.wait_ge(S("ln_o"), ln_no(j, r))
                        pool.tensor_tensor(dst, dst, gam[:, :].unsqueeze(1).to_broadcast([128, CH, D]), ALU.mult).then_inc(S("f_g"), 1)
            for r in range(2):
                power(NC - 1, r)
            pool.wait_ge(S("ln_o"), 4 * NC)

            def step(i, k, first=False, last=False, drain=False):
                B = 8 * i + k
                if not has(1, k, first, drain):
                    return
                pool.wait_ge(S("a_rv"), B)
                Pn = Pb[:, (k - 1) % 4, :, :, :].rearrange("p a h j -> p (a h) j")
                pool.tensor_tensor(Pn, Pn, am[:, (k - 1) % 4, 3, :].unsqueeze(2).to_broadcast([T, NH, T]), ALU.mult).then_inc(S("a_pn"), 1)

            att_loop(pool, step)
            pool.wait_ge(S("a_pn"), NB)
            pool.wait_ge(S("ao_tp"), 2)
            pool.memset(XF[D:D + 1, 0:CW], 1.0).then_inc(S("ones"), 1)
            pool.wait_ge(S("ones"), 1)

            def norm(c):
                pool.wait_ge(S("ln_v"), ln_last(c))
                pool.tensor_tensor(st[:, 3, 0:CH], st[:, 2, 0:CH], mhalf[:, 0:CH], ALU.pow).then_inc(S("ln_r"), 1)
                pool.wait_ge(S("ln_r"), ln_last(c))
                pool.tensor_tensor(Xnrm, Xcen, st[:, 3, 0:CH].unsqueeze(2).to_broadcast([128, CH, D]), ALU.mult).then_inc(S("ln_o"), 1)

            norm(0)
            pool.wait_ge(S("ln_o"), ln_last(0))
            pool.wait_ge(S("ao_tp"), NQ)
            pool.memset(XF[D:D + 1, CW:TOK], 1.0).then_inc(S("ones"), 1)
            pool.wait_ge(S("ones"), 2)
            with pool.Fori(1, NC) as c:
                norm(c)

        @block.scalar
        def _(act):
            act.dma_start(Am[:, 0, :, :], A.rearrange("l n m -> n l m")).then_inc(S("ld_a"), 16)
            act.dma_start(Cs[:, :, :], Cm.rearrange("l h n -> h l n")).then_inc(S("ld_a"), 16)
            for s in range(2):
                act.dma_start(BB[:, :, s, :], Bm.rearrange("l n h -> n l h")).then_inc(S("ld_a"), 16)
            def power(i):
                act.wait_ge(S("p_kry"), i + 1)
                nxt = (Am if i == 0 else (Am2 if i % 2 else Am))
                act.activation(nxt[:, 1, :, :], PS[0:D, 1, 0:L * D].rearrange("p (l m) -> p l m", l=L), ACT.Copy).then_inc(S("p_at"), 1)

            power(0)
            act.wait_ge(S("p_wm"), 1)
            for i, c in enumerate(XFOLD):
                act.wait_ge(S("ld_x%d" % c), 32)
                act.activation(H[:, c * CH:(c + 1) * CH, :].rearrange("p m d -> p (m d)"), xcol(c, 0), ACT.Identity,
                               bias=wm[:, NF:NF + 1], scale=wm[:, 0:1]).then_inc(S("tok0"), 1)
                power(i + 1)
            ln_act(act, 0, FOLD, lambda i: power(i + 1 + len(XFOLD)) if i + 1 + len(XFOLD) <= nsq else None)
            for j in range(NJ):
                act.wait_ge(S("w_tp"), j + 1)
                act.activation(UF[:, j * KC:(j + 1) * KC, :], bank4(4 + j % 2), ACT.Copy).then_inc(S("w_x"), 1)
            for j in range(NJ):
                act.wait_ge(S("s_tp"), j + 1)
                act.activation(UF[:, j * KC:(j + 1) * KC, :], bank4(4 + j % 2), ACT.Copy).then_inc(S("s_uf"), 1)
            with act.Fori(0, L) as l:
                act.activation(scr[:, :], mhalf[:, 0:1], ACT.Gelu)
                for w in range(NJ + 3):
                    if w < NJ:
                        sl = slice(w * 512, w * 512 + 512)
                        if w == 0:
                            act.wait_ge(S("s_cc"), 2 * l + 2)
                        act.wait_ge(S("s_du"), l * NJ + w + 1)
                        for a in range(2 * KC):
                            last = act.activation(Y2[:, sl][:, a * D:(a + 1) * D], PS[:, w % 3, a * D:(a + 1) * D], ACT.Gelu,
                                                bias=Cc[:, w * KC + a // 2, a % 2:a % 2 + 1])
                        last.then_inc(S("s_gelu"), 1)
                    if 0 <= w - 1 < NJ:
                        j = w - 1
                        sl = slice(j * 512, j * 512 + 512)
                        act.wait_ge(S("s_c"), l * NJ + j + 1)
                        act.activation(Y2[:, sl], XC[:, sl], ACT.Square).then_inc(S("s_q"), 1)
                    if 0 <= w - 3 < NJ:
                        j = w - 3
                        act.wait_ge(S("s_tp"), l * NJ + NJ + j + 1)
                        act.activation(UF[:, j * KC:(j + 1) * KC, :], bank4(4 + j % 2), ACT.Copy).then_inc(S("s_uf"), 1)
            ln_act(act, 1)

            def gates_exp(p):
                m = slice(*GPART[p])
                act.wait_ge(S("gchain"), gates_done(p, GEXP))
                act.activation(gs[:, 4, m], gs[:, 3, m], ACT.Exp).then_inc(S("g_exp"), 1)

            xs_act(act, lambda c: gates_exp(0) if c == 4 else None)
            act.wait_ge(S("p_wvt"), 1)
            act.activation(WvT[:, :, :], PS[:, 7, 0:NP * D].rearrange("p (c d) -> p c d", d=D), ACT.Copy).then_inc(S("WvT"), 1)

            def gates_out(c):
                act.wait_ge(S("gp_tp"), c + 1)
                act.activation(GP[0:3 * E, c * CW:(c + 1) * CW], PSb[0:3 * E, 2 + c % 2, :], ACT.Copy).then_inc(S("gp"), 1)

            for c in range(2):
                gates_out(c)

            def square(j, r):
                act.wait_ge(S("ln_c"), ln_no(j, r))
                act.activation(Ysqr[:, r, :, :], Ycen[:, r, :, :], ACT.Square).then_inc(S("ln_q"), 1)

            def hi_part(j, a):
                if a == 0:
                    act.wait_ge(S("xs_tp"), NC + j + 1)
                act.activation(XSp()[0:64, bass.ds(4 * j, 4), a, :], bank4(2)[64 * a:64 * a + 64], ACT.Copy).then_inc(S("xs_h"), 1)

            def experts(i, first=False):
                for qq in range(2):
                    for e in range(E):
                        n = i * 2 * E + qq * E + e
                        act.wait_ge(S("m_z"), n + 1)
                        act.wait_ge(S("m_h"), n + 1)
                        act.activation(Rb[:, e % 4, :], PS[:, e % 2, :], ACT.Relu, bias=b1T[:, e:e + 1]).then_inc(S("m_r"), 1)
                        if e == 2 and not (first and qq == 0):
                            act.wait_ge(S("m_d"), i * 2 * E + qq * E + 4)
                            act.activation(MO[:, (1 - qq) * 512:(2 - qq) * 512], PS[:, 7 - qq, :], ACT.Copy).then_inc(S("m_mo"), 1)
                        if first and (qq, e) == (0, 12):
                            gates_exp(1)
                        if first and (qq, e) in ((1, 13), (1, 14)):
                            for c in range(NC - 4 + 2 * (e - 13), NC - 2 + 2 * (e - 13)):
                                gates_out(c)
                        if not first:
                            if (qq, e) in ((0, 11), (1, 4)):
                                square(i - 1, qq)
                            if (qq, e) in ((1, 11), (1, 12)):
                                hi_part(i - 1, e - 11)

            experts(0, first=True)
            with act.Fori(1, NC) as i:
                experts(i)
            act.wait_ge(S("m_d"), NQ * E + 4)
            act.activation(MO[:, 512:1024], PS[:, 7, :], ACT.Copy).then_inc(S("m_mo"), 1)
            for r in range(2):
                square(NC - 1, r)
            for a in range(2):
                hi_part(NC - 1, a)

            def q_evac(g, par, tile, bank):
                sc, bi = (D ** -0.5, bqk[:, 0, tile:tile + 1]) if tile < NP else (1.0, bqk[:, 1, tile - NP:tile - NP + 1])
                act.wait_ge(S("a_q"), 2 * NP * g + tile + 1)
                act.activation(QK[par][:, tile, :], PS[:, bank, 0:GB * T], ACT.Identity, bias=bi, scale=sc).then_inc(S("q_ev"), 1)

            def step(i, k, first=False, last=False, drain=False):
                B, g, bb = 8 * i + k, 2 * i + k // 4, k % 4
                nextq = not drain and not (last and k >= 4)
                if (bb == 0 and not first) or (drain and k == 3):
                    og = g - 2 + k // 3 if drain else g - 2
                    act.wait_ge(S("a_o"), og + 1)
                    o = AO.rearrange("p (t b) -> p b t", b=NB)[:, bass.ds(og * GB, GB), :]
                    ps = PS[:, 1, 0:GB * T].rearrange("p (b t) -> p b t", b=GB)
                    act.activation(o[:, :, 1:T], ps[:, :, 1:T], ACT.Identity, bias=bus[:, 1:2]).then_inc(S("o_ev"), 1)
                    act.activation(o[:, :, 0:1], ps[:, :, 0:1], ACT.Identity, bias=bus[:, 0:1]).then_inc(S("o_ev"), 1)
                if bb == 1 and not drain:
                    act.wait_ge(S("a_xt"), g + 1)
                    if not first:
                        act.wait_ge(S("a_z"), 4 * g - 4)
                    act.activation(XT[:, (k // 4) % 2, :, :], PS[0:T, 1, 0:GB * D].rearrange("p (b d) -> p b d", d=D), ACT.Copy).then_inc(S("xt_ev"), 1)
                if nextq:
                    if bb == 0 and not (first and k == 0):
                        act.wait_ge(S("a_s"), 4 * g)
                    q_evac(g + 1, (k // 4 + 1) % 2, 2 * bb, 0)
                if has(2, k, first, drain):
                    act.wait_ge(S("a_t"), B - 1)
                    if has(4, k, first, False):
                        act.wait_ge(S("a_z"), B - 3)
                    act.activation(PT[:, k % 2, :, :], PS[0:T, 6:8, 0:NP * T], ACT.Copy).then_inc(S("pt_ev"), 1)
                if nextq:
                    q_evac(g + 1, (k // 4 + 1) % 2, 2 * bb + 1, 1)
                if has(3, k, first, drain):
                    zg, zb = (k - 3) // 4, (k - 3) % 4
                    act.wait_ge(S("a_z"), B - 2)
                    if zb == 0 and not first:
                        act.wait_ge(S("a_o"), 2 * i + zg - 1)
                    act.activation(Zg[zg % 2][:, :, zb, :], PS[:, 0, 0:NP * T].rearrange("p (h c) -> p h c", h=NP), ACT.Copy).then_inc(S("z_ev"), 1)
                if not drain:
                    act.wait_ge(S("a_sub"), B + 1)
                    Pn = Pb[:, k % 4, :, :, :].rearrange("p a h j -> p (a h j)")
                    act.activation(Pn, Pn, ACT.Exp).then_inc(S("a_e"), 1)

            for tile in range(2 * NP):
                q_evac(0, 0, tile, tile)
            att_loop(act, step)
            def square_x(c):
                act.wait_ge(S("ln_c"), ln_last(c))
                act.activation(Xsqr, Xcen, ACT.Square).then_inc(S("ln_q"), 1)

            def copy_x(c, k):
                act.wait_ge(S("x_tp"), 2 * c + k + 1)
                act.activation(XF[0:D, bass.ds(c * CW + k * 512, 512)], PS[0:D, k, :], ACT.Copy).then_inc(S("x_f"), 1)

            def gates(i, u):
                t = 4 * i + u
                act.wait_ge(S("l_vi"), t + 1)
                act.activation(Tb[0:64, u % 2, 0:64], PS[0:64, 2 + u % 2, 0:64], ACT.Tanh).then_inc(S("l_t"), 1)
                act.wait_ge(S("l_vg"), t + 1)
                act.activation(Tb[0:64, u % 2, 64:128], PS[0:64, 6 + u % 2, 0:64], ACT.Tanh).then_inc(S("l_t"), 1)
                act.wait_ge(S("l_vo"), t + 1)
                act.activation(Tb[64:128, u % 2, 0:64], PS[64:128, 2 + u % 2, 0:64], ACT.Tanh).then_inc(S("l_to"), 1)
                act.wait_ge(S("l_c"), t + 1)
                act.activation(TC[64:128, :], Cb[:, 1, :], ACT.Tanh).then_inc(S("l_tc"), 1)

            def steps(c, last=False):
                for u in range(2 * CH):
                    gates(4 * c + u // 4, u % 4)
                    if last:
                        continue
                    if u == 4:
                        square_x(c + 1)
                    if u == 12:
                        copy_x(c + 1, 0)
                    if u == 13:
                        copy_x(c + 1, 1)

            square_x(0)
            act.wait_ge(S("ones"), 1)
            copy_x(0, 0)
            copy_x(0, 1)
            with act.Fori(0, NC - 1) as c:
                steps(c)
            steps(NC - 1, last=True)

        @block.vector
        def _(dve):
            dve.wait_ge(S("ident"), 1)
            for h in range(2):
                dve.tensor_copy(ii[64 * h:64 * h + 64, :], ident[64 * h:64 * h + 64, 64 * h:64 * h + 64]).then_inc(S("ii"), 1)
            dve.wait_ge(S("p_wmps"), 1)
            dve.tensor_copy(wm[:, :], PS[:, 0, 0:NF + 1]).then_inc(S("p_wm"), 1)
            dve.wait_ge(S("p_g0"), 1)
            dve.tensor_copy(Gk[:, :, 0], PS[0:D, 4, 0:L]).then_inc(S("p_gk"), 1)

            def krylov(i):
                m = 1 << i
                nm = min(m, T - m)
                dve.wait_ge(S("p_kry"), i + 2)
                dve.tensor_copy(Gk[:, :, m:m + nm], PS[0:D, 0, 0:L * nm].rearrange("p (l m) -> p l m", l=L)).then_inc(S("p_gk"), 1)
                if i < nsq:
                    nxt = Am2 if (i + 1) % 2 else Am
                    dve.tensor_copy(nxt[:, 0, :, :], PS[0:D, 2, 0:L * D].rearrange("p (l m) -> p l m", l=L)).then_inc(S("p_am"), 1)

            for i, c in enumerate(XFOLD):
                dve.wait_ge(S("tok0"), i + 1)
                hc = H[:, c * CH:(c + 1) * CH, :].rearrange("p m d -> p (m d)")
                for f in range(1, NF):
                    if f > 1:
                        dve.wait_ge(S("tokf"), (NF - 1) * i + f - 1)
                    dve.scalar_tensor_tensor(hc, xcol(c, f), wm[:, f:f + 1], hc, ALU.mult, ALU.add).then_inc(S("tokf"), 1)
                krylov(i)

            def ready(c):
                if c in XFOLD:
                    dve.wait_ge(S("tokf"), (NF - 1) * (XFOLD.index(c) + 1))
                else:
                    dve.wait_ge(S("ld_txt"), 32)
            ln_dve(dve, 0, H, ready, FOLD, lambda i: krylov(i + len(XFOLD)) if i + len(XFOLD) <= nsq else None)
            dve.wait_ge(S("p_w"), 1)
            dve.wait_ge(S("cst"), 8)
            pw = PS[:, 3, 0:L * T].rearrange("p (l t) -> p l t", l=L)
            dve.tensor_copy(WB[0:64, :, T // 2:T // 2 + T - 1], pw[0:64, :, 0:T - 1]).then_inc(S("p_wb"), 1)
            dve.tensor_copy(WB[64:128, :, T:T + T // 2 - 1], pw[64:128, :, 0:T // 2 - 1]).then_inc(S("p_wb"), 1)
            for h in range(2):
                dve.wait_ge(S("p_bd"), h + 1)
                dve.tensor_copy(bdt[:, 3 * h:3 * h + 3, :], PS[:, 6 + h, 0:384].rearrange("p (a c) -> p a c", a=3)).then_inc(S("p_bdt"), 1)
            dve.wait_ge(S("ld_bd"), 16 * 8)
            for j in range(NJ):
                dve.wait_ge(S("w_mm"), j + 1)
                dve.tensor_tensor(ssm_cols(UT, j).rearrange("p (a d) -> p a d", d=D),
                                  PS[:, j % 3, :].rearrange("p (a d) -> p a d", d=D),
                                  binr[:, :].unsqueeze(1).to_broadcast([128, KC * 2, D]), ALU.add).then_inc(S("w_u"), 1)
                if j == 1:
                    dve.wait_ge(S("ld_w1"), 16 * 8)
                    dve.tensor_copy(W1h[:, :, :], W1s[:, :, :]).then_inc(S("whi"), 1)
                    dve.tensor_copy(WQKh[:, :, :], WQs[:, :, :]).then_inc(S("whi"), 1)
                    dve.tensor_copy(GWhl[:, 0, :], GWs[:, :]).then_inc(S("whi"), 1)
            dve.wait_ge(S("p_b1"), 1)
            dve.tensor_copy(b1T[:, :], PS[:, 7, 0:E]).then_inc(S("b1T"), 1)
            dve.wait_ge(S("wlo"), 3)
            with dve.Fori(0, L) as l:
                dve.wait_ge(S("s_cps"), l + 1)
                cps = PS[0:64, 6, 0:T].rearrange("p (h k s) -> p k h s", h=2, s=2)
                for s in range(2):
                    dve.tensor_copy(Cc[64 * s:64 * s + 64, :, :], cps[:, :, :, s]).then_inc(S("s_cc"), 1)
                dve.wait_ge(S("s_cc"), 2 * l + 2)

                def back(j):
                    n = l * NJ + j + 1
                    sj = slice(j * KC * 2, (j + 1) * KC * 2)
                    dve.wait_ge(S("s_q"), n)
                    dve.tensor_reduce(st[:, 2, sj], Y2[:, j * 512:j * 512 + 512].rearrange("p (a d) -> p a d", d=D),
                                      AX_X, ALU.add).then_inc(S("s_v0"), 1)
                    dve.wait_ge(S("s_v0"), n)
                    dve.tensor_scalar(st[:, 2, sj], st[:, 2, sj], lnab[:, bass.ds(l, 1), 0], lnab[:, bass.ds(l, 1), 1],
                                      ALU.mult, ALU.add).then_inc(S("s_v"), 1)

                for j in range(NJ):
                    n = l * NJ + j + 1
                    sj = slice(j * KC * 2, (j + 1) * KC * 2)
                    y = Y1[:, j * 512:j * 512 + 512]
                    y3 = y.rearrange("p (a d) -> p a d", d=D)
                    dve.wait_ge(S("s_gelu"), n)
                    dve.tensor_tensor(y, Y2[:, j * 512:j * 512 + 512], ssm_cols(UT, j), ALU.add).then_inc(S("s_y"), 1)
                    if j:
                        back(j - 1)
                    dve.wait_ge(S("s_y"), n)
                    dve.tensor_reduce(st[:, 0, sj], y3, AX_X, ALU.add).then_inc(S("s_s"), 1)
                    dve.wait_ge(S("s_s"), n)
                    dve.scalar_tensor_tensor(XC[:, j * 512:j * 512 + 512].rearrange("p (a d) -> p a d", d=D),
                                             st[:, 0, sj].unsqueeze(2).to_broadcast([128, KC * 2, D]), -1.0 / D, y3,
                                             ALU.mult, ALU.add).then_inc(S("s_c"), 1)
                back(NJ - 1)
            dve.wait_ge(S("hb"), 1)
            for j in range(NJ):
                dve.wait_ge(S("o_mm"), j + 1)
                hv = view_km(H)[:, j * KC:(j + 1) * KC, :, :]
                dve.tensor_tensor(hv, PS[:, j % 3, :].rearrange("p (k h d) -> p k h d", h=2, d=D), hv, ALU.add).then_inc(S("o_h"), 1)
            ln_dve(dve, 1, H, lambda c: dve.wait_ge(S("o_h"), 2 * (c % (NC // 2)) + 2))
            def gate(p, k):
                a, b = GPART[p]
                n = b - a

                def tile(i):
                    return Y1[:, NM * E * i:NM * E * (i + 1)].rearrange("p (m e) -> p m e", e=E)[:, a:b, :]

                def stat(i):
                    return gs[:, i, a:b]

                def spread(i):
                    return stat(i).unsqueeze(2).to_broadcast([128, n, E])

                LG, SC, K1, K2 = tile(0), tile(1), tile(2), tile(3)
                revb = rev[:, :].unsqueeze(1).to_broadcast([128, n, E])
                lps = PS[:, 0:NM // 16, :].rearrange("p b (m a e) -> p (b m) a e", a=2, e=E)[:, a:b, :, :]
                gp = GPT.rearrange("p (m g e) -> p m g e", g=3, e=E)[:, a:b, :, :]
                if k == 0:
                    dve.wait_ge(S("gt_mm"), b // CH)
                elif k == GEXP:
                    dve.wait_ge(S("g_exp"), p + 1)
                if p or k:
                    dve.wait_ge(S("gchain"), gates_done(p, k))
                if k == 0:
                    op = dve.tensor_tensor(LG, lps[:, :, 1, :], gbr[:, :].unsqueeze(1).to_broadcast([128, n, E]), ALU.add)
                elif k == 1:
                    op = dve.tensor_tensor(LG, lps[:, :, 0, :], LG, ALU.add)
                elif k in (2, 8):
                    op = dve.tensor_reduce(stat(k // 8), LG, AX_X, ALU.max)
                elif k in (3, 9):
                    op = dve.tensor_tensor(SC, LG, spread(k // 8), ALU.is_equal)
                elif k in (4, 10):
                    op = dve.tensor_tensor(SC, SC, revb, ALU.mult)
                elif k in (5, 11):
                    op = dve.tensor_reduce(stat(2), SC, AX_X, ALU.max)
                elif k in (6, 12):
                    op = dve.tensor_tensor(K1 if k == 6 else K2, revb, spread(2), ALU.is_equal)
                elif k == 7:
                    op = dve.scalar_tensor_tensor(LG, K1, -3e38, LG, ALU.mult, ALU.add)
                elif k == 13:
                    op = dve.tensor_tensor(stat(3), stat(1), stat(0), ALU.subtract)
                elif k == 14:
                    op = dve.tensor_scalar(stat(5), stat(4), 1.0, None, ALU.add)
                elif k == 15:
                    op = dve.reciprocal(stat(6), stat(5))
                elif k == 16:
                    op = dve.tensor_tensor(stat(7), stat(4), stat(6), ALU.mult)
                elif k in (17, 18):
                    K = K1 if k == 17 else K2
                    op = dve.tensor_tensor(K, K, spread(k - 11), ALU.mult)
                elif k == 19:
                    op = dve.tensor_tensor(LG, K1, K2, ALU.add)
                elif k in (20, 22, 24):
                    op = dve.tensor_copy(gp[:, :, (k - 20) // 2, :], (LG, SC, K1)[(k - 20) // 2])
                elif k == 21:
                    op = dve.tensor_tensor(SC, LG, gp[:, :, 0, :], ALU.subtract)
                else:
                    op = dve.tensor_tensor(K1, SC, gp[:, :, 1, :], ALU.subtract)
                op.then_inc(S("gchain"), 1)

            def first_gates(c):
                if c == 1:
                    dve.wait_ge(S("ld_moe"), 16 * 8)
                    dve.wait_ge(S("rev"), E)
                if c >= 2:
                    for k in range((0, 7, 14, 20)[c - 2], (7, 14, 20, GOPS)[c - 2]):
                        gate(0, k)

            xs_dve(dve, first_gates)
            for k in range(2):
                gate(1, k)
            dve.wait_ge(S("p_np"), 1)
            dve.memset(bus[D:128, :], 0.0).then_inc(S("bus0"), 1)
            dve.tensor_copy(NPt[:, :, :], PS[:, 6, 0:NP * D].rearrange("p (c d) -> p c d", d=D)).then_inc(S("NPt"), 1)
            dve.tensor_tensor(bus[0:D, 1:2], PS[0:D, 6, NP * D:NP * D + 1], bus[0:D, 0:1], ALU.add).then_inc(S("NPt"), 1)
            def settle(j, k):
                def step(*ks):
                    return k in ks
                if step(0, 1, 2, 3):
                    q, odd = k // 2, k % 2
                    ps = PS[:, 2 + q, :].rearrange("p (m a d) -> p m a d", a=2, d=D)[:, :, odd, :]
                    y = Ysum[:, q * QM:(q + 1) * QM, :]
                    if odd:
                        dve.wait_ge(S("mo_y"), 4 * j + k)
                        dve.tensor_tensor(y, ps, y, ALU.add).then_inc(S("mo_y"), 1)
                    else:
                        dve.wait_ge(S("mo_tp"), 2 * j + q + 1)
                        dve.tensor_tensor(y, ps, X[:, bass.ds(j * CH + q * QM, QM), :], ALU.add).then_inc(S("mo_y"), 1)
                if step(8):
                    dve.wait_ge(S("f_g"), j + 1)
                    h = H[:, bass.ds(j * CH, CH), :]
                    dve.tensor_tensor(h, h, Ygam, ALU.add).then_inc(S("f_h"), 1)
                    dve.wait_ge(S("f_h"), j + 1)
                r = 0 if k < 8 else 1
                src = H[:, bass.ds(j * CH, CH), :] if r else Ysum
                if step(4, 9):
                    if not r:
                        dve.wait_ge(S("mo_y"), 4 * j + 4)
                    dve.tensor_reduce(st[:, 0, ln_part(r)], src, AX_X, ALU.add).then_inc(S("ln_s"), 1)
                if step(5, 10):
                    dve.wait_ge(S("ln_s"), ln_no(j, r))
                    dve.scalar_tensor_tensor(Ycen[:, r, :, :], st[:, 0, ln_part(r)].unsqueeze(2).to_broadcast([128, CH, D]), -1.0 / D,
                                             src, ALU.mult, ALU.add).then_inc(S("ln_c"), 1)
                if step(6, 11):
                    dve.wait_ge(S("ln_q"), ln_no(j, r))
                    dve.tensor_reduce(st[:, 2, ln_part(r)], Ysqr[:, r, :, :], AX_X, ALU.add).then_inc(S("ln_v0"), 1)
                if step(7, 12):
                    dve.wait_ge(S("ln_v0"), ln_no(j, r))
                    dve.tensor_scalar(st[:, 2, ln_part(r)], st[:, 2, ln_part(r)], 1.0 / D, EPS, ALU.mult, ALU.add).then_inc(S("ln_v"), 1)
                if step(13, 14):
                    a = k - 13
                    dve.wait_ge(S("xs_h"), 2 * (NC + j) + a + 1)
                    dve.tensor_tensor(XSp()[64:128, bass.ds(4 * j, 4), a, :], bank4(2)[64 * a:64 * a + 64],
                                      XSp()[0:64, bass.ds(4 * j, 4), a, :].bitcast(F32), ALU.subtract).then_inc(S("xs_l"), 1)

            SETTLE = [(0, e) for e in (5, 6, 7, 8, 9, 10, 12, 13)] + [(1, e) for e in (1, 2, 3, 5, 6, 12, 13)]

            def experts(i, first=False):
                for qq in range(2):
                    for e in range(E):
                        n = i * 2 * E + qq * E + e
                        dve.wait_ge(S("m_r"), n + 5)
                        dve.wait_ge(S("m_g"), n + 1)
                        dve.wait_ge(S("m_d"), n + 1)
                        dve.tensor_tensor(Hb[:, e % 4, :], PS[:, 4 + e % 2, :], Rb[:, e % 4, :], ALU.mult).then_inc(S("m_h"), 1)
                        step = qq * E + e
                        if first and step < 12:
                            gate(1, step + 2)
                        if first and GEXP <= step < GOPS:
                            gate(1, step)
                        if not first and (qq, e) in SETTLE:
                            settle(i - 1, SETTLE.index((qq, e)))

            experts(0, first=True)
            dve.wait_ge(S("hb"), 2)
            with dve.Fori(1, NC) as i:
                experts(i)
            for k in range(len(SETTLE)):
                settle(NC - 1, k)
                if k in (7, 12):
                    r = 0 if k == 7 else 1
                    dst = (Ygam, Ynrm)[r]
                    dve.wait_ge(S("ln_r"), ln_no(NC - 1, r))
                    dve.tensor_tensor(dst, Ycen[:, r, :, :], st[:, 3, ln_part(r)].unsqueeze(2).to_broadcast([128, CH, D]),
                                      ALU.mult).then_inc(S("ln_o"), 1)
                    if r == 0:
                        dve.wait_ge(S("ln_o"), ln_no(NC - 1, r))
                        dve.tensor_tensor(dst, dst, gam[:, :].unsqueeze(1).to_broadcast([128, CH, D]), ALU.mult).then_inc(S("f_g"), 1)

            xsb = XS[:, :].rearrange("p (t b) -> p b t", b=NB)

            def step(i, k, first=False, last=False, drain=False):
                B, g, bb = 8 * i + k, 2 * i + k // 4, k % 4
                gp = (k // 4) % 2
                if bb == 2 and not drain and not last:
                    dve.wait_ge(S("a_q"), 2 * NP * g + 2 * NP)
                    dve.wait_ge(S("a_xt"), g + 1)
                    dve.tensor_copy(XSg[:, gp, :, :], xsb[:, bass.ds(GB * g + 2 * GB, GB), :]).then_inc(S("a_st"), 1)
                if has(1, k, first, drain):
                    s1 = am[:, (k - 1) % 4, :, :]
                    dve.wait_ge(S("a_e"), B)
                    dve.tensor_reduce(s1[:, 1, :], Pb[:, (k - 1) % 4, :, :, :].rearrange("p a h j -> p (a h) j"),
                                      AX_X, ALU.add).then_inc(S("a_sm"), 1)
                    dve.wait_ge(S("a_sm"), B)
                    dve.reciprocal(s1[:, 2, :], s1[:, 1, :]).then_inc(S("a_rc"), 1)
                    dve.wait_ge(S("a_rc"), B)
                    dve.tensor_scalar(s1[:, 3, :], s1[:, 2, :], valid[:, 0:1], None, ALU.mult).then_inc(S("a_rv"), 1)
                if drain:
                    return
                ps = PS[0:T, 2 + 2 * (k % 2):4 + 2 * (k % 2), 0:NP * T].rearrange("p a (h j) -> p a h j", h=NP)
                dve.wait_ge(S("a_s"), B + 1)
                dve.tensor_reduce(am[:, k % 4, 0, :], ps, AX_X, ALU.max).then_inc(S("a_mx"), 1)
                dve.wait_ge(S("a_mx"), B + 1)
                if not (first and k < 4):
                    dve.wait_ge(S("a_t"), B - 3)
                mx = am[:, k % 4, 0, :].rearrange("p (a h) -> p a h", a=2)
                for a in range(2):
                    dve.tensor_tensor(Pb[:, k % 4, a, :, :], ps[:, a, :, :], mx[:, a, :].unsqueeze(2).to_broadcast([T, NP, T]),
                                      ALU.subtract).then_inc(S("a_sub%d" % a if a == 0 else "a_sub"), 1)

            dve.wait_ge(S("mask"), 4)
            dve.wait_ge(S("xs_l"), 4 * NC)
            for g in range(2):
                dve.tensor_copy(XSg[:, g, :, :], xsb[:, g * GB:(g + 1) * GB, :]).then_inc(S("a_st"), 1)
            att_loop(dve, step)

            def att_residual(c):
                for a in range(2):
                    for q in (2 * c, 2 * c + 1):
                        ps = PS[:, 4 + q % 4, :].rearrange("p (m a d) -> p m a d", a=2, d=D)
                        hc = H[:, q * QM:(q + 1) * QM, :]
                        if a == 0:
                            dve.wait_ge(S("ao_tp"), q + 1)
                        else:
                            dve.wait_ge(S("a_h"), 4 * c + q % 2 + 1)
                        dve.tensor_tensor(hc, ps[:, :, a, :], hc, ALU.add).then_inc(S("a_h"), 1)

            def norm(c, k):
                h = H[:, bass.ds(c * CH, CH), :]
                if k == 0:
                    dve.tensor_reduce(st[:, 0, 0:CH], h, AX_X, ALU.add).then_inc(S("ln_s"), 1)
                if k == 1:
                    dve.wait_ge(S("ln_s"), ln_last(c))
                    dve.scalar_tensor_tensor(Xcen, st[:, 0, 0:CH].unsqueeze(2).to_broadcast([128, CH, D]), -1.0 / D, h,
                                             ALU.mult, ALU.add).then_inc(S("ln_c"), 1)
                if k == 2:
                    dve.wait_ge(S("ln_q"), ln_last(c))
                    dve.tensor_reduce(st[:, 2, 0:CH], Xsqr, AX_X, ALU.add).then_inc(S("ln_v0"), 1)
                if k == 3:
                    dve.wait_ge(S("ln_v0"), ln_last(c))
                    dve.tensor_scalar(st[:, 2, 0:CH], st[:, 2, 0:CH], 1.0 / D, EPS, ALU.mult, ALU.add).then_inc(S("ln_v"), 1)

            def cell(i, u, first=False):
                t = 4 * i + u
                tb = Tb[:, u % 2, :]
                if not first and u % 2 == 0:
                    dve.wait_ge(S("l_tp"), 2 * i + u // 2 - 1)
                dve.wait_ge(S("l_t"), 2 * t + 2)
                dve.scalar_tensor_tensor(Cb[:, 0, :], tb[0:64, 0:64], 1.0, tb[0:64, 64:128], ALU.add, ALU.mult).then_inc(S("l_a"), 1)
                dve.wait_ge(S("l_a"), t + 1)
                if first and u == 0:
                    dve.tensor_scalar(Cb[:, 1, :], Cb[:, 0, :], 0.5, None, ALU.mult).then_inc(S("l_c"), 1)
                else:
                    dve.wait_ge(S("l_hc"), t)
                    dve.scalar_tensor_tensor(Cb[:, 1, :], Cb[:, 0, :], 0.5, HC[:, :], ALU.mult, ALU.add).then_inc(S("l_c"), 1)
                dve.wait_ge(S("l_tc"), t + 1)
                dve.scalar_tensor_tensor(HB[:, u, :], tb[64:128, 0:64], 1.0, TC[64:128, :], ALU.add, ALU.mult).then_inc(S("l_h"), 1)
                dve.wait_ge(S("l_h"), t + 1)
                dve.scalar_tensor_tensor(HC[:, :], HB[:, u, :], 0.5, Cb[:, 1, :], ALU.mult, ALU.mult).then_inc(S("l_hc"), 1)
                if u % 2 == 0 and not (first and u == 0):
                    output(2 * i + u // 2 - 1, (u // 2 - 1) % 2)

            def output(m, par):
                dve.wait_ge(S("l_tp"), m + 1)
                dve.scalar_tensor_tensor(X[:, bass.ds(m, 1), :].rearrange("p a d -> p (a d)"), PS[:, 4 + par, 0:D], 0.5,
                                         H[:, bass.ds(m, 1), :].rearrange("p a d -> p (a d)"), ALU.mult, ALU.add).then_inc(S("l_out"), 1)

            def steps(c, first=False, last=False):
                for u in range(2 * CH):
                    cell(4 * c + u // 4, u % 4, first=first and u < 4)
                    if u in (1, 2, 5, 6) and not last:
                        norm(c + 1, (1, 2, 5, 6).index(u))

            att_residual(0)
            dve.wait_ge(S("a_h"), 4)
            norm(0, 0)
            norm(0, 1)
            for c in range(1, NC):
                att_residual(c)
                if c == 1:
                    norm(0, 2)
                    norm(0, 3)
            dve.wait_ge(S("a_h"), 4 * NC)
            steps(0, first=True)
            with dve.Fori(1, NC - 1) as c:
                steps(c)
            steps(NC - 1, last=True)
            output(NM - 1, 1)

        @block.tensor
        def _(pe):
            pe.wait_ge(S("cst"), 1)
            pe.wait_ge(S("ld_tok"), 32)
            pe.matmul(PS[:, 0, 0:NF + 1], o128[:, :], wtok[:, :], start=True, stop=True).then_inc(S("p_wmps"), 1)
            pe.wait_ge(S("ident"), 1)
            pe.wait_ge(S("ld_a"), 64)
            for l in range(L):
                last = pe.transpose(PS[0:D, 1, l * D:l * D + D], Am[:, 0, l, :], ident[0:D, 0:D])
            last.then_inc(S("p_kry"), 1)
            pe.wait_ge(S("cst"), 2)
            for l in range(L):
                last = pe.matmul(PS[0:D, 4, l:l + 1], Cs[:, l, :], cD[0:D, :], start=True, stop=True)
            last.then_inc(S("p_g0"), 1)
            for i in range(nsq + 1):
                m = 1 << i
                nm = min(m, T - m)
                cur = Am if i % 2 == 0 else Am2
                pe.wait_ge(S("p_gk"), i + 1)
                if i:
                    pe.wait_ge(S("p_am"), i)
                pe.wait_ge(S("p_at"), i + 1)
                for l in range(L):
                    last = pe.matmul(PS[0:D, 0, l * nm:l * nm + nm], cur[:, 0, l, :], Gk[:, l, 0:nm], start=True, stop=True)
                if i < nsq:
                    for l in range(L):
                        pe.matmul(PS[0:D, 2, l * D:l * D + D], cur[:, 1, l, :], cur[:, 0, l, :], start=True, stop=True)
                    for l in range(L):
                        last = pe.matmul(PS[0:D, 1, l * D:l * D + D], cur[:, 0, l, :], cur[:, 1, l, :], start=True, stop=True)
                last.then_inc(S("p_kry"), 1)
            pe.wait_ge(S("p_gk"), nsq + 2)
            for l in range(L):
                last = pe.matmul(PS[:, 3, l * T:l * T + T], BB[:, l, :, :].rearrange("p a b -> p (a b)"), Gk[:, l, :], start=True, stop=True)
            last.then_inc(S("p_w"), 1)
            pe.wait_ge(S("ld_bd"), 16 * 8)
            for h in range(2):
                for a in range(3):
                    last = pe.transpose(PS[:, 6 + h, a * 128:a * 128 + 128], bds[:, 3 * h + a, :], ident[:, :])
                last.then_inc(S("p_bd"), 1)
            xk = halves(X)
            def normalised(j):
                pe.wait_ge(S("ln_o"), 2 * (j * KC // CH) + 2)
                if j >= 2:
                    pe.wait_ge(S("w_x"), j - 1)
                for k in range(KC):
                    mm = pe.transpose(PS[:, 4 + j % 2, k * 128:k * 128 + 128], xk[:, j * KC + k, :, :].rearrange("p h d -> p (h d)"), ident[:, :])
                mm.then_inc(S("w_tp"), 1)

            def win(j):
                pe.wait_ge(S("w_x"), j + 1)
                if j >= 3:
                    pe.wait_ge(S("w_u"), j - 2)
                for k in range(KC):
                    mm = pe.matmul(PS[:, j % 3, k * 128:k * 128 + 128], UF[:, j * KC + k, :], bdt[:, 0, :], start=True, stop=True)
                mm.then_inc(S("w_mm"), 1)

            def toeplitz(l, j):
                pe.wait_ge(S("s_uf"), l * NJ + j + 1)
                for tt in range(2 * KC * j, 2 * KC * (j + 1)):
                    o = T // 2 - 1 - tt
                    mm = pe.matmul(PS[0:64, 6, 0:T], UF[:, tt // 2, 64 * (tt % 2):64 * (tt % 2) + 64],
                                   WB[:, bass.ds(l, 1), o:o + T].rearrange("p a t -> p (a t)"), start=(tt == 0), stop=(tt == T // 2 - 1))
                if j == NJ - 1:
                    mm.then_inc(S("s_cps"), 1)

            def du(l, j):
                if j >= 3:
                    pe.wait_ge(S("s_gelu"), l * NJ + j - 2)
                for k in range(KC):
                    mm = pe.matmul(PS[:, j % 3, k * 128:k * 128 + 128], UF[:, j * KC + k, :],
                                   bdt[:, bass.ds(l + 1, 1), :].rearrange("p a t -> p (a t)"), start=True, stop=True)
                mm.then_inc(S("s_du"), 1)

            def feature_major(j):
                for k in range(KC):
                    mm = pe.transpose(PS[:, 4 + j % 2, k * 128:k * 128 + 128], UT[:, j * KC + k, :, :].rearrange("p h d -> p (h d)"), ident[:, :])
                mm.then_inc(S("s_tp"), 1)

            for j in range(NJ - 2):
                normalised(j)
            pe.wait_ge(S("p_gk"), nsq + 2)
            pe.wait_ge(S("p_bdt"), 2)
            win(0)
            win(1)
            normalised(NJ - 2)
            normalised(NJ - 1)
            win(2)
            for j in range(NJ):
                pe.wait_ge(S("w_u"), j + 1)
                if j < 2:
                    pe.wait_ge(S("w_x"), NJ - 1 + j)
                else:
                    pe.wait_ge(S("s_uf"), j - 1)
                feature_major(j)
                if j == 0:
                    pe.wait_ge(S("p_wb"), 2)
                else:
                    toeplitz(0, j - 1)
                if j + 3 < NJ:
                    win(j + 3)
            pe.wait_ge(S("ld_moe"), 16 * 8)
            pe.transpose(PS[:, 7, 0:E], b1s[:, :], ident[0:E, 0:E]).then_inc(S("p_b1"), 1)
            pe.wait_ge(S("w_u"), NJ)
            du(0, 0)
            toeplitz(0, NJ - 1)
            for j in range(1, 3):
                du(0, j)

            def layer(l, last=False):
                for j in range(3, NJ):
                    du(l, j)
                for j in range(NJ):
                    pe.wait_ge(S("s_un"), l * NJ + j + 1)
                    pe.wait_ge(S("s_uf"), l * NJ + NJ + j - 1)
                    feature_major(j)
                    if not last and j:
                        toeplitz(l + 1, j - 1)
                        if j >= NJ - 3:
                            pe.wait_ge(S("s_gelu"), l * NJ + j + 1)
                            du(l + 1, j - (NJ - 3))
                if not last:
                    toeplitz(l + 1, NJ - 1)

            with pe.Fori(0, L - 1) as l:
                layer(l)
            layer(L - 1, last=True)
            for j in range(NJ):
                pe.wait_ge(S("s_uf"), L * NJ + j + 1)
                if j < 3:
                    pe.wait_ge(S("s_gelu"), L * NJ - 2 + j)
                else:
                    pe.wait_ge(S("o_h"), j - 2)
                for k in range(KC):
                    last = pe.matmul(PS[:, j % 3, k * 128:k * 128 + 128], UF[:, j * KC + k, :], bdt[:, L + 1, :], start=True, stop=True)
                last.then_inc(S("o_mm"), 1)
            def logits(c):
                if c == 0:
                    pe.wait_ge(S("wlo"), 3)
                    pe.wait_ge(S("o_h"), NJ)
                pe.wait_ge(S("xs_l"), 2 * c + 2)
                for m in range(c * CH, (c + 1) * CH):
                    last = pe.matmul(PS[:, m // 16, (m % 16) * 2 * E:(m % 16 + 1) * 2 * E], XS[:, m * 128:(m + 1) * 128],
                                     GWhl[:, :, :].rearrange("p a e -> p (a e)"), start=True, stop=True)
                last.then_inc(S("gt_mm"), 1)

            xs_pe(pe, 1, logits)
            pe.wait_ge(S("ld_at"), 16 * 6)
            for c in range(NP):
                last = pe.transpose(PS[:, 7, c * D:(c + 1) * D], Wvs[:, c * 128:(c + 1) * 128], ident[0:D, 0:D])
            last.then_inc(S("p_wvt"), 1)
            pe.wait_ge(S("WvT"), 1)
            for c in range(NP):
                for a in range(2):
                    r = slice(64 * a, 64 * a + 64)
                    pe.matmul(PS[r, 6, c * D:(c + 1) * D], WvT[r, c, :], Wus[r, c, :], start=True, stop=True)
            for c in range(NP):
                last = pe.matmul(PS[0:D, 6, NP * D:NP * D + 1], Wus[:, c, :], bvs[:, c:c + 1], start=(c == 0), stop=(c == NP - 1))
            last.then_inc(S("p_np"), 1)
            def gates_turn(c):
                if c >= 2:
                    pe.wait_ge(S("gp"), c - 1)
                for k in range(8):
                    last = pe.transpose(PSb[0:3 * E, 2 + c % 2, k * 128:(k + 1) * 128],
                                        GPT[:, (c * 8 + k) * 3 * E:(c * 8 + k + 1) * 3 * E], identb[:, :])
                last.then_inc(S("gp_tp"), 1)

            pe.wait_ge(S("gchain"), gates_done(1, 2))
            pe.wait_ge(S("identb"), 1)
            for c in range(2):
                gates_turn(c)
            pe.wait_ge(S("NPt"), 2)
            pe.wait_ge(S("b2c"), 5)
            pe.wait_ge(S("b2z"), 1)
            pe.wait_ge(S("sel"), 4)
            pe.wait_ge(S("ld_moe"), 16 * 8)
            grant(pe, "m_r", 4)
            grant(pe, "m_h", 4)
            grant(pe, "m_d", 4)
            grant(pe, "m_mo", 2)
            def sums_out(j):
                pe.wait_ge(S("m_mo"), 2 * j + 4)
                pe.wait_ge(S("xs_l"), 2 * (NC + j))
                for q in range(2):
                    for k in range(QM):
                        last = pe.transpose(PS[:, 2 + q, k * 128:(k + 1) * 128], MO[:, q * 512 + k * 128:q * 512 + (k + 1) * 128], ident[:, :])
                    last.then_inc(S("mo_tp"), 1)

            def norm_out(j):
                pe.wait_ge(S("ln_o"), ln_no(j, 1))
                for k in range(4):
                    last = pe.transpose(PS[:, 2, k * 128:k * 128 + 128], Ynrm[:, 2 * k:2 * k + 2, :].rearrange("p m d -> p (m d)"), ident[:, :])
                last.then_inc(S("xs_tp"), 1)

            def experts(i, first=False):
                for qq in range(2):
                    col = i * 1024 + qq * 512

                    def down(q, e):
                        pe.wait_ge(S("m_h"), i * 2 * E + q * E + e + 5)
                        pe.matmul(PS[64 * (e % 2):64 * (e % 2) + 64, 6 + q % 2, :], w2s[:, e, :], Hb[:, e % 4, :],
                                  start=False, stop=(e >= E - 2)).then_inc(S("m_d"), 1)

                    for e in range(E):
                        n = i * 2 * E + qq * E + e
                        if e == 0:
                            pe.wait_ge(S("gp"), i + 1)
                            pe.wait_ge(S("m_mo"), i * 2 + qq + 1)
                        pe.wait_ge(S("m_h"), n + 3)
                        pe.wait_ge(S("m_r"), n + 1)
                        pe.matmul(PS[:, e % 2, :], W1h[:, e, :], XS[:, bass.ds(col, 512)], start=True, stop=False)
                        pe.matmul(PS[:, e % 2, :], W1l[:, e, :], XS[:, bass.ds(col, 512)], start=False, stop=True).then_inc(S("m_z"), 1)
                        if e == 0:
                            for g in range(3):
                                pe.matmul(PS[:, 6 + qq, :], b2p[:, g, :], GP[0:3 * E, bass.ds(col, 512)], start=(g == 0), stop=False)
                        pe.matmul(PS[:, 4 + e % 2, :], sel[:, e, :], GP[0:3 * E, bass.ds(col, 512)], start=True, stop=True).then_inc(S("m_g"), 1)
                        if e % 2 and not (first and qq == 0 and e == 1):
                            down(qq if e > 1 else qq - 1, (e - 3) % E)
                            down(qq if e > 1 else qq - 1, (e - 2) % E)
                        if first and (qq, e) in ((1, 12), (1, 14)):
                            pe.wait_ge(S("gchain"), gates_done(1, GOPS))
                            for c in range(NC - 4 + (e - 12), NC - 2 + (e - 12)):
                                gates_turn(c)
                        if not first and (qq, e) == (0, 4):
                            sums_out(i - 1)
                        if not first and (qq, e) == (1, 10):
                            norm_out(i - 1)

            experts(0, first=True)
            with pe.Fori(1, NC) as i:
                experts(i)
            for e in (E - 2, E - 1):
                pe.wait_ge(S("m_h"), NQ * E - E + e + 5)
                pe.matmul(PS[64 * (e % 2):64 * (e % 2) + 64, 6 + (NQ - 1) % 2, :], w2s[:, e, :], Hb[:, e % 4, :],
                          start=False, stop=True).then_inc(S("m_d"), 1)
            sums_out(NC - 1)
            norm_out(NC - 1)

            def q_tile(par, tile, bank):
                W = (WQKh, WQKl)
                for a in range(2):
                    last = pe.matmul(PS[:, bank, 0:GB * T], W[a][:, tile // NP, (tile % NP) * 128:(tile % NP + 1) * 128],
                                     XSg[:, par, :, :].rearrange("p b t -> p (b t)"), start=(a == 0), stop=(a == 1))
                last.then_inc(S("a_q"), 1)

            def step(i, k, first=False, last=False, drain=False):
                B, g, bb = 8 * i + k, 2 * i + k // 4, k % 4
                gp = (k // 4) % 2
                nq = 2 * NP
                if not drain:
                    if bb == 0:
                        pe.wait_ge(S("q_ev"), nq * g + nq)
                    if has(2, k, first, False):
                        pe.wait_ge(S("a_sub"), B - 1)
                    for a in range(2):
                        pe.matmul(PS[0:T, 2 + 2 * (k % 2) + a, 0:NP * T], identb[0:T, 0:T],
                                  mask[:, :, :].rearrange("p h j -> p (h j)"), start=True, stop=False)
                    for h in range(NP):
                        for a in range(2):
                            r = slice(64 * a, 64 * a + 64)
                            mm = pe.matmul(PS[0:T, 2 + 2 * (k % 2) + a, h * T:(h + 1) * T], QK[gp][r, h, bb * T:(bb + 1) * T],
                                           QK[gp][r, NP + h, bb * T:(bb + 1) * T], start=False, stop=(h == NP - 1))
                    mm.then_inc(S("a_s"), 1)
                nextq = not drain and not (last and k >= 4)
                if (bb == 0 and not first) or (drain and k == 3):
                    og = g - 2 + k // 3 if drain else g - 2
                    pe.wait_ge(S("z_ev"), 4 * og + 4)
                    if drain:
                        if k == 0:
                            pe.wait_ge(S("xt_ev"), g)
                        else:
                            pe.wait_ge(S("o_ev"), 2 * g - 2)
                    for h in range(NP):
                        r = slice(64 * (h % 2), 64 * (h % 2) + 64)
                        mm = pe.matmul(PS[r, 1, 0:GB * T], NPt[:, h, :], Zg[(k // 4 + k // 3 * drain) % 2][:, h, :, :].rearrange("p b t -> p (b t)"),
                                       start=(h < 2), stop=(h >= NP - 2))
                    mm.then_inc(S("a_o"), 1)
                if bb == 1 and not drain:
                    if nextq:
                        pe.wait_ge(S("q_ev"), nq * (g + 1) + 2)
                    else:
                        pe.wait_ge(S("o_ev"), 2 * g - 2)
                    for b in range(GB):
                        mm = pe.matmul(PS[0:T, 1, b * D:(b + 1) * D], XSg[:, gp, b, :], ii[:, :], start=True, stop=True)
                    mm.then_inc(S("a_xt"), 1)
                if nextq:
                    if bb == 0:
                        pe.wait_ge(S("a_st"), g + 2)
                    if has(4, k, first, False):
                        pe.wait_ge(S("z_ev"), B - 3)
                    elif k:
                        pe.wait_ge(S("q_ev"), nq * (g + 1) + 2 * bb - 1)
                    q_tile(1 - gp, 2 * bb, 0)
                if has(2, k, first, drain):
                    pe.wait_ge(S("a_pn"), B - 1)
                    if has(3, k, first, False):
                        pe.wait_ge(S("pt_ev"), B - 2)
                    for h in range(NP):
                        for a in range(2):
                            mm = pe.transpose(PS[0:T, 6 + a, h * T:(h + 1) * T], Pb[:, (k - 2) % 4, a, h, :], ident[0:T, 0:T])
                    mm.then_inc(S("a_t"), 1)
                if nextq:
                    if bb == 0 and not first:
                        pe.wait_ge(S("o_ev"), 2 * g - 2)
                    if bb == 1:
                        pe.wait_ge(S("xt_ev"), g + 1)
                    if bb >= 2:
                        pe.wait_ge(S("q_ev"), nq * (g + 1) + 2 * bb)
                    q_tile(1 - gp, 2 * bb + 1, 1)
                if has(3, k, first, drain):
                    zg = (k - 3) // 4
                    pe.wait_ge(S("pt_ev"), B - 2)
                    if nextq:
                        pe.wait_ge(S("q_ev"), nq * (g + 1) + 2 * bb + 1)
                    elif has(4, k, first, False):
                        pe.wait_ge(S("z_ev"), B - 3)
                    for a in range(2):
                        mm = pe.matmul(PS[64 * a:64 * a + 64, 0, 0:NP * T], XT[:, zg % 2, (k - 3) % 4, :],
                                       PT[:, (k - 3) % 2, a, :], start=True, stop=True)
                    mm.then_inc(S("a_z"), 1)

            pe.wait_ge(S("a_st"), 1)
            pe.wait_ge(S("wsc"), 4)
            pe.wait_ge(S("mask"), 4)
            pe.wait_ge(S("ii"), 2)
            pe.wait_ge(S("NPt"), 2)
            pe.wait_ge(S("bus0"), 1)
            for tile in range(2 * NP):
                q_tile(0, tile, tile)
            att_loop(pe, step)
            for q in range(NQ):
                pe.wait_ge(S("o_ev"), 2 * NG)
                if q >= 4:
                    pe.wait_ge(S("a_h"), 4 * (q // 2 - 2) + 3 + q % 2)
                for k in range(QM):
                    m = q * QM + k
                    mm = pe.transpose(PS[:, 4 + q % 4, k * 128:(k + 1) * 128], AO[:, m * 128:(m + 1) * 128], ident[:, :])
                mm.then_inc(S("ao_tp"), 1)
            def turn_x(c, k):
                if k == 0:
                    pe.wait_ge(S("ln_o"), ln_last(c))
                    pe.nop().then_inc(S("x_go"), 1)
                for p in (2 * k, 2 * k + 1):
                    mm = pe.transpose(PS[0:D, p // 4, (p % 4) * 128:(p % 4 + 1) * 128], Xnrm[:, p, :], ident[:, :])
                if k % 2:
                    mm.then_inc(S("x_tp"), 1)

            def gates_x(i, u, first, late):
                xt = XF[:, bass.ds(256 * i + 64 * u, 64)]
                bank = PS[:, 2 + u % 2, :]
                if not (first and u < 2):
                    pe.wait_ge(S("l_to"), 4 * i + u - 1)
                if u % 2 == 0 and late:
                    pe.wait_ge(S("l_out"), 2 * i + u // 2 - 2)
                mm = pe.matmul(bank[:, 0:64], UIO[:, :], xt, start=True, stop=False, skip_group_check=True)
                if first and u == 0:
                    mm.then_inc(S("l_vi"), 1)
                mm = pe.matmul(PS[0:64, 6 + u % 2, 0:64], UG[:, :], xt, start=True, stop=(first and u == 0), skip_group_check=True)
                if first and u == 0:
                    mm.then_inc(S("l_vg"), 1)
                    pe.nop().then_inc(S("l_vo"), 1)

            def gates_h(i, u, first=False):
                bank = PS[:, 2 + u % 2, :]
                pe.wait_ge(S("l_h"), 4 * i + u)
                pe.nop().then_inc(S("l_hp"), 1)
                hp = HB[:, (u - 1) % 4, :]
                pe.matmul(bank[0:64, 0:64], VIO[:, 0:64], hp, start=False, stop=True, skip_group_check=True).then_inc(S("l_vi"), 1)
                pe.matmul(PS[0:64, 6 + u % 2, 0:64], VG[:, :], hp, start=False, stop=True, skip_group_check=True).then_inc(S("l_vg"), 1)
                pe.matmul(bank[64:128, 0:64], VIO[:, 64:128], hp, start=False, stop=True, skip_group_check=True).then_inc(S("l_vo"), 1)
                if u % 2 == 0:
                    out_tp((u // 2 - 1) % 2)

            def out_tp(par):
                pe.transpose(PS[:, 4 + par, 0:D], HB[:, 2 * par:2 * par + 2, :].rearrange("p a b -> p (a b)"), ident[0:D, 0:D]).then_inc(S("l_tp"), 1)

            def steps(c, first=False, last=False):
                for u in range(2 * CH):
                    if u == 0:
                        pe.wait_ge(S("x_f"), 2 * c + 2)
                    gates_x(4 * c + u // 4, u % 4, first=first and u < 4, late=not first or u > 5)
                    if not (first and u == 0):
                        gates_h(4 * c + u // 4, u % 4, first=first and u < 4)
                    if u in (8, 9, 10, 11) and not last:
                        turn_x(c + 1, u - 8)

            for k in range(4):
                turn_x(0, k)
            pe.wait_ge(S("a_h"), 4 * NC)
            steps(0, first=True)
            with pe.Fori(1, NC - 1) as c:
                steps(c)
            steps(NC - 1, last=True)
            pe.wait_ge(S("l_out"), NM - 2)
            pe.wait_ge(S("l_h"), T)
            out_tp(1)


_INS = ["x", "txt", "L0_tok_W", "L0_tok_b", "L0_attn_Win", "L0_attn_bin_", "L0_attn_Wout", "L0_attn_bout",
        "L0_attn_A", "L0_attn_Bm", "L0_attn_Cm", "L0_attn_Dm",
        "L0_ffn_gate_w", "L0_ffn_gate_b", "L0_ffn_w1", "L0_ffn_b1", "L0_ffn_w2", "L0_ffn_b2",
        "L0_ffn_gamma", "L0_ffn_beta",
        "L1_attn_Wq", "L1_attn_bq", "L1_attn_Wk", "L1_attn_bk", "L1_attn_Wv", "L1_attn_bv",
        "L1_attn_Wu", "L1_attn_bu",
        "L1_ffn_U_i", "L1_ffn_V_i", "L1_ffn_b_i", "L1_ffn_U_c", "L1_ffn_V_c", "L1_ffn_b_c",
        "L1_ffn_U_o", "L1_ffn_V_o", "L1_ffn_b_o"]


def kernel(**inputs):
    import numpy as np
    import concourse.bacc as bacc
    from concourse.bass_utils import run_bass_kernel_spmd

    nc = bacc.Bacc("TRN2", target_bir_lowering=False, num_devices=1)
    arrays, args = {}, []
    for name in _INS:
        a = np.ascontiguousarray(inputs[name])
        arrays["in_" + name] = a
        args.append(nc.dram_tensor("in_" + name, a.shape, mybir.dt.from_np(a.dtype), kind="ExternalInput").ap())
    b, tx, d, _ = inputs["x"].shape
    shape = (b, tx + inputs["txt"].shape[1], d)
    out = nc.dram_tensor("out_0", shape, F32, kind="ExternalOutput").ap()
    early_fusion(nc, *args, out)
    r = run_bass_kernel_spmd(nc, [arrays], core_ids=[0])
    return r.results[0]["out_0"]
```
